# Optimizing a Trainium2 kernel written in Bass

```python
import numpy as np
import jax
import jax.numpy as jnp

def _softmax(x, axis=-1):
    return jax.nn.softmax(x, axis=axis)

def _gelu(x):
    return jax.nn.gelu(x, approximate=True)

def _silu(x):
    return jax.nn.silu(x)

def _sigmoid(x):
    return jax.nn.sigmoid(x)

def _layernorm(x, axis=-1, eps=1e-05):
    m = jnp.mean(x, axis=axis, keepdims=True)
    v = jnp.var(x, axis=axis, keepdims=True)
    return (x - m) / jnp.sqrt(v + eps)

def _scatter_add(tgt, idx, src, axis=0):
    return tgt.at[idx].add(src)

def _segment_sum(src, seg, n):
    return jax.ops.segment_sum(src, seg, n)
kernel_name = 'mk_xattn_ffn_d2_seqx_r8_2029af'

def setup_inputs(seed: int=0):
    np.random.seed(seed)
    _w = jnp.asarray

    def _rec_inputs():
        import jax
        import jax.numpy as jnp
        _rk = jax.random.key(seed)
        x = 7.22e-05 + 1 * jax.random.normal(jax.random.fold_in(_rk, 1), (32, 128, 128), jnp.float32)
        _lenS = 128 - jax.random.randint(jax.random.fold_in(_rk, 7), (32,), 0, max(1, 128 // 4) + 1, jnp.int32)
        _lenS2 = 128 - jax.random.randint(jax.random.fold_in(_rk, 8), (32,), 0, max(1, 128 // 4) + 1, jnp.int32)
        _ctx_1024P = jax.random.normal(jax.random.fold_in(_rk, 11), (32, 16, 128), jnp.float32)
        _ctx_1024c = jax.random.dirichlet(jax.random.fold_in(_rk, 511), 0.3 * jnp.ones((16,), jnp.float32), (32, 128))
        _ctx_1024t = jnp.einsum('bsk,bkd->bsd', _ctx_1024c, _ctx_1024P)
        _ctx_1024t = _ctx_1024t * jax.lax.rsqrt(jnp.mean(jnp.square(_ctx_1024t)) + 1e-12) * 0.953939
        ctx_1024 = 2.81802e-05 + 1.00001 * (_ctx_1024t + 0.3 * jax.random.normal(jax.random.fold_in(_rk, 611), (32, 128, 128), jnp.float32))
        return (x, ctx_1024)
    x, ctx_1024 = _rec_inputs()

    def _L0_xattn_setup():
        import jax, jax.numpy as jnp
        import numpy as np
        B, T, S, D = (4, 256, 512, 128)
        TOP_K = 32

        def _read(query, mem_state, top_k, Wq, bq, Wk, bk, Wv, bv, Wo, bo):
            b, t, d = query.shape
            s = mem_state.shape[1]
            scale = 1.0 / np.sqrt(d)
            q = query @ Wq.T + bq
            k = mem_state @ Wk.T + bk
            v = mem_state @ Wv.T + bv
            scores = jnp.einsum('btd,bsd->bts', q, k) * scale
            if top_k < s:
                vals, idx = jax.lax.top_k(scores, top_k)
                b_ix = jnp.arange(b)[:, None, None]
                t_ix = jnp.arange(t)[None, :, None]
                masked = jnp.full_like(scores, -jnp.inf)
                scores = masked.at[b_ix, t_ix, idx].set(vals)
            attn = jax.nn.softmax(scores, axis=-1)
            ctx = jnp.einsum('bts,bsd->btd', attn, v)
            return ctx @ Wo.T + bo
        key = jax.random.key(seed)
        ks = jax.random.split(key, 12)
        std = 0.02
        inp = {'query': jax.random.normal(ks[0], (B, T, D), dtype=jnp.float32), 'mem_state': jax.random.normal(ks[1], (B, S, D), dtype=jnp.float32), 'top_k': TOP_K, 'Wq': jax.random.normal(ks[2], (D, D), dtype=jnp.float32) * std, 'bq': jnp.zeros((D,), dtype=jnp.float32), 'Wk': jax.random.normal(ks[3], (D, D), dtype=jnp.float32) * std, 'bk': jnp.zeros((D,), dtype=jnp.float32), 'Wv': jax.random.normal(ks[4], (D, D), dtype=jnp.float32) * std, 'bv': jnp.zeros((D,), dtype=jnp.float32), 'Wo': jax.random.normal(ks[5], (D, D), dtype=jnp.float32) * std, 'bo': jnp.zeros((D,), dtype=jnp.float32)}
        return inp
    _L0_xattn_all = _L0_xattn_setup()
    _L0_xattn_in = {k: v for k, v in _L0_xattn_all.items() if k in ('Wq', 'bq', 'Wk', 'bk', 'Wv', 'bv', 'Wo', 'bo')}
    del _L0_xattn_all

    def _L0_ffn_setup():
        import jax, jax.numpy as jnp
        import numpy as np
        D_MODEL = 128
        M = 64
        INNER = 16
        key = jax.random.key(seed)
        ks = jax.random.split(key, 9)

        def init(k, shape, fan_in):
            bound = 1.0 / np.sqrt(fan_in)
            return jax.random.uniform(k, shape, jnp.float32, -bound, bound)
        x = jax.random.normal(ks[0], (16, 512, D_MODEL), dtype=jnp.float32)
        Win = init(ks[1], (D_MODEL, M), D_MODEL)
        bin_ = init(ks[2], (M,), D_MODEL)
        W1 = init(ks[3], (M, INNER), 1)
        b1 = init(ks[4], (M, INNER), 1)
        W2 = init(ks[5], (M, INNER), INNER)
        b2 = init(ks[6], (M,), INNER)
        Wout = init(ks[7], (M, D_MODEL), M)
        bout = init(ks[8], (D_MODEL,), M)
        return {'x': x, 'Win': Win, 'bin_': bin_, 'W1': W1, 'b1': b1, 'W2': W2, 'b2': b2, 'Wout': Wout, 'bout': bout}
    _L0_ffn_all = _L0_ffn_setup()
    _L0_ffn_in = {k: v for k, v in _L0_ffn_all.items() if k in ('Win', 'bin_', 'W1', 'b1', 'W2', 'b2', 'Wout', 'bout')}
    del _L0_ffn_all

    def _L1_xattn_setup():
        import jax, jax.numpy as jnp
        import numpy as np
        DIM = 128
        NUM_HEADS = 16
        DIM_HEAD = 64
        INNER = NUM_HEADS * DIM_HEAD
        SCALE = DIM_HEAD ** (-0.5)

        def _layernorm(x, gamma, beta, eps=1e-05):
            mu = jnp.mean(x, axis=-1, keepdims=True)
            var = jnp.mean(jnp.square(x - mu), axis=-1, keepdims=True)
            return (x - mu) * jax.lax.rsqrt(var + eps) * gamma + beta
        key = jax.random.key(seed)
        ks = jax.random.split(key, 8)
        B, SQ, SK = (2, 256, 512)
        x = jax.random.normal(ks[0], (B, SQ, DIM), dtype=jnp.float32)
        context = jax.random.normal(ks[1], (B, SK, DIM), dtype=jnp.float32)
        ln_gamma = jnp.ones((DIM,), jnp.float32)
        ln_beta = jnp.zeros((DIM,), jnp.float32)
        w_q = jax.random.normal(ks[2], (DIM, INNER), dtype=jnp.float32) / np.sqrt(DIM)
        w_kv = jax.random.normal(ks[3], (DIM, 2 * INNER), dtype=jnp.float32) / np.sqrt(DIM)
        w_out = jax.random.normal(ks[4], (INNER, DIM), dtype=jnp.float32) / np.sqrt(INNER)
        b_out = jnp.zeros((DIM,), jnp.float32)
        gate = jnp.array([0.5], jnp.float32)
        return {'x': x, 'context': context, 'ln_gamma': ln_gamma, 'ln_beta': ln_beta, 'w_q': w_q, 'w_kv': w_kv, 'w_out': w_out, 'b_out': b_out, 'gate': gate}
    _L1_xattn_all = _L1_xattn_setup()
    _L1_xattn_in = {k: v for k, v in _L1_xattn_all.items() if k in ('ln_gamma', 'ln_beta', 'w_q', 'w_kv', 'w_out', 'b_out', 'gate')}
    del _L1_xattn_all

    def _L1_ffn_setup():
        import jax, jax.numpy as jnp
        import numpy as np
        B, T, D, H, E, K = (2, 256, 128, 512, 8, 2)
        EPS = 1e-12

        def moe_forward(x, Wg, bg, W1, b1, W2, b2):
            gates = jax.nn.softmax(x @ Wg + bg, axis=-1)
            _, top_idx = jax.lax.top_k(gates, K)
            mask = jax.nn.one_hot(top_idx, E, dtype=gates.dtype).sum(axis=-2)
            g = gates * mask
            g = g / jnp.maximum(jnp.sum(jnp.abs(g), axis=-1, keepdims=True), EPS)
            h = jnp.einsum('btd,edh->bteh', x, W1) + b1[None, None]
            h = jax.nn.gelu(h, approximate=False)
            eo = jnp.einsum('bteh,ehd->bted', h, W2) + b2[None, None]
            return jnp.einsum('bte,bted->btd', g, eo)
        key = jax.random.key(seed)
        ks = jax.random.split(key, 8)
        s_d = 1.0 / np.sqrt(D)
        s_h = 1.0 / np.sqrt(H)
        return {'x': jax.random.normal(ks[0], (B, T, D), dtype=jnp.float32), 'Wg': jax.random.uniform(ks[1], (D, E), jnp.float32, -s_d, s_d), 'bg': jax.random.uniform(ks[2], (E,), jnp.float32, -s_d, s_d), 'W1': jax.random.uniform(ks[3], (E, D, H), jnp.float32, -s_d, s_d), 'b1': jax.random.uniform(ks[4], (E, H), jnp.float32, -s_d, s_d), 'W2': jax.random.uniform(ks[5], (E, H, D), jnp.float32, -s_h, s_h), 'b2': jax.random.uniform(ks[6], (E, D), jnp.float32, -s_h, s_h)}
    _L1_ffn_all = _L1_ffn_setup()
    _L1_ffn_in = {k: v for k, v in _L1_ffn_all.items() if k in ('Wg', 'bg', 'W1', 'b1', 'W2', 'b2')}
    del _L1_ffn_all
    return {'x': x, 'ctx_1024': ctx_1024, 'L0_xattn_Wq': _L0_xattn_in['Wq'], 'L0_xattn_bq': _L0_xattn_in['bq'], 'L0_xattn_Wk': _L0_xattn_in['Wk'], 'L0_xattn_bk': _L0_xattn_in['bk'], 'L0_xattn_Wv': _L0_xattn_in['Wv'], 'L0_xattn_bv': _L0_xattn_in['bv'], 'L0_xattn_Wo': _L0_xattn_in['Wo'], 'L0_xattn_bo': _L0_xattn_in['bo'], 'L0_ffn_Win': _L0_ffn_in['Win'], 'L0_ffn_bin_': _L0_ffn_in['bin_'], 'L0_ffn_W1': _L0_ffn_in['W1'], 'L0_ffn_b1': _L0_ffn_in['b1'], 'L0_ffn_W2': _L0_ffn_in['W2'], 'L0_ffn_b2': _L0_ffn_in['b2'], 'L0_ffn_Wout': _L0_ffn_in['Wout'], 'L0_ffn_bout': _L0_ffn_in['bout'], 'L1_xattn_ln_gamma': _L1_xattn_in['ln_gamma'], 'L1_xattn_ln_beta': _L1_xattn_in['ln_beta'], 'L1_xattn_w_q': _L1_xattn_in['w_q'], 'L1_xattn_w_kv': _L1_xattn_in['w_kv'], 'L1_xattn_w_out': _L1_xattn_in['w_out'], 'L1_xattn_b_out': _L1_xattn_in['b_out'], 'L1_xattn_gate': _L1_xattn_in['gate'], 'L1_ffn_Wg': _L1_ffn_in['Wg'], 'L1_ffn_bg': _L1_ffn_in['bg'], 'L1_ffn_W1': _L1_ffn_in['W1'], 'L1_ffn_b1': _L1_ffn_in['b1'], 'L1_ffn_W2': _L1_ffn_in['W2'], 'L1_ffn_b2': _L1_ffn_in['b2']}

def reference(x, ctx_1024, L0_xattn_Wq, L0_xattn_bq, L0_xattn_Wk, L0_xattn_bk, L0_xattn_Wv, L0_xattn_bv, L0_xattn_Wo, L0_xattn_bo, L0_ffn_Win, L0_ffn_bin_, L0_ffn_W1, L0_ffn_b1, L0_ffn_W2, L0_ffn_b2, L0_ffn_Wout, L0_ffn_bout, L1_xattn_ln_gamma, L1_xattn_ln_beta, L1_xattn_w_q, L1_xattn_w_kv, L1_xattn_w_out, L1_xattn_b_out, L1_xattn_gate, L1_ffn_Wg, L1_ffn_bg, L1_ffn_W1, L1_ffn_b1, L1_ffn_W2, L1_ffn_b2):
    import jax
    import jax.numpy as jnp

    def _L0_xattn_ref(query, mem_state, top_k, Wq, bq, Wk, bk, Wv, bv, Wo, bo):
        import jax, jax.numpy as jnp
        import numpy as np
        B, T, S, D = (4, 256, 512, 128)
        TOP_K = 32

        def _read(query, mem_state, top_k, Wq, bq, Wk, bk, Wv, bv, Wo, bo):
            b, t, d = query.shape
            s = mem_state.shape[1]
            scale = 1.0 / np.sqrt(d)
            q = query @ Wq.T + bq
            k = mem_state @ Wk.T + bk
            v = mem_state @ Wv.T + bv
            scores = jnp.einsum('btd,bsd->bts', q, k) * scale
            if top_k < s:
                vals, idx = jax.lax.top_k(scores, top_k)
                b_ix = jnp.arange(b)[:, None, None]
                t_ix = jnp.arange(t)[None, :, None]
                masked = jnp.full_like(scores, -jnp.inf)
                scores = masked.at[b_ix, t_ix, idx].set(vals)
            attn = jax.nn.softmax(scores, axis=-1)
            ctx = jnp.einsum('bts,bsd->btd', attn, v)
            return ctx @ Wo.T + bo
        return _read(query, mem_state, top_k, Wq, bq, Wk, bk, Wv, bv, Wo, bo)

    def _L0_ffn_ref(x, Win, bin_, W1, b1, W2, b2, Wout, bout):
        import jax, jax.numpy as jnp
        import numpy as np
        D_MODEL = 128
        M = 64
        INNER = 16
        s = jnp.einsum('btd,dm->btm', x, Win) + bin_
        h = jax.nn.relu(s[..., None] * W1 + b1)
        g = jnp.einsum('btmh,mh->btm', h, W2) + b2
        out = jnp.einsum('btm,md->btd', g, Wout) + bout
        return out

    def _L1_xattn_ref(x, context, ln_gamma, ln_beta, w_q, w_kv, w_out, b_out, gate):
        import jax, jax.numpy as jnp
        import numpy as np
        DIM = 128
        NUM_HEADS = 16
        DIM_HEAD = 64
        INNER = NUM_HEADS * DIM_HEAD
        SCALE = DIM_HEAD ** (-0.5)

        def _layernorm(x, gamma, beta, eps=1e-05):
            mu = jnp.mean(x, axis=-1, keepdims=True)
            var = jnp.mean(jnp.square(x - mu), axis=-1, keepdims=True)
            return (x - mu) * jax.lax.rsqrt(var + eps) * gamma + beta
        B, SQ, _ = x.shape
        SK = context.shape[1]
        xn = _layernorm(x, ln_gamma, ln_beta)
        q = (xn @ w_q).reshape(B, SQ, NUM_HEADS, DIM_HEAD)
        kv = context @ w_kv
        k, v = jnp.split(kv, 2, axis=-1)
        k = k.reshape(B, SK, NUM_HEADS, DIM_HEAD)
        v = v.reshape(B, SK, NUM_HEADS, DIM_HEAD)
        scores = jnp.einsum('bqhd,bkhd->bhqk', q * SCALE, k)
        attn = jax.nn.softmax(scores, axis=-1)
        out = jnp.einsum('bhqk,bkhd->bqhd', attn, v).reshape(B, SQ, INNER)
        out = out @ w_out + b_out
        return out * jnp.tanh(gate[0])

    def _L1_ffn_ref(x, Wg, bg, W1, b1, W2, b2):
        import jax, jax.numpy as jnp
        import numpy as np
        B, T, D, H, E, K = (2, 256, 128, 512, 8, 2)
        EPS = 1e-12

        def moe_forward(x, Wg, bg, W1, b1, W2, b2):
            gates = jax.nn.softmax(x @ Wg + bg, axis=-1)
            _, top_idx = jax.lax.top_k(gates, K)
            mask = jax.nn.one_hot(top_idx, E, dtype=gates.dtype).sum(axis=-2)
            g = gates * mask
            g = g / jnp.maximum(jnp.sum(jnp.abs(g), axis=-1, keepdims=True), EPS)
            h = jnp.einsum('btd,edh->bteh', x, W1) + b1[None, None]
            h = jax.nn.gelu(h, approximate=False)
            eo = jnp.einsum('bteh,ehd->bted', h, W2) + b2[None, None]
            return jnp.einsum('bte,bted->btd', g, eo)
        return moe_forward(x, Wg, bg, W1, b1, W2, b2)
    x = x + _L0_xattn_ref(_layernorm(x, axis=-1), ctx_1024, 32, L0_xattn_Wq, L0_xattn_bq, L0_xattn_Wk, L0_xattn_bk, L0_xattn_Wv, L0_xattn_bv, L0_xattn_Wo, L0_xattn_bo)
    x = x + _L0_ffn_ref(_layernorm(x, axis=-1), L0_ffn_Win, L0_ffn_bin_, L0_ffn_W1, L0_ffn_b1, L0_ffn_W2, L0_ffn_b2, L0_ffn_Wout, L0_ffn_bout)
    x = x + _L1_xattn_ref(_layernorm(x, axis=-1), ctx_1024, L1_xattn_ln_gamma, L1_xattn_ln_beta, L1_xattn_w_q, L1_xattn_w_kv, L1_xattn_w_out, L1_xattn_b_out, L1_xattn_gate)
    x = x + _L1_ffn_ref(_layernorm(x, axis=-1), L1_ffn_Wg, L1_ffn_bg, L1_ffn_W1, L1_ffn_b1, L1_ffn_W2, L1_ffn_b2)
    return x

_drawn_inputs = setup_inputs


def setup_inputs(seed=0):
    import zlib

    import numpy as np

    out = dict(_drawn_inputs(seed))
    spreads = {'L0_xattn_bq': (0.0, 1.978),
     'L0_xattn_bk': (0.0, 2.0),
     'L0_xattn_bv': (0.0, 0.269),
     'L0_xattn_bo': (0.0, 0.1),
     'L1_xattn_ln_gamma': (1.0, 0.546),
     'L1_xattn_ln_beta': (0.0, 0.463),
     'L1_xattn_b_out': (0.0, 0.1)}
    factors = {'L0_xattn_Wq': 9.371,
     'L0_xattn_Wk': 2.9,
     'L0_ffn_bin_': 5.728,
     'L1_ffn_b1': 4.493,
     'L1_ffn_b2': 3.214}
    for name, (base, spread) in spreads.items():
        noise = np.random.default_rng([zlib.crc32(name.encode()), seed]).standard_normal(out[name].shape)
        drawn = base * np.exp(spread * noise) if base else spread * noise
        out[name] = jnp.asarray(drawn.astype(out[name].dtype))
    for name, factor in factors.items():
        out[name] = (out[name] * factor).astype(out[name].dtype)
    return out
```

```python
from contextlib import ExitStack

import concourse.bass as bass
from concourse import mybir

F32 = mybir.dt.float32
F32R = mybir.dt.float32r
I32 = mybir.dt.int32
U32 = mybir.dt.uint32
ALU = mybir.AluOpType
ACT = mybir.ActivationFunctionType
AX_X = mybir.AxisListType.X

P = 128
B = 32
J = 4
G = B // J
N = J * P
TOPK = 32
BLANK = -3.0e38
M, INNER = 64, 16
HT = M * INNER // P
HEADS, DH = 16, 64
QUADS = HEADS // 4 * J
E, HID = 8, 512
HC = HID // P
LN_EPS = 1e-5
GATE_EPS = 1e-12
LEAD = 1
A_PH, B_PH, C_PH, D_PH = range(4)


class Own:

    def __init__(self, eng, sem):
        self.eng, self.sem, self.base, self.n, self.i, self.per = eng, sem, 0, 0, 0, 0

    def round(self, i, per):
        self.i, self.per, self.n = i, per, 0

    def end_round(self):
        assert self.n == self.per, f"{self.n} marks in a round, {self.per} said"

    def end_loop(self, rounds):
        self.base += rounds * self.per
        self.i, self.per, self.n = 0, 0, 0

    def did(self, ins):
        ins.then_inc(self.sem, 1)
        self.n += 1
        return self.n

    def after(self, k=None):
        k = self.n if k is None else k
        self.eng.wait_ge(self.sem, self.i * self.per + (self.base + k))

    def after_apart(self, gone_by):
        self.after()
        self.eng.sem_inc(gone_by, 1)


def build(nc, t, out):
    with ExitStack() as ctx:
        def sb(name, shape, dt=F32):
            return ctx.enter_context(nc.sbuf_tensor(name, shape, dt))

        def sem(name):
            return ctx.enter_context(nc.semaphore(name))

        x_all = sb("x_all", [P, G, N])
        ctxT_all = sb("ctxT_all", [P, G, N])
        ctx_raw = sb("ctx_raw", [P, N])
        ident = sb("ident", [P, P])
        xn1 = ctx_raw[:, :]
        xn = sb("xn", [P, N])
        x32 = sb("x32", [P, N])
        xhi = sb("xhi", [P, N], F32R)
        xlo = sb("xlo", [P, N], F32R)
        stats = sb("stats", [P, J, 6])
        mv = sb("mv", [P, J, 2])
        var = sb("var", [P, J])
        nwt = sb("nwt", [P, 5, J])

        hid = sb("hid", [P, 8, N])
        w0raw = sb("w0raw", [P, 4, P])
        w0T = sb("w0T", [P, 3, P])
        wvo = sb("wvo", [P, P])
        ctxA = hid[:, 0, :]
        qA = hid[:, 1, :]
        kA = hid[:, 2, :]
        vA = hid[:, 3, :]
        sA = hid[:, 4, :]
        work = hid[:, 5, :]
        top8 = sb("top8", [P, 4, J, 8])
        negA = sb("negA", [P, J])
        eA = hid[:, 6, :]
        sumA = sb("sumA", [P, J])
        rA = sb("rA", [P, J])
        ptA = hid[:, 7, :]

        boA = sb("boA", [P, P])
        boB = sb("boB", [P, P])
        boC = sb("boC", [P, P])
        bo_in = sb("bo_in", [P, 3, P])
        rowsum = sb("rowsum", [P, P])

        vrows = sb("vrows", [8, P])
        w1row = sb("w1row", [HT, P])
        b1row = sb("b1row", [HT, P])
        binrow = sb("binrow", [HT, P])
        w2row = sb("w2row", [HT, P])
        crow = sb("crow", [HT, P])
        moe_b1row = sb("moe_b1row", [E * HC, P])
        cols = sb("cols", [P, 64])
        VC, CC, W2C, B1C = 0, 8, 16, 24
        bcol = sb("bcol", [P, 2, P])

        win = sb("win", [P, M])
        w2o = sb("w2o", [P, HT, P])
        wout0 = sb("wout0", [M, P])
        wzhi = sb("wzhi", [P, HT * P], F32R)
        wzlo = sb("wzlo", [P, HT * P], F32R)

        gate = sb("gate", [P, 1])
        tgate = sb("tgate", [P, 1])
        mhi = sb("mhi", [P, HEADS * P], F32R)
        mlo = sb("mlo", [P, HEADS * P], F32R)
        vohi = sb("vohi", [P, HEADS * P], F32R)
        volo = sb("volo", [P, HEADS * P], F32R)
        chi = sb("chi", [P, N], F32R)
        clo = sb("clo", [P, N], F32R)
        c32 = sb("c32", [P, N])
        vp = sb("vp", [P, 2, HEADS * P])
        qp = sb("qp", [P, HEADS, N // 2])
        pr = hid[:, 0:3, :]
        pt = hid[:, 3:5, :]
        nmax = sb("nmax", [P, 3, 4])
        psum_ = sb("psum_", [P, 3, 4])
        prec = sb("prec", [P, 3, 4])

        w1hi = sb("w1hi", [P, E * HID], F32R)
        w1lo = sb("w1lo", [P, E * HID], F32R)
        w2e = sb("w2e", [P, E * HC, P])
        wg = sb("wg", [P, E])
        bg = sb("bg", [P, E])
        b2e = sb("b2e", [E, P])
        iota = sb("iota", [P, E])
        iota_i = sb("iota_i", [P, E], I32)
        lg = sb("lg", [P, J, E])
        lmax = sb("lmax", [P, J])
        ge = sb("ge", [P, J, E])
        gs = sb("gs", [P, J])
        gr = sb("gr", [P, J])
        g8 = sb("g8", [P, J, 8])
        gi = sb("gi", [P, J, 8], U32)
        gif = sb("gif", [P, J, 8])
        gm = sb("gm", [P, 2, J, E])
        gw = sb("gw", [P, J, E])
        gT = ctx_raw[0:E, :]
        acc = c32

        vflat = vp[:, :, :].rearrange("p j n -> p (j n)")
        wq_raw = vflat[:, 0:1024]
        wkv_raw = vflat[:, 1024:3072]
        wo_raw = vflat[:, 3072:4096].rearrange("p (a n) -> p a n", n=P)
        w1_raw = vflat[:, 0:4096]
        qflat = qp[:, :, :].rearrange("p h n -> p (h n)")
        wT = [qflat[:, 1024 * k:1024 * (k + 1)].rearrange("p (a n) -> p a n", n=P) for k in range(3)]
        w1b = qflat[:, 3072:4096]
        eflat = w2e[:, :, :].rearrange("p a n -> p (a n)")
        wz32 = eflat[:, 0:1024]
        woutrep = eflat[:, 1024:2048].rearrange("p (k n) -> p k n", n=P)

        ps = ctx.enter_context(nc.psum_tensor("ps", [P, 8, N], F32))

        ld_w0 = sem("ld_w0")
        ld_rows = sem("ld_rows")
        ld_w = sem("ld_w")
        ld_e = sem("ld_e")
        ld_x = sem("ld_x")
        ld_ctx = sem("ld_ctx")
        ident_ok = sem("ident_ok")
        pool_own = sem("pool_own")
        dve_own = sem("dve_own")
        act_own = sem("act_own")
        gone_by = sem("gone_by")
        set_pe = sem("set_pe")
        set_act = sem("set_act")
        set_dve = sem("set_dve")
        xn_ok = sem("xn_ok")
        xn_turned = sem("xn_turned")
        x32_ok = sem("x32_ok")
        xsplit_ok = sem("xsplit_ok")
        ctx_turned = sem("ctx_turned")
        ctxA_ok = sem("ctxA_ok")
        x_done = [sem(f"x_done{p}") for p in range(3)]
        a_q, a_k, a_v, a_s, a_t, a_o = map(sem, ("a_q", "a_k", "a_v", "a_s", "a_t", "a_o"))
        a_qe, a_ke, a_ve, a_se, a_te = map(sem, ("a_qe", "a_ke", "a_ve", "a_se", "a_te"))
        a_first = sem("a_first")
        a_exp = sem("a_exp")
        a_p = sem("a_p")
        b_z, b_ra, b_rv, b_o = map(sem, ("b_z", "b_ra", "b_rv", "b_o"))
        c_fed, c_qe, c_ve, c_s, c_max = map(sem, ("c_fed", "c_qe", "c_ve", "c_s", "c_max"))
        c_exp, c_norm, c_t, c_te, c_pv = map(sem, ("c_exp", "c_norm", "c_t", "c_te", "c_pv"))
        c_csplit, c_c32 = sem("c_csplit"), sem("c_c32")
        d_lg, d_lgs, d_ex, d_gate, d_gt, d_gte, d_b2, d_init = map(
            sem, ("d_lg", "d_lgs", "d_ex", "d_gate", "d_gt", "d_gte", "d_b2", "d_init"))
        d_l1, d_g, d_l2, d_comb, d_store = map(sem, ("d_l1", "d_g", "d_l2", "d_comb", "d_store"))

        SIGNALS = {
            "pe": (xn_turned, ctx_turned, a_q, a_k, a_v, a_s, a_t, a_o, b_z, b_o, c_fed, c_s, c_t, c_pv, d_lg, d_gt, d_b2, d_l1, d_l2),
            "act": (x32_ok, ctxA_ok, a_qe, a_ke, a_ve, a_se, a_te, a_exp, b_ra, c_qe, c_exp, c_te, d_ex, d_g),
            "dve": (xn_ok, xsplit_ok, a_first, a_p, b_rv, c_ve, c_max, c_norm, c_csplit, d_lgs, d_gate, d_gte, d_init, d_comb, *x_done),
            "pool": (c_c32,),
        }

        def start(eng, who):
            for s in SIGNALS[who]:
                eng.sem_inc(s, LEAD)

        NW0, NROWS, NLW = 4, 23, 3

        def grp(a, i):
            return a[:, bass.ds(i, 1), :].rearrange("p a n -> p (a n)")

        def blk(a, j):
            return a[:, P * j:P * (j + 1)]

        def bank(b):
            return ps[:, b, :]

        def groups(eng, step):
            with eng.Fori(0, G - 1) as i:
                step(i, False)
            step(G - 1, True)

        FEEDS = []
        for s in range(QUADS):
            if s // 4 % 2 == 0:
                FEEDS += [("q", s, 0), ("q", s, 1)]
            FEEDS += [("v", s, 0)]
        NF = len(FEEDS)

        def q_before(f):
            return sum(kind == "q" for kind, _, _ in FEEDS[:f])

        def four_heads(w, s):
            return w[:, :].rearrange("p (g a o n) -> p g a o n", g=2, a=4, o=2)[:, s % 4 // 2, :, s % 2, :]

        TURN, CTURN = 7, 6

        block = ctx.enter_context(nc.Block())

        @block.sync
        def _(sp):
            sp.sem_inc(d_store, 16 * LEAD)
            for k, name in enumerate(("L0_xattn_Wq", "L0_xattn_Wk", "L0_xattn_Wv", "L0_xattn_Wo")):
                sp.dma_start(w0raw[:, k, :], t[name]).then_inc(ld_w0, 16)

            def row(a):
                return a.rearrange("(a n) -> a n", a=1)

            n = 0
            for r, name in enumerate(("L0_xattn_bq", "L0_xattn_bk", "L1_xattn_ln_gamma", "L1_xattn_ln_beta",
                                      "L0_xattn_bv")):
                sp.dma_start(vrows[r:r + 1, :], row(t[name])).then_inc(ld_rows, 16)
                n += 1
            sp.dma_start(vrows[5:6, 0:M], row(t["L0_ffn_b2"])).then_inc(ld_rows, 16)
            sp.dma_start(vrows[5:6, M:P], row(t["L0_ffn_b2"])).then_inc(ld_rows, 16)
            for r in (6, 7):
                sp.dma_start(vrows[r:r + 1, :], row(t["L0_xattn_bq"])).then_inc(ld_rows, 16)
            n += 4
            flat = "(k q) h -> k (q h)"
            sp.dma_start(w1row[:, :], t["L0_ffn_W1"].rearrange(flat, k=HT)).then_inc(ld_rows, 16)
            sp.dma_start(b1row[:, :], t["L0_ffn_b1"].rearrange(flat, k=HT)).then_inc(ld_rows, 16)
            sp.dma_start(w2row[:, :], t["L0_ffn_W2"].rearrange(flat, k=HT)).then_inc(ld_rows, 16)
            sp.dma_start(binrow[:, 0:M // HT], t["L0_ffn_bin_"].rearrange("(k q) -> k q", k=HT)).then_inc(ld_rows, 16)
            sp.dma_start(moe_b1row[:, :], t["L1_ffn_b1"].rearrange("e (c p) -> (e c) p", p=P)).then_inc(ld_rows, 16)
            for r, name in enumerate(("L0_xattn_bo", "L0_ffn_bout", "L1_xattn_b_out")):
                sp.dma_start(bo_in[:, r, :], row(t[name]).to_broadcast([P, P])).then_inc(ld_rows, 16)
            sp.dma_start(gate[:, :], row(t["L1_xattn_gate"]).to_broadcast([P, 1])).then_inc(ld_rows, 16)
            sp.dma_start(bg[:, :], row(t["L1_ffn_bg"]).to_broadcast([P, E])).then_inc(ld_rows, 16)
            sp.dma_start(wg[:, :], t["L1_ffn_Wg"]).then_inc(ld_rows, 16)
            sp.dma_start(b2e[:, :], t["L1_ffn_b2"]).then_inc(ld_rows, 16)
            sp.dma_start(win[:, :], t["L0_ffn_Win"]).then_inc(ld_rows, 16)
            sp.dma_start(wout0[:, :], t["L0_ffn_Wout"]).then_inc(ld_rows, 16)
            sp.dma_start(w1b, row(t["L0_ffn_W1"].rearrange("m h -> (m h)")).to_broadcast([P, M * INNER])).then_inc(ld_rows, 16)
            n += 15
            assert n + 0 == NROWS + 1, n
            wo4 = t["L0_ffn_Wout"].rearrange("(k q) n -> q k n", k=HT)
            for q in range(P // INNER):
                sp.dma_start(woutrep[INNER * q:INNER * (q + 1), :, :],
                             wo4[q:q + 1, :, :].to_broadcast([INNER, HT, P])).then_inc(ld_w, 16)
            sp.dma_start(wq_raw, t["L1_xattn_w_q"]).then_inc(ld_w, 16)
            sp.dma_start(wkv_raw, t["L1_xattn_w_kv"]).then_inc(ld_w, 16)
            sp.dma_start(wo_raw, t["L1_xattn_w_out"].rearrange("(a p) n -> p a n", p=P)).then_inc(ld_w, 16)
            sp.wait_ge(set_dve, 12)
            sp.dma_start(w1_raw.rearrange("p (e h) -> p e h", e=E), t["L1_ffn_W1"].rearrange("e p h -> p e h")).then_inc(ld_e, 16)
            sp.dma_start(w2e[:, :, :].rearrange("p (e c) n -> p e c n", e=E),
                         t["L1_ffn_W2"].rearrange("e (c p) n -> p e c n", p=P)).then_inc(ld_e, 16)
            out_v = out.rearrange("(g j) t d -> t g j d", j=J)
            with sp.Fori(0, G) as i:
                sp.wait_ge(d_comb, LEAD + E * i + E)
                sp.dma_start(out_v[:, bass.ds(i, 1), :, :].rearrange("t a j d -> t (a j) d"),
                             acc[:, :].rearrange("p (j d) -> p j d", j=J)).then_inc(d_store, 16)
            sp.wait_ge(d_store, 16 * LEAD + 16 * G)

        NROWS += 1
        NLW += P // INNER

        @block.gpsimd
        def _(pool):
            start(pool, "pool")
            pool.memset(ident[:, :], 0.0).then_inc(pool_own, 1)
            pool.iota(iota_i[:, :], pattern=[[1, E]], base=0, channel_multiplier=0).then_inc(pool_own, 1)
            pool.wait_ge(pool_own, 2)
            pool.affine_select(out=ident[:, :], in_=ident[:, :], compare_op=ALU.not_equal, fill=1.0, base=0,
                               pattern=[[-1, P]], channel_multiplier=1).then_inc(ident_ok, 1)
            pool.tensor_copy(iota[:, :], iota_i[:, :]).then_inc(ident_ok, 1)
            x_v = t["x"].rearrange("(g j) t d -> t g j d", j=J)
            c_v = t["ctx_1024"].rearrange("(g j) t d -> t g j d", j=J)
            with pool.Fori(0, G) as i:
                pool.dma_start(grp(x_all, i).rearrange("p (j d) -> p j d", j=J),
                               x_v[:, bass.ds(i, 1), :, :].rearrange("t a j d -> t (a j) d")).then_inc(ld_x, 16)
                pool.wait_ge(ctx_turned, LEAD + i)
                pool.sem_inc(gone_by, 1)
                pool.dma_start(ctx_raw[:, :].rearrange("p (j d) -> p j d", j=J),
                               c_v[:, bass.ds(i, 1), :, :].rearrange("t a j d -> t (a j) d")).then_inc(ld_ctx, 16)
                pool.wait_ge(ld_x, 16 * i + 16)
                pool.wait_ge(ld_ctx, 16 * i + 16)
            pool.wait_ge(ctxA_ok, LEAD + 2 * G)
            for j in range(J):
                pool.tensor_copy(blk(c32, j), ctxT_all[:, 0, P * j:P * (j + 1)]).then_inc(c_c32, 1)
            with pool.Fori(0, G - 1) as i:
                for j in range(J):
                    pool.wait_ge(c_s, LEAD + QUADS * i + 4 * j + 4)
                    pool.tensor_copy(blk(c32, j), blk(grp(ctxT_all, i + 1), j)).then_inc(c_c32, 1)

        @block.tensor
        def _(pe):
            start(pe, "pe")

            def turn(dst, src, n=P, mark=None):
                ins = pe.transpose(dst, src, ident[0:n, 0:n])
                if mark is not None:
                    ins.then_inc(mark, 1)

            def split_mm(dst, wh, wl, ah, al, mark=None):
                pe.matmul(dst, wh, ah, start=True, stop=False)
                pe.matmul(dst, wh, al, start=False, stop=False)
                ins = pe.matmul(dst, wl, ah, start=False, stop=True)
                if mark is not None:
                    ins.then_inc(mark, 1)

            def turn_x(n):
                pe.wait_ge(xn_ok, LEAD + n + 1)
                pe.wait_ge(x32_ok, LEAD + n)
                for j in range(J):
                    turn(blk(bank(TURN), j), blk(xn, j), mark=xn_turned if j == J - 1 else None)

            def turn_ctx(i):
                pe.wait_ge(ld_ctx, 16 * i + 16)
                pe.wait_ge(ctxA_ok, LEAD + 2 * i)
                for j in range(J):
                    turn(blk(bank(CTURN), j), blk(ctx_raw, j), mark=ctx_turned if j == J - 1 else None)

            pe.wait_ge(ident_ok, 2)
            pe.wait_ge(ld_w0, 16 * NW0)
            for k, w in enumerate((0, 1, 3)):
                turn(blk(bank(0), k), w0raw[:, w, :], mark=set_pe if k == 2 else None)
            pe.wait_ge(set_dve, 1)
            pe.wait_ge(ld_rows, 16 * NROWS)
            cb = bank(1)
            turn(cb[:, VC:VC + 8], vrows[:, :], 8)
            turn(cb[:, CC:CC + 8], crow[:, :], 8)
            turn(cb[:, W2C:W2C + 8], w2row[:, :], 8)
            turn(cb[:, B1C:B1C + 32], moe_b1row[:, :], 32, mark=set_pe)
            pe.wait_ge(set_act, 2)
            pe.wait_ge(set_dve, 2)
            pe.matmul(blk(bank(2), 0), w0raw[:, 2, :], w0T[:, 2, :], start=True, stop=True)
            pe.matmul(blk(bank(2), 1), bcol[:, 0, :], w0T[:, 2, :], start=True, stop=True)
            pe.matmul(blk(bank(2), 2), bcol[0:M, 1, :], wout0[:, :], start=True, stop=True).then_inc(set_pe, 1)
            pe.wait_ge(ld_w, 16 * NLW)
            for k in range(3):
                for half in range(2):
                    s = 2 * k + half
                    b = 3 + s % 3
                    if s >= 3:
                        pe.wait_ge(set_act, s)
                    for a in range(4):
                        src = (wq_raw if k == 0 else wkv_raw[:, 1024 * (k - 1):1024 * k])
                        turn(blk(bank(b), a), blk(src, 4 * half + a), mark=set_pe if a == 3 else None)
            for s in range(8):
                b = 3 + s % 3
                pe.wait_ge(set_act, min(8, 6 + s) if s < 3 else 8)
                if s >= 3:
                    pe.wait_ge(set_dve, 5 + s - 3)
                for a in range(4):
                    h = 8 * (s % 4 // 2) + 2 * a + s % 2
                    r = DH * (h % 2)
                    left, right = (wT[0], wT[1]) if s < 4 else (wT[2], wo_raw)
                    ins = pe.matmul(blk(bank(b), a), left[r:r + DH, h // 2, :], right[r:r + DH, h // 2, :],
                                    start=True, stop=True)
                ins.then_inc(set_pe, 1)
            pe.wait_ge(set_act, 9)

            def a_front(i, n):
                pe.wait_ge(x32_ok, LEAD + n + 1)
                if not isinstance(i, int) or i > 0:
                    pe.wait_ge(a_qe, LEAD + i)
                pe.matmul(bank(0), w0T[:, 0, :], x32[:, :], start=True, stop=True).then_inc(a_q, 1)
                pe.wait_ge(ctxA_ok, LEAD + 2 * i + 2)
                pe.wait_ge(a_ke, LEAD + i)
                pe.matmul(bank(1), w0T[:, 1, :], ctxA, start=True, stop=True).then_inc(a_k, 1)
                pe.wait_ge(a_ve, LEAD + i)
                for j in range(J):
                    ins = pe.matmul(blk(bank(2), j), blk(ctxA, j), wvo[:, :], start=True, stop=True)
                ins.then_inc(a_v, 1)
                pe.wait_ge(a_qe, LEAD + i + 1)
                pe.wait_ge(a_ke, LEAD + i + 1)
                pe.wait_ge(a_se, LEAD + i)
                for j in range(J):
                    ins = pe.matmul(blk(bank(3), j), blk(qA, j), blk(kA, j), start=True, stop=True)
                ins.then_inc(a_s, 1)

            def a_step(i, last):
                turn_x(i + 1)
                if not last:
                    turn_ctx(i + 1)
                    a_front(i + 1, i + 1)
                pe.wait_ge(a_p, LEAD + J * i + J)
                pe.wait_ge(a_te, LEAD + i)
                for j in range(J):
                    turn(blk(bank(4), j), blk(eA, j), mark=a_t if j == J - 1 else None)
                pe.wait_ge(a_te, LEAD + i + 1)
                pe.wait_ge(a_ve, LEAD + i + 1)
                pe.wait_ge(x_done[A_PH], LEAD + J * i)
                for j in range(J):
                    ins = pe.matmul(blk(bank(5), j), blk(ptA, j), blk(vA, j), start=True, stop=True)
                ins.then_inc(a_o, 1)

            turn_x(0)
            turn_ctx(0)
            a_front(0, 0)
            groups(pe, a_step)

            def b_step(i, last):
                n = G * B_PH + i
                pe.wait_ge(xsplit_ok, LEAD + i + 1)
                for k in range(HT):
                    s, per = (b_ra, b_rv)[k % 2], HT // 2
                    pe.wait_ge(s, LEAD + per * i + (k // 2 - 1 if k >= 4 else 0))
                    w = slice(P * k, P * (k + 1))
                    split_mm(bank(k % 4), wzhi[:, w], wzlo[:, w], xhi[:, :], xlo[:, :], mark=b_z)
                pe.wait_ge(b_ra, LEAD + 4 * i + 4)
                pe.wait_ge(b_rv, LEAD + 4 * i + 4)
                pe.wait_ge(x_done[B_PH], LEAD + J * i)
                for j in range(J):
                    for k in range(HT):
                        ins = pe.matmul(blk(bank(4 + j // 2), j % 2), blk(hid[:, k, :], j), w2o[:, k, :],
                                        start=(k == 0), stop=(k == HT - 1))
                    if j % 2:
                        ins.then_inc(b_o, 1)
                    if j == 1:
                        turn_x(n + 1)

            pe.wait_ge(a_te, LEAD + G)
            pe.wait_ge(a_se, LEAD + G)
            pe.wait_ge(x_done[A_PH], LEAD + B)
            groups(pe, b_step)

            def c_step(i, last):
                n = G * C_PH + i

                def feed_bank(f):
                    if f < 2:
                        pe.wait_ge(c_ve, LEAD + QUADS * i)
                        pe.wait_ge(c_qe, LEAD + 16 * i)
                    else:
                        kind, s, a = FEEDS[f - 2]
                        if kind == "q":
                            pe.wait_ge(c_qe, LEAD + 16 * i + q_before(f - 2) + 1)
                        else:
                            pe.wait_ge(c_ve, LEAD + QUADS * i + s + 1)
                    return bank(4 + f % 2)

                def feed_q(f):
                    b = feed_bank(f)
                    _, s, a = FEEDS[f]
                    c = slice(0, N // 2) if s < 8 else slice(N // 2, N)
                    for k in range(2):
                        h = 4 * (s % 4) + 2 * a + k
                        w = slice(P * h, P * (h + 1))
                        split_mm(b[:, N // 2 * k:N // 2 * (k + 1)], mhi[:, w], mlo[:, w], xhi[:, c], xlo[:, c],
                                 mark=c_fed if k else None)

                def feed_v(f):
                    b = feed_bank(f)
                    _, s, _ = FEEDS[f]
                    j, q = s // 4, s % 4
                    if q == 0:
                        pe.wait_ge(c_csplit, LEAD + J * i + j + 1)
                    w = slice(N * q, N * (q + 1))
                    split_mm(b, blk(chi, j), blk(clo, j), vohi[:, w], volo[:, w], mark=c_fed)

                def scores(s):
                    j, q = s // 4, s % 4
                    if q == 0:
                        pe.wait_ge(c_c32, LEAD + J * i + j + 1)
                    if j % 2 == 0:
                        pe.wait_ge(c_qe, LEAD + 16 * i + 8 * (j // 2) + 2 * q + 2)
                    pe.wait_ge(c_exp, LEAD + QUADS * i + max(s - 2, 0))
                    for a in range(4):
                        ins = pe.matmul(blk(bank(s % 3), a), blk(qp[:, 4 * q + a, :], j % 2), blk(c32, j),
                                        start=True, stop=True)
                    ins.then_inc(c_s, 1)

                def turn_p(s):
                    pe.wait_ge(c_norm, LEAD + QUADS * i + s + 1)
                    pe.wait_ge(c_te, LEAD + QUADS * i + s)
                    for a in range(4):
                        turn(blk(bank(3), a), blk(pr[:, s % 3, :], a), mark=c_t if a == 3 else None)

                def attend(s):
                    j, q = s // 4, s % 4
                    pe.wait_ge(c_te, LEAD + QUADS * i + s + 1)
                    pe.wait_ge(c_ve, LEAD + QUADS * i + s + 1)
                    if q == 0:
                        pe.wait_ge(x_done[C_PH], LEAD + J * i + j)
                    for a in range(4):
                        h = 4 * q + a
                        ins = pe.matmul(bank(6)[:, 0:P], blk(pt[:, s % 2, :], a), blk(vp[:, j % 2, :], h),
                                        start=(h == 0), stop=(h == HEADS - 1))
                    ins.then_inc(c_pv, 1)

                pe.wait_ge(xsplit_ok, LEAD + G + i + 1)
                for s in range(QUADS + 3):
                    if s < QUADS:
                        for f, (kind, fs, _) in enumerate(FEEDS):
                            if fs == s:
                                (feed_q if kind == "q" else feed_v)(f)
                        scores(s)
                    if 2 <= s < QUADS + 2:
                        turn_p(s - 2)
                    if s >= 3:
                        attend(s - 3)
                    if s == (15 if last else 9):
                        turn_x(n + 1)

            pe.wait_ge(x_done[B_PH], LEAD + B)
            groups(pe, c_step)

            def d_step(i, last):
                n = G * D_PH + i

                def layer1(e):
                    for c in range(HC):
                        if e == 0:
                            pe.wait_ge(d_g, LEAD + E * HC * i)
                        else:
                            pe.wait_ge(d_g, LEAD + E * HC * i + HC * (e - 1) + c + 1)
                        w = slice(HID * e + P * c, HID * e + P * (c + 1))
                        split_mm(bank(c), w1hi[:, w], w1lo[:, w], xhi[:, :], xlo[:, :], mark=d_l1)

                def layer2(e):
                    pe.wait_ge(d_g, LEAD + E * HC * i + HC * (e + 1))
                    pe.wait_ge(d_comb, LEAD + E * i + max(e - 1, 0))
                    for j in range(J):
                        for c in range(HC):
                            ins = pe.matmul(blk(bank(4 + e % 2), j), blk(hid[:, HC * (e % 2) + c, :], j),
                                            w2e[:, HC * e + c, :], start=(c == 0), stop=(c == HC - 1))
                    ins.then_inc(d_l2, 1)

                pe.wait_ge(x32_ok, LEAD + n + 1)
                pe.wait_ge(d_init, LEAD + i)
                for j in range(J):
                    ins = pe.matmul(bank(6)[:, E * j:E * (j + 1)], blk(x32, j), wg[:, :], start=True, stop=True)
                ins.then_inc(d_lg, 1)
                pe.wait_ge(xsplit_ok, LEAD + 2 * G + i + 1)
                for s in range(E + 1):
                    if s < E:
                        layer1(s)
                    if s == 2:
                        pe.wait_ge(d_gate, LEAD + i + 1)
                        for j in range(J):
                            ins = pe.transpose(bank(6)[0:E, P * j:P * (j + 1)], gw[:, j, :], ident[:, :])
                        ins.then_inc(d_gt, 1)
                    if s >= 1:
                        layer2(s - 1)
                    if s == 2:
                        pe.wait_ge(d_gte, LEAD + i + 1)
                        for j in range(J):
                            ins = pe.matmul(blk(bank(6), j), gT[:, P * j:P * (j + 1)], b2e[:, :], start=True, stop=True)
                        ins.then_inc(d_b2, 1)
                    if s == 6 and not last:
                        turn_x(n + 1)

            pe.wait_ge(x_done[C_PH], LEAD + B)
            pe.wait_ge(c_te, LEAD + QUADS * G)
            groups(pe, d_step)

        @block.scalar
        def _(act):
            start(act, "act")

            def empty_turn(n, aff, *freed):
                act.wait_ge(xn_turned, LEAD + n + 1)
                for s, v in freed:
                    act.wait_ge(s, LEAD + v)
                if aff:
                    act.activation(x32[:, :], bank(TURN), ACT.Identity, scale=cols[:, VC + 2:VC + 3],
                                   bias=cols[:, VC + 3:VC + 4]).then_inc(x32_ok, 1)
                else:
                    act.activation(x32[:, :], bank(TURN), ACT.Copy).then_inc(x32_ok, 1)

            def empty_ctx(i):
                act.wait_ge(ctx_turned, LEAD + i + 1)
                act.wait_ge(a_v, LEAD + i)
                act.wait_ge(a_k, LEAD + i)
                act.activation(ctxA, bank(CTURN), ACT.Copy).then_inc(ctxA_ok, 1)
                act.activation(grp(ctxT_all, i), bank(CTURN), ACT.Copy).then_inc(ctxA_ok, 1)

            act.wait_ge(set_pe, 1)
            act.activation(w0T[:, :, :].rearrange("p a n -> p (a n)"), bank(0)[:, 0:3 * P], ACT.Copy).then_inc(set_act, 1)
            act.wait_ge(set_pe, 2)
            act.activation(cols[:, 0:B1C + 32], bank(1)[:, 0:B1C + 32], ACT.Copy).then_inc(set_act, 1)
            act.wait_ge(ld_rows, 16 * NROWS)
            act.activation(tgate[:, :], gate[:, :], ACT.Tanh).then_inc(act_own, 1)
            for s in range(6):
                act.wait_ge(set_pe, 4 + s)
                act.activation(wT[s // 2][:, 4 * (s % 2):4 * (s % 2) + 4, :].rearrange("p a n -> p (a n)"),
                               bank(3 + s % 3), ACT.Copy).then_inc(set_act, 1)
            act.wait_ge(act_own, 1)
            for s in range(8):
                act.wait_ge(set_pe, 10 + s)
                src = bank(3 + s % 3).rearrange("p (a n) -> p a n", n=P)
                if s < 4:
                    act.activation(four_heads(mhi, s), src, ACT.Copy, scale=-1.0 / 8).then_inc(act_own, 1)
                else:
                    act.activation(four_heads(vohi, s), src, ACT.Copy, scale=tgate[:, 0:1]).then_inc(act_own, 1)
            act.wait_ge(set_pe, 3)
            act.activation(wvo[:, :], blk(bank(2), 0), ACT.Copy).then_inc(set_act, 1)

            def a_front(i):
                act.wait_ge(a_q, LEAD + i + 1)
                act.wait_ge(a_s, LEAD + i)
                act.activation(qA, bank(0), ACT.Identity, bias=cols[:, VC:VC + 1]).then_inc(a_qe, 1)
                act.wait_ge(a_k, LEAD + i + 1)
                act.activation(kA, bank(1), ACT.Identity, bias=cols[:, VC + 1:VC + 2]).then_inc(a_ke, 1)

            def scores_out(i):
                act.wait_ge(a_s, LEAD + i + 1)
                act.activation(sA, bank(3), ACT.Copy, scale=P ** -0.5).then_inc(a_se, 1)

            def values_out(i):
                act.wait_ge(a_v, LEAD + i + 1)
                act.wait_ge(a_o, LEAD + i)
                act.activation(vA, bank(2), ACT.Copy).then_inc(a_ve, 1)

            def a_step(i, last):
                if last:
                    empty_turn(i + 1, False, (a_q, i + 1))
                else:
                    empty_turn(i + 1, False, (a_q, i + 1))
                    empty_ctx(i + 1)
                    a_front(i + 1)
                act.wait_ge(a_first, LEAD + i + 1)
                act.wait_ge(a_se, LEAD + i + 1)
                act.wait_ge(a_t, LEAD + i)
                for j in range(J):
                    ins = act.activation(blk(eA, j), blk(sA, j), ACT.Exp, bias=negA[:, j:j + 1])
                ins.then_inc(a_exp, 1)
                if not last:
                    act.wait_ge(a_exp, LEAD + i + 1)
                    scores_out(i + 1)
                act.wait_ge(a_t, LEAD + i + 1)
                act.wait_ge(a_o, LEAD + i)
                act.activation(ptA, bank(4), ACT.Copy).then_inc(a_te, 1)
                if not last:
                    values_out(i + 1)

            empty_turn(0, False)
            empty_ctx(0)
            a_front(0)
            scores_out(0)
            values_out(0)
            groups(act, a_step)
            act.wait_ge(ld_e, 32)
            act.activation(w1hi[:, :], w1_raw, ACT.Copy).then_inc(act_own, 1)

            def b_step(i, last):
                n = G * B_PH + i
                act.wait_ge(b_o, LEAD + 2 * i)
                for k in range(0, HT, 2):
                    act.wait_ge(b_z, LEAD + HT * i + k + 1)
                    act.activation(hid[:, k, :], bank(k % 4), ACT.Relu, bias=cols[:, CC + k:CC + k + 1]).then_inc(b_ra, 1)
                empty_turn(n + 1, last, (b_z, HT * i + HT))

            groups(act, b_step)

            def c_step(i, last):
                n = G * C_PH + i
                for s in range(QUADS + 3):
                    for f, (kind, fs, a) in enumerate(FEEDS):
                        if fs == s and kind == "q":
                            h = 4 * (s % 4) + 2 * a
                            act.wait_ge(c_fed, LEAD + NF * i + f + 1)
                            act.activation(qp[:, h:h + 2, :].rearrange("p h n -> p (h n)"), bank(4 + f % 2),
                                           ACT.Copy).then_inc(c_qe, 1)
                    if s < QUADS:
                        r = s % 3
                        act.wait_ge(c_max, LEAD + QUADS * i + s + 1)
                        if s >= 3:
                            act.wait_ge(c_t, LEAD + QUADS * i + s - 2)
                        for a in range(4):
                            ins = act.activation(blk(pr[:, r, :], a), blk(bank(r), a), ACT.Exp, scale=-1.0,
                                                 bias=nmax[:, r, a:a + 1], accum_out=psum_[:, r, a:a + 1])
                        ins.then_inc(c_exp, 1)
                    if 2 <= s < QUADS + 2:
                        act.wait_ge(c_t, LEAD + QUADS * i + s - 1)
                        if s >= 4:
                            act.wait_ge(c_pv, LEAD + QUADS * i + s - 3)
                        act.activation(pt[:, s % 2, :], bank(3), ACT.Copy).then_inc(c_te, 1)
                    if s == (15 if last else 12):
                        empty_turn(n + 1, not last, (c_fed, NF * i + 27))

            groups(act, c_step)

            def d_step(i, last):
                n = G * D_PH + i
                act.wait_ge(d_lgs, LEAD + i + 1)
                act.activation(ge[:, :, :], lg[:, :, :], ACT.Exp).then_inc(d_ex, 1)
                for e in range(E):
                    if e >= 2:
                        act.wait_ge(d_l2, LEAD + E * i + e - 1)
                    else:
                        act.wait_ge(d_l2, LEAD + E * i)
                    for c in range(HC):
                        act.wait_ge(d_l1, LEAD + E * HC * i + HC * e + c + 1)
                        act.activation(hid[:, HC * (e % 2) + c, :], bank(c), ACT.Gelu,
                                       bias=cols[:, B1C + HC * e + c:B1C + HC * e + c + 1]).then_inc(d_g, 1)
                if not last:
                    empty_turn(n + 1, False, (d_l1, E * HC * i + E * HC))

            groups(act, d_step)

        @block.vector
        def _(dve):
            start(dve, "dve")
            own = Own(dve, dve_own)

            def rstd(into):
                own.after()
                own.did(dve.tensor_scalar(nwt[:, 0, :].bitcast(I32), var[:, :].bitcast(I32), 1, None,
                                          ALU.arith_shift_right))
                own.after()
                own.did(dve.tensor_scalar(nwt[:, 1, :].bitcast(I32), nwt[:, 0, :].bitcast(I32), -1.0,
                                          float(0x5F3759DF), ALU.mult, ALU.add))
                y = 1
                for k in range(4):
                    z = into if k == 3 else nwt[:, 4 if y == 1 else 1, :]
                    own.after()
                    own.did(dve.tensor_tensor(nwt[:, 2, :], nwt[:, y, :], nwt[:, y, :], ALU.mult))
                    own.after()
                    own.did(dve.scalar_tensor_tensor(nwt[:, 3, :], nwt[:, 2, :], -0.5, var[:, :], ALU.mult, ALU.mult))
                    own.after()
                    own.did(dve.scalar_tensor_tensor(z, nwt[:, 3, :], 1.5, nwt[:, y, :], ALU.add, ALU.mult))
                    y = 4 if y == 1 else 1

            def norm(src, dst, mark=None):
                for j in range(J):
                    own.did(dve.bn_stats(stats[:, j, :], blk(src, j)))
                own.after_apart(gone_by)
                for j in range(J):
                    own.did(dve.bn_aggr(mv[:, j, :], stats[:, j, :]))
                own.after()
                own.did(dve.tensor_scalar(var[:, :], mv[:, :, 1], LN_EPS, None, ALU.add))
                rstd(nwt[:, 0, :])
                own.after()
                for j in range(J):
                    ins = dve.tensor_scalar(blk(dst, j), blk(src, j), mv[:, j, 0:1], nwt[:, 0, j:j + 1],
                                            ALU.subtract, ALU.mult)
                    if mark is None or j < J - 1:
                        own.did(ins)
                    else:
                        ins.then_inc(mark, 1)

            NORM = 8 + 1 + 2 + 12 + 3

            def norm_x(n, src, twice):
                dve.wait_ge(xn_turned, LEAD + n)
                if twice:
                    norm(src, xn1)
                    own.after()
                    norm(xn1, xn, xn_ok)
                else:
                    norm(src, xn, xn_ok)

            def split_x(n):
                dve.wait_ge(x32_ok, LEAD + n + 1)
                own.did(dve.tensor_copy(xhi[:, :], x32[:, :]))
                own.after()
                dve.tensor_tensor(xlo[:, :], x32[:, :], xhi[:, :].bitcast(F32), ALU.subtract).then_inc(xsplit_ok, 1)

            def update(src, i, j, bias, done):
                own.did(dve.tensor_tensor(rowsum[:, :], src, bias[:, :], ALU.add))
                own.after()
                xj = blk(grp(x_all, i), j)
                dve.tensor_tensor(xj, xj, rowsum[:, :], ALU.add).then_inc(done, 1)

            dve.wait_ge(ld_rows, 16 * NROWS)
            hb = crow[:, :].rearrange("k (q h) -> k q h", h=INNER)
            own.did(dve.tensor_tensor(hb, w1row[:, :].rearrange("k (q h) -> k q h", h=INNER),
                                      binrow[:, 0:M // HT].unsqueeze(2).to_broadcast([HT, M // HT, INNER]), ALU.mult))
            own.after()
            dve.tensor_tensor(crow[:, :], crow[:, :], b1row[:, :], ALU.add).then_inc(set_dve, 1)
            own.did(dve.tensor_tensor(wz32.rearrange("p (m h) -> p m h", h=INNER),
                                      w1b.rearrange("p (m h) -> p m h", h=INNER),
                                      win[:, :].unsqueeze(2).to_broadcast([P, M, INNER]), ALU.mult))
            dve.wait_ge(set_act, 2)
            own.did(dve.tensor_copy(bcol[:, 0, :], cols[:, VC + 4:VC + 5].to_broadcast([P, P])))
            dve.tensor_copy(bcol[0:M, 1, :], cols[0:M, VC + 5:VC + 6].to_broadcast([M, P])).then_inc(set_dve, 1)
            own.after()
            own.did(dve.tensor_copy(wzhi[:, :], wz32))
            own.after()
            dve.tensor_tensor(wzlo[:, :], wz32, wzhi[:, :].bitcast(F32), ALU.subtract).then_inc(set_dve, 1)
            dve.wait_ge(ld_w, 16 * NLW)
            for k in range(HT):
                ins = dve.tensor_scalar(w2o[:, k, :], woutrep[:, k, :], cols[:, W2C + k:W2C + k + 1], None, ALU.mult)
            ins.then_inc(set_dve, 1)
            for s in range(8):
                dve.wait_ge(act_own, 2 + s)
                src = bank(3 + s % 3).rearrange("p (a n) -> p a n", n=P)
                if s < 4:
                    dve.scalar_tensor_tensor(four_heads(mlo, s), src, -1.0 / 8, four_heads(mhi, s).bitcast(F32),
                                             ALU.mult, ALU.subtract).then_inc(set_dve, 1)
                else:
                    dve.scalar_tensor_tensor(four_heads(volo, s), src, tgate[:, 0:1], four_heads(vohi, s).bitcast(F32),
                                             ALU.mult, ALU.subtract).then_inc(set_dve, 1)
            dve.wait_ge(set_act, 9)
            own.did(dve.tensor_tensor(boA[:, :], blk(bank(2), 1), bo_in[:, 0, :], ALU.add))
            own.did(dve.tensor_tensor(boB[:, :], blk(bank(2), 2), bo_in[:, 1, :], ALU.add))
            own.did(dve.tensor_scalar(boC[:, :], bo_in[:, 2, :], tgate[:, 0:1], None, ALU.mult))

            dve.wait_ge(ld_x, 16)
            norm_x(0, x_all[:, 0, :], False)
            own.base += own.n
            own.n = 0

            def a_step(i, last):
                if last:
                    dve.wait_ge(x_done[A_PH], LEAD + J)
                    norm_x(i + 1, x_all[:, 0, :], False)
                else:
                    dve.wait_ge(ld_x, 16 * (i + 1) + 16)
                    norm_x(i + 1, grp(x_all, i + 1), False)
                dve.wait_ge(a_se, LEAD + i + 1)
                dve.sem_inc(gone_by, 1)
                for r in range(TOPK // 8):
                    for j in range(J):
                        own.did(dve.max(top8[:, r, j, :], blk(sA if r == 0 else work, j)))
                    if r == 0:
                        own.after()
                        dve.wait_ge(a_exp, LEAD + i)
                        own.did(dve.tensor_scalar(negA[:, :], top8[:, 0, :, 0], -1.0, None, ALU.mult))
                    own.after_apart(gone_by)
                    for j in range(J):
                        ins = dve.match_replace(blk(work, j), top8[:, r, j, :], blk(sA if r == 0 else work, j), BLANK)
                        if r == 0 and j == J - 1:
                            ins.then_inc(a_first, 1)
                            dve.wait_ge(a_first, LEAD + i + 1)
                        else:
                            own.did(ins)
                    own.after_apart(gone_by)
                dve.wait_ge(a_exp, LEAD + i + 1)
                for j in range(J):
                    ins = dve.scalar_tensor_tensor(blk(eA, j), blk(work, j), BLANK, blk(eA, j), ALU.is_equal, ALU.mult,
                                                   accum_out=sumA[:, j:j + 1])
                    ins.then_inc(a_p, 1)
                dve.wait_ge(a_p, LEAD + J * i + J)
                own.did(dve.reciprocal(rA[:, :], sumA[:, :]))
                dve.wait_ge(a_o, LEAD + i + 1)
                own.after()
                for j in range(J):
                    own.did(dve.scalar_tensor_tensor(rowsum[:, :], blk(bank(5), j), rA[:, j:j + 1], boA[:, :],
                                                     ALU.mult, ALU.add))
                    own.after()
                    xj = blk(grp(x_all, i), j)
                    dve.tensor_tensor(xj, xj, rowsum[:, :], ALU.add).then_inc(x_done[A_PH], 1)
                    dve.wait_ge(x_done[A_PH], LEAD + J * i + j + 1)
                if last:
                    split_x(i + 1)

            def run(step, per, extra=0):
                with dve.Fori(0, G - 1) as i:
                    own.round(i, per)
                    step(i, False)
                    own.end_round()
                own.end_loop(G - 1)
                own.round(0, per + extra)
                step(G - 1, True)
                own.end_round()
                own.end_loop(1)

            run(a_step, NORM + 1 + 32 - 1 + 1 + J + 32 - 32, 1)

            def b_step(i, last):
                n = G * B_PH + i
                dve.wait_ge(b_o, LEAD + 2 * i)
                for k in range(1, HT, 2):
                    dve.wait_ge(b_z, LEAD + HT * i + k + 1)
                    dve.tensor_scalar(hid[:, k, :], bank(k % 4), cols[:, CC + k:CC + k + 1], 0.0,
                                      ALU.add, ALU.max).then_inc(b_rv, 1)
                if last:
                    dve.wait_ge(x_done[B_PH], LEAD + J)
                    norm_x(n + 1, x_all[:, 0, :], True)
                else:
                    norm_x(n + 1, grp(x_all, i + 1), False)
                for half in range(2):
                    dve.wait_ge(b_o, LEAD + 2 * i + half + 1)
                    for j in range(2 * half, 2 * half + 2):
                        update(blk(bank(4 + half), j % 2), i, j, boB, x_done[B_PH])
                        dve.wait_ge(x_done[B_PH], LEAD + J * i + j + 1)
                    if half == 0:
                        split_x(n + 1)

            dve.wait_ge(act_own, 10)
            own.did(dve.tensor_tensor(w1lo[:, :], w1_raw, w1hi[:, :].bitcast(F32), ALU.subtract))
            own.base += own.n
            own.n = 0
            dve.wait_ge(x_done[A_PH], LEAD + B)
            run(b_step, NORM + J + 1, NORM + 1)

            def split_ctx(src, j):
                own.did(dve.tensor_copy(blk(chi, j), src))
                own.after()
                dve.tensor_tensor(blk(clo, j), src, blk(chi, j).bitcast(F32), ALU.subtract).then_inc(c_csplit, 1)

            def c_step(i, last):
                n = G * C_PH + i
                for s in range(QUADS + 4):
                    if s >= 7 and (s - 7) % 4 == 0:
                        j = (s - 7) // 4
                        dve.wait_ge(c_pv, LEAD + QUADS * i + 4 * j + 4)
                        update(bank(6)[:, 0:P], i, j, boC, x_done[C_PH])
                        dve.wait_ge(x_done[C_PH], LEAD + J * i + j + 1)
                    if s < QUADS:
                        f = FEEDS.index(("v", s, 0))
                        dve.wait_ge(c_fed, LEAD + NF * i + f + 1)
                        dve.tensor_copy(vp[:, s // 4 % 2, N * (s % 4):N * (s % 4 + 1)], bank(4 + f % 2)).then_inc(c_ve, 1)
                        dve.wait_ge(c_s, LEAD + QUADS * i + s + 1)
                        dve.tensor_reduce(nmax[:, s % 3, :], bank(s % 3).rearrange("p (a n) -> p a n", n=P),
                                          AX_X, ALU.min).then_inc(c_max, 1)
                    if 1 <= s < QUADS + 1:
                        r = (s - 1) % 3
                        dve.wait_ge(c_exp, LEAD + QUADS * i + s)
                        own.did(dve.reciprocal(prec[:, r, :], psum_[:, r, :]))
                        own.after()
                        pv = pr[:, r, :].rearrange("p (a n) -> p a n", n=P)
                        dve.tensor_tensor(pv, pv, prec[:, r, :].unsqueeze(2).to_broadcast([P, 4, P]),
                                          ALU.mult).then_inc(c_norm, 1)
                    if s == 6:
                        if last:
                            dve.wait_ge(x_done[C_PH], LEAD + 1)
                        else:
                            norm_x(n + 1, grp(x_all, i + 1), True)
                    if s == 13 and last:
                        dve.wait_ge(x_done[C_PH], LEAD + J * i)
                        norm_x(n + 1, x_all[:, 0, :], False)
                    if s == (16 if last else 13):
                        split_x(n + 1)
                    if s >= 5 and (s - 5) % 4 == 0 and not last:
                        j = (s - 5) // 4
                        if j < J:
                            split_ctx(blk(grp(ctxT_all, i + 1), j), j)

            dve.wait_ge(x_done[B_PH], LEAD + B)
            for j in range(J):
                split_ctx(ctxT_all[:, 0, P * j:P * (j + 1)], j)
            own.base += J
            own.n = 0
            run(c_step, QUADS + 2 * NORM + 1 + 1 + J + J, -NORM - 1 - J)

            def d_step(i, last):
                n = G * D_PH + i
                bcast = lambda a: a.unsqueeze(2).to_broadcast([P, J, E])
                dve.wait_ge(d_lg, LEAD + i + 1)
                own.did(dve.tensor_tensor(lg[:, :, :], bank(6)[:, 0:J * E].rearrange("p (j e) -> p j e", e=E),
                                          bg[:, :].unsqueeze(1).to_broadcast([P, J, E]), ALU.add))
                own.after()
                own.did(dve.tensor_reduce(lmax[:, :], lg[:, :, :], AX_X, ALU.max))
                own.after()
                dve.tensor_tensor(lg[:, :, :], lg[:, :, :], bcast(lmax[:, :]), ALU.subtract).then_inc(d_lgs, 1)
                dve.wait_ge(d_ex, LEAD + i + 1)
                own.did(dve.tensor_reduce(gs[:, :], ge[:, :, :], AX_X, ALU.add))
                own.after()
                own.did(dve.reciprocal(gr[:, :], gs[:, :]))
                own.after()
                own.did(dve.tensor_tensor(lg[:, :, :], ge[:, :, :], bcast(gr[:, :]), ALU.mult))
                own.after_apart(gone_by)
                for j in range(J):
                    own.did(dve.max(g8[:, j, :], lg[:, j, :]))
                own.after_apart(gone_by)
                for j in range(J):
                    own.did(dve.max_index(gi[:, j, :], g8[:, j, :], lg[:, j, :]))
                own.after()
                own.did(dve.tensor_copy(gif[:, :, :], gi[:, :, :]))
                own.after()
                for k in range(2):
                    own.did(dve.tensor_tensor(gm[:, k, :, :], iota[:, :].unsqueeze(1).to_broadcast([P, J, E]),
                                              bcast(gif[:, :, k]), ALU.is_equal))
                own.after()
                own.did(dve.tensor_tensor(gm[:, 0, :, :], gm[:, 0, :, :], gm[:, 1, :, :], ALU.add))
                own.after()
                own.did(dve.tensor_tensor(ge[:, :, :], lg[:, :, :], gm[:, 0, :, :], ALU.mult))
                own.after()
                own.did(dve.tensor_reduce(gs[:, :], ge[:, :, :], AX_X, ALU.add))
                own.after()
                own.did(dve.tensor_scalar(gs[:, :], gs[:, :], GATE_EPS, None, ALU.max))
                own.after()
                own.did(dve.reciprocal(gr[:, :], gs[:, :]))
                own.after()
                dve.wait_ge(d_gt, LEAD + i)
                dve.tensor_tensor(gw[:, :, :], ge[:, :, :], bcast(gr[:, :]), ALU.mult).then_inc(d_gate, 1)
                dve.wait_ge(d_gt, LEAD + i + 1)
                dve.wait_ge(d_b2, LEAD + i)
                dve.tensor_copy(gT[:, :], bank(6)[0:E, :]).then_inc(d_gte, 1)
                dve.wait_ge(d_b2, LEAD + i + 1)
                dve.wait_ge(d_store, 16 * LEAD + 16 * i)
                dve.tensor_tensor(acc[:, :], grp(x_all, i), bank(6), ALU.add).then_inc(d_init, 1)
                dve.wait_ge(d_init, LEAD + i + 1)
                for e in range(E):
                    dve.wait_ge(d_l2, LEAD + E * i + e + 1)
                    for j in range(J):
                        ins = dve.scalar_tensor_tensor(blk(acc, j), blk(bank(4 + e % 2), j), gw[:, j, e:e + 1],
                                                       blk(acc, j), ALU.mult, ALU.add)
                    ins.then_inc(d_comb, 1)
                    dve.wait_ge(d_comb, LEAD + E * i + e + 1)
                    if e == 3 and not last:
                        norm_x(n + 1, grp(x_all, i + 1), False)
                    if e == 6 and not last:
                        split_x(n + 1)

            dve.wait_ge(x_done[C_PH], LEAD + B)
            GATES = 2 + 3 + 2 * J + 1 + 2 + 1 + 1 + 1 + 1 + 1
            run(d_step, GATES + NORM + 1, -NORM - 1)


_INS = ['x', 'ctx_1024', 'L0_xattn_Wq', 'L0_xattn_bq', 'L0_xattn_Wk', 'L0_xattn_bk', 'L0_xattn_Wv', 'L0_xattn_bv',
        'L0_xattn_Wo', 'L0_xattn_bo', 'L0_ffn_Win', 'L0_ffn_bin_', 'L0_ffn_W1', 'L0_ffn_b1', 'L0_ffn_W2',
        'L0_ffn_b2', 'L0_ffn_Wout', 'L0_ffn_bout', 'L1_xattn_ln_gamma', 'L1_xattn_ln_beta', 'L1_xattn_w_q',
        'L1_xattn_w_kv', 'L1_xattn_w_out', 'L1_xattn_b_out', 'L1_xattn_gate', 'L1_ffn_Wg', 'L1_ffn_bg',
        'L1_ffn_W1', 'L1_ffn_b1', 'L1_ffn_W2', 'L1_ffn_b2']


def kernel(**inputs):
    import numpy as np
    import concourse.bacc as bacc
    from concourse.bass_utils import run_bass_kernel_spmd

    nc = bacc.Bacc("TRN2", target_bir_lowering=False, num_devices=1)
    arrays, t = {}, {}
    for name in _INS:
        a = np.ascontiguousarray(inputs[name])
        arrays[f"in_{name}"] = a
        t[name] = nc.dram_tensor(f"in_{name}", a.shape, mybir.dt.from_np(a.dtype), kind="ExternalInput").ap()
    out = nc.dram_tensor("out_0", (B, P, P), F32, kind="ExternalOutput").ap()
    build(nc, t, out)
    r = run_bass_kernel_spmd(nc, [arrays], core_ids=[0])
    return r.results[0]["out_0"]
```

```python
from contextlib import ExitStack

import concourse.bass as bass
from concourse import mybir

F32 = mybir.dt.float32
F32R = mybir.dt.float32r
F16 = mybir.dt.float16
I32 = mybir.dt.int32
U32 = mybir.dt.uint32
ALU = mybir.AluOpType
ACT = mybir.ActivationFunctionType
AX_X = mybir.AxisListType.X

P = 128
B = 32
J = 4
G = B // J
N = J * P
TOPK = 32
BLANK = -3.0e38
M, INNER = 64, 16
HT = M * INNER // P
HEADS, DH = 16, 64
QUADS = HEADS // 4 * J
E, HID = 8, 512
HC = HID // P
LN_EPS = 1e-5
GATE_EPS = 1e-12
LEAD = 2
A_PH, B_PH, C_PH = range(3)
W2SCALE = 256
C_NORM, D_NORM = 2 * G, 3 * G


class Own:

    def __init__(self, eng, sem, gone_by):
        self.eng, self.sem, self.gone_by = eng, sem, gone_by
        self.base, self.n, self.i, self.per, self.first = 0, 0, 0, 0, 0

    def loop(self, i, first, per):
        self.base += self.n
        self.i, self.first, self.per, self.n = i, first, per, 0

    def end_loop(self, rounds):
        assert self.n == self.per, f"{self.n} marks in a round, {self.per} said"
        self.base += rounds * self.per
        self.i, self.per, self.first, self.n = 0, 0, 0, 0

    def did(self, ins):
        ins.then_inc(self.sem, 1)
        self.n += 1

    def after(self):
        self.eng.wait_ge(self.sem, self.i * self.per + (self.base - self.first * self.per + self.n))

    def after_apart(self):
        self.after()
        self.eng.sem_inc(self.gone_by, 1)


def build(nc, t, out):
    with ExitStack() as ctx:
        def sb(name, shape, dt=F32):
            return ctx.enter_context(nc.sbuf_tensor(name, shape, dt))

        def sem(name):
            return ctx.enter_context(nc.semaphore(name))

        x_all = sb("x_all", [P, G, N])
        ctxT_all = sb("ctxT_all", [P, G, N])
        ctx_raw = sb("ctx_raw", [P, N])
        ident = sb("ident", [P, P])
        xn1 = ctx_raw[:, :]
        xn = sb("xn", [P, N])
        x32 = sb("x32", [P, N])
        xhi = sb("xhi", [P, N], F32R)
        xlo = sb("xlo", [P, N], F32R)
        stats = sb("stats", [P, J, 6])
        mv = sb("mv", [P, J, 2])
        var = sb("var", [P, J])
        nwt = sb("nwt", [P, 5, J])

        hid = sb("hid", [P, 8, N])
        w0raw = sb("w0raw", [P, 4, P])
        w0T = sb("w0T", [P, 3, P])
        wvo = sb("wvo", [P, P])
        ctxA = hid[:, 0, :]
        qA = hid[:, 1, :]
        kA = hid[:, 2, :]
        vA = hid[:, 3, :]
        sA = hid[:, 4, :]
        work = hid[:, 5, :]
        top8 = sb("top8", [P, 4, J, 8])
        negA = sb("negA", [P, J])
        eA = hid[:, 6, :]
        sumA = sb("sumA", [P, J])
        rA = sb("rA", [P, J])
        ptA = hid[:, 7, :]

        boA = sb("boA", [P, P])
        boB = sb("boB", [P, P])
        boC = sb("boC", [P, P])
        bo_in = sb("bo_in", [P, 3, P])

        vrows = sb("vrows", [8, P])
        w1row = sb("w1row", [HT, P])
        b1row = sb("b1row", [HT, P])
        binrow = sb("binrow", [HT, P])
        w2row = sb("w2row", [HT, P])
        crow = sb("crow", [HT, P])
        moe_b1row = sb("moe_b1row", [E * HC, P])
        cols = sb("cols", [P, 64])
        VC, CC, W2C, B1C = 0, 8, 16, 24
        bcol = sb("bcol", [P, 2, P])

        win = sb("win", [P, M])
        w2o = sb("w2o", [P, HT, P])
        wout0 = sb("wout0", [M, P])
        wzhi = sb("wzhi", [P, HT * P], F32R)
        wzlo = sb("wzlo", [P, HT * P], F32R)

        gate = sb("gate", [P, 1])
        tgate = sb("tgate", [P, 1])
        mhi = sb("mhi", [P, HEADS * P], F32R)
        mlo = sb("mlo", [P, HEADS * P], F32R)
        vohi = sb("vohi", [P, HEADS * P], F32R)
        volo = sb("volo", [P, HEADS * P], F32R)
        chi = sb("chi", [P, N], F32R)
        clo = sb("clo", [P, N], F32R)
        c32 = sb("c32", [P, N])
        vp = sb("vp", [P, 2, HEADS * P])
        qp = sb("qp", [P, HEADS, N // 2])
        pr = hid[:, 0:4, :]
        pt = hid[:, 4:6, :]
        nmax = sb("nmax", [P, 4, 4])
        psums = sb("psums", [P, 4, 4])
        prec = sb("prec", [P, 4, 4])

        w1hi = sb("w1hi", [P, E * HID], F32R)
        w1lo = sb("w1lo", [P, E * HID], F32R)
        w2hi = sb("w2hi", [P, E * HC, P], F16)
        w2lo = sb("w2lo", [P, E * HC, P], F16)
        h16 = vp[:, :, :].rearrange("p j n -> p (j n)").bitcast(F16).rearrange("p (a k n) -> p a k n", a=2, n=N)
        hhi, hlo = h16[:, 0, :, :], h16[:, 1, :, :]
        wg = sb("wg", [P, E])
        bg = sb("bg", [P, E])
        b2e = sb("b2e", [E, P])
        iota = sb("iota", [P, E])
        iota_i = sb("iota_i", [P, E], I32)
        lg = sb("lg", [P, J, E])
        lmax = sb("lmax", [P, J])
        ge = sb("ge", [P, J, E])
        gs = sb("gs", [P, J])
        gr = sb("gr", [P, J])
        g8 = sb("g8", [P, J, 8])
        gi = sb("gi", [P, J, 8], U32)
        gif = sb("gif", [P, J, 8])
        gm = sb("gm", [P, 2, J, E])
        gnext = sb("gnext", [P, J, E])
        gw = sb("gw", [P, J, E])
        gT = ctx_raw[0:E, :]
        acc = c32

        zb = vp[:, :, :].rearrange("p j n -> p (j n)").rearrange("p (k n) -> p k n", n=N)
        w1_raw = c32
        w2_raw = sb("w2_raw", [P, HC, P])

        vflat = vp[:, :, :].rearrange("p j n -> p (j n)")
        wq_raw = vflat[:, 0:1024]
        wkv_raw = vflat[:, 1024:3072]
        wo_raw = vflat[:, 3072:4096].rearrange("p (a n) -> p a n", n=P)
        qflat = qp[:, :, :].rearrange("p h n -> p (h n)")
        wT = [qflat[:, 1024 * k:1024 * (k + 1)].rearrange("p (a n) -> p a n", n=P) for k in range(3)]
        w1b = qflat[:, 3072:4096]
        wz32 = w2hi[:, :, :].rearrange("p a n -> p (a n)").bitcast(F32)[:, 0:1024]
        woutrep = w2lo[:, :, :].rearrange("p a n -> p (a n)").bitcast(F32)[:, 0:1024].rearrange("p (k n) -> p k n", n=P)

        ps = ctx.enter_context(nc.psum_tensor("ps", [P, 8, N], F32))

        ld_w0 = sem("ld_w0")
        ld_rows = sem("ld_rows")
        ld_w = sem("ld_w")
        ld_e = sem("ld_e")
        e_split = sem("e_split")
        ctx_kept = sem("ctx_kept")
        xb_ok = sem("xb_ok")
        ld_x = sem("ld_x")
        ld_ctx = sem("ld_ctx")
        ident_ok = sem("ident_ok")
        pool_own = sem("pool_own")
        pool_own2 = sem("pool_own2")
        dve_own = sem("dve_own")
        act_own = sem("act_own")
        gone_by = sem("gone_by")
        set_pe = sem("set_pe")
        set_act = sem("set_act")
        set_dve = sem("set_dve")
        xn_ok = sem("xn_ok")
        xn_turned = sem("xn_turned")
        x32_ok = sem("x32_ok")
        xsplit_ok = sem("xsplit_ok")
        ctx_turned = sem("ctx_turned")
        ctxA_ok = sem("ctxA_ok")
        x_done = [sem(f"x_done{p}") for p in range(3)]
        a_q, a_k, a_v, a_s, a_t, a_o = map(sem, ("a_q", "a_k", "a_v", "a_s", "a_t", "a_o"))
        a_qe, a_ke, a_ve, a_se, a_te = map(sem, ("a_qe", "a_ke", "a_ve", "a_se", "a_te"))
        a_first = sem("a_first")
        a_exp = sem("a_exp")
        a_p = sem("a_p")
        b_z, b_r, b_o = map(sem, ("b_z", "b_r", "b_o"))
        c_fed, c_qe, c_ve, c_s, c_max = map(sem, ("c_fed", "c_qe", "c_ve", "c_s", "c_max"))
        c_exp, c_norm, c_t, c_te, c_pv = map(sem, ("c_exp", "c_norm", "c_t", "c_te", "c_pv"))
        c_csplit, c_c32 = sem("c_csplit"), sem("c_c32")
        d_lg, d_lgs, d_ex, d_gate, d_gt, d_gte, d_b2, d_init = map(
            sem, ("d_lg", "d_lgs", "d_ex", "d_gate", "d_gt", "d_gte", "d_b2", "d_init"))
        d_hi = sem("d_hi")
        d_h = sem("d_h")
        d_l1, d_g, d_l2, d_comb, d_store = map(sem, ("d_l1", "d_g", "d_l2", "d_comb", "d_store"))

        SIGNALS = {
            "pe": (xn_turned, ctx_turned, a_q, a_k, a_v, a_s, a_t, a_o, b_z, b_o, c_fed, c_s, c_t, c_pv,
                   d_lg, d_gt, d_b2, d_l1, d_l2),
            "act": (x32_ok, ctxA_ok, a_qe, a_ke, a_ve, a_se, a_te, a_exp, b_r, c_qe, c_exp, c_te, d_ex, d_g, d_gte,
                    d_hi),
            "dve": (xn_ok, xsplit_ok, a_first, a_p, c_ve, c_max, c_norm, c_csplit, d_lgs, d_gate,
                    d_init, d_comb, d_h, *x_done),
            "pool": (c_c32, e_split, ctx_kept, xb_ok),
        }

        def start(eng, who):
            for s in SIGNALS[who]:
                eng.sem_inc(s, LEAD)

        NW0, NROWS, NLW = 4, 23, 3

        def grp(a, i):
            return a[:, bass.ds(i, 1), :].rearrange("p a n -> p (a n)")

        def blk(a, j):
            return a[:, P * j:P * (j + 1)]

        def bank(b):
            return ps[:, b, :]

        def groups(eng, step):
            with eng.Fori(0, G - 1) as i:
                step(i, False)
            step(G - 1, True)

        FEEDS = []
        for s in range(QUADS):
            if s // 4 % 2 == 0:
                FEEDS += [("q", s, 0), ("q", s, 1)]
            FEEDS += [("v", s, 0)]
        NF = len(FEEDS)

        def q_before(f):
            return sum(kind == "q" for kind, _, _ in FEEDS[:f])

        SETUP_BANKS = (0, 1, 6)

        def four_heads(w, s):
            return w[:, :].rearrange("p (g a o n) -> p g a o n", g=2, a=4, o=2)[:, s % 4 // 2, :, s % 2, :]

        TURN = 7

        block = ctx.enter_context(nc.Block())

        @block.sync
        def _(sp):
            sp.sem_inc(d_store, 16 * LEAD)
            x_v = t["x"].rearrange("(g j) t d -> t g j d", j=J)
            c_v = t["ctx_1024"].rearrange("(g j) t d -> t g j d", j=J)

            def load(i):
                sp.dma_start(grp(x_all, i).rearrange("p (j d) -> p j d", j=J),
                             x_v[:, bass.ds(i, 1), :, :].rearrange("t a j d -> t (a j) d")).then_inc(ld_x, 16)
                if not isinstance(i, int):
                    sp.wait_ge(ctx_turned, LEAD + i)
                    sp.sem_inc(gone_by, 1)
                sp.dma_start(ctx_raw[:, :].rearrange("p (j d) -> p j d", j=J),
                             c_v[:, bass.ds(i, 1), :, :].rearrange("t a j d -> t (a j) d")).then_inc(ld_ctx, 16)

            def load_expert(e):
                sp.wait_ge(e_split, LEAD + e)
                sp.sem_inc(gone_by, 1)
                sp.dma_start(w1_raw[:, :].unsqueeze(1),
                             t["L1_ffn_W1"].rearrange("e p h -> p e h")[:, bass.ds(e, 1), :]).then_inc(ld_e, 16)
                sp.dma_start(w2_raw[:, :, :],
                             t["L1_ffn_W2"].rearrange("e (c p) n -> p e c n", p=P)[:, bass.ds(e, 1), :, :]
                             .rearrange("p a c n -> p (a c) n")).then_inc(ld_e, 16)
                sp.wait_ge(ld_e, 32 * e + 32)
                sp.sem_inc(gone_by, 1)

            load(0)
            for k, name in enumerate(("L0_xattn_Wq", "L0_xattn_Wk", "L0_xattn_Wv", "L0_xattn_Wo")):
                sp.dma_start(w0raw[:, k, :], t[name]).then_inc(ld_w0, 16)

            def row(a):
                return a.rearrange("(a n) -> a n", a=1)

            n = 0
            for r, name in enumerate(("L0_xattn_bq", "L0_xattn_bk", "L1_xattn_ln_gamma", "L1_xattn_ln_beta",
                                      "L0_xattn_bv")):
                sp.dma_start(vrows[r:r + 1, :], row(t[name])).then_inc(ld_rows, 16)
                n += 1
            sp.dma_start(vrows[5:6, 0:M], row(t["L0_ffn_b2"])).then_inc(ld_rows, 16)
            sp.dma_start(vrows[5:6, M:P], row(t["L0_ffn_b2"])).then_inc(ld_rows, 16)
            for r in (6, 7):
                sp.dma_start(vrows[r:r + 1, :], row(t["L0_xattn_bq"])).then_inc(ld_rows, 16)
            n += 4
            flat = "(k q) h -> k (q h)"
            sp.dma_start(w1row[:, :], t["L0_ffn_W1"].rearrange(flat, k=HT)).then_inc(ld_rows, 16)
            sp.dma_start(b1row[:, :], t["L0_ffn_b1"].rearrange(flat, k=HT)).then_inc(ld_rows, 16)
            sp.dma_start(w2row[:, :], t["L0_ffn_W2"].rearrange(flat, k=HT)).then_inc(ld_rows, 16)
            sp.dma_start(binrow[:, 0:M // HT], t["L0_ffn_bin_"].rearrange("(k q) -> k q", k=HT)).then_inc(ld_rows, 16)
            sp.dma_start(moe_b1row[:, :], t["L1_ffn_b1"].rearrange("e (c p) -> (e c) p", p=P)).then_inc(ld_rows, 16)
            for r, name in enumerate(("L0_xattn_bo", "L0_ffn_bout", "L1_xattn_b_out")):
                sp.dma_start(bo_in[:, r, :], row(t[name]).to_broadcast([P, P])).then_inc(ld_rows, 16)
            sp.dma_start(gate[:, :], row(t["L1_xattn_gate"]).to_broadcast([P, 1])).then_inc(ld_rows, 16)
            sp.dma_start(bg[:, :], row(t["L1_ffn_bg"]).to_broadcast([P, E])).then_inc(ld_rows, 16)
            sp.dma_start(wg[:, :], t["L1_ffn_Wg"]).then_inc(ld_rows, 16)
            sp.dma_start(b2e[:, :], t["L1_ffn_b2"]).then_inc(ld_rows, 16)
            sp.dma_start(win[:, :], t["L0_ffn_Win"]).then_inc(ld_rows, 16)
            sp.dma_start(wout0[:, :], t["L0_ffn_Wout"]).then_inc(ld_rows, 16)
            sp.dma_start(w1b, row(t["L0_ffn_W1"].rearrange("m h -> (m h)")).to_broadcast([P, M * INNER])).then_inc(ld_rows, 16)
            n += 15
            assert n + 0 == NROWS + 1, n
            wo4 = t["L0_ffn_Wout"].rearrange("(k q) n -> q k n", k=HT)
            for q in range(P // INNER):
                sp.dma_start(woutrep[INNER * q:INNER * (q + 1), :, :],
                             wo4[q:q + 1, :, :].to_broadcast([INNER, HT, P])).then_inc(ld_w, 16)
            sp.dma_start(wq_raw, t["L1_xattn_w_q"]).then_inc(ld_w, 16)
            sp.dma_start(wkv_raw, t["L1_xattn_w_kv"]).then_inc(ld_w, 16)
            sp.dma_start(wo_raw, t["L1_xattn_w_out"].rearrange("(a p) n -> p a n", p=P)).then_inc(ld_w, 16)
            with sp.Fori(1, G) as i:
                sp.wait_ge(ld_x, 16 * i)
                sp.wait_ge(ld_ctx, 16 * i)
                sp.sem_inc(gone_by, 1)
                load(i)
                load_expert(i - 1)
            load_expert(G - 1)
            out_v = out.rearrange("(g j) t d -> t g j d", j=J)
            with sp.Fori(0, G) as i:
                sp.wait_ge(d_comb, LEAD + E * i + E)
                sp.sem_inc(gone_by, 1)
                sp.dma_start(out_v[:, bass.ds(i, 1), :, :].rearrange("t a j d -> t (a j) d"),
                             acc[:, :].rearrange("p (j d) -> p j d", j=J)).then_inc(d_store, 16)
            sp.wait_ge(d_store, 16 * LEAD + 16 * G)

        NROWS += 1
        NLW += P // INNER

        @block.gpsimd
        def _(pool):
            start(pool, "pool")
            pool.memset(ident[:, :], 0.0).then_inc(pool_own, 1)
            pool.iota(iota_i[:, :], pattern=[[1, E]], base=0, channel_multiplier=0).then_inc(pool_own, 1)
            pool.wait_ge(pool_own, 2)
            pool.affine_select(out=ident[:, :], in_=ident[:, :], compare_op=ALU.not_equal, fill=1.0, base=0,
                               pattern=[[-1, P]], channel_multiplier=1).then_inc(ident_ok, 1)
            pool.tensor_copy(iota[:, :], iota_i[:, :]).then_inc(ident_ok, 1)

            def add_bias(i, count, bias):
                pool.wait_ge(xn_ok, LEAD + count)
                x = grp(x_all, i).rearrange("p (j d) -> p j d", j=J)
                pool.tensor_tensor(x, x, bias[:, :].unsqueeze(1).to_broadcast([P, J, P]), ALU.add).then_inc(xb_ok, 1)

            def keep_ctx(i):
                pool.wait_ge(ctxA_ok, LEAD + i + 1)
                pool.tensor_copy(grp(ctxT_all, i), ctxA).then_inc(ctx_kept, 1)

            def split_expert(e):
                pool.wait_ge(ld_e, 32 * e + 32)
                w = w1hi[:, :].rearrange("p (e h) -> p e h", e=E)[:, bass.ds(e, 1), :]
                l = w1lo[:, :].rearrange("p (e h) -> p e h", e=E)[:, bass.ds(e, 1), :]
                w2 = w2hi[:, :, :].rearrange("p (e c) n -> p e (c n)", e=E)[:, bass.ds(e, 1), :]
                l2 = w2lo[:, :, :].rearrange("p (e c) n -> p e (c n)", e=E)[:, bass.ds(e, 1), :]
                raw, raw2 = w1_raw[:, :].unsqueeze(1), w2_raw[:, :, :].rearrange("p c n -> p (c n)").unsqueeze(1)
                pool.tensor_copy(w, raw).then_inc(pool_own, 1)
                pool.tensor_scalar(raw2, raw2, float(W2SCALE), None, ALU.mult).then_inc(pool_own, 1)
                pool.wait_ge(pool_own, 3 * e + 4)
                pool.tensor_copy(w2, raw2).then_inc(pool_own, 1)
                pool.tensor_tensor(l, raw, w.bitcast(F32), ALU.subtract).then_inc(pool_own2, 1)
                pool.wait_ge(pool_own, 3 * e + 5)
                pool.tensor_tensor(l2, raw2, w2, ALU.subtract).then_inc(e_split, 1)

            def a_step(g):
                keep_ctx(g + 1)
                add_bias(g + 1, 2 * g + 2, boA)
                if isinstance(g, int):
                    pool.wait_ge(set_dve, 12)
                add_bias(g, 2 * g + 3, boB)

            keep_ctx(0)
            add_bias(0, 1, boA)
            a_step(0)
            with pool.Fori(0, G - 2) as i:
                a_step(i + 1)
                split_expert(i)
            add_bias(G - 1, 2 * G, boB)
            split_expert(G - 2)
            split_expert(G - 1)
            pool.wait_ge(ctx_kept, LEAD + G)
            pool.wait_ge(pool_own2, E)
            for j in range(J):
                pool.tensor_copy(blk(c32, j), ctxT_all[:, 0, P * j:P * (j + 1)]).then_inc(c_c32, 1)
            with pool.Fori(0, G - 1) as i:
                add_bias(i, C_NORM + 1 + i, boC)
                for j in range(J):
                    pool.wait_ge(c_s, LEAD + QUADS * i + 4 * j + 4)
                    pool.tensor_copy(blk(c32, j), blk(grp(ctxT_all, i + 1), j)).then_inc(c_c32, 1)
            add_bias(G - 1, C_NORM + G, boC)

        @block.tensor
        def _(pe):
            start(pe, "pe")

            def turn(dst, src, n=P, mark=None):
                ins = pe.transpose(dst, src, ident[0:n, 0:n])
                if mark is not None:
                    ins.then_inc(mark, 1)

            def split_mm(dst, wh, wl, ah, al, mark=None):
                pe.matmul(dst, wh, ah, start=True, stop=False)
                pe.matmul(dst, wh, al, start=False, stop=False)
                ins = pe.matmul(dst, wl, ah, start=False, stop=True)
                if mark is not None:
                    ins.then_inc(mark, 1)

            def turn_x(n, *free):
                pe.wait_ge(xn_ok, LEAD + n + 1)
                pe.wait_ge(x32_ok, LEAD + n)
                for s, v in free:
                    pe.wait_ge(s, LEAD + v)
                for j in range(J):
                    turn(blk(bank(TURN), j), blk(xn, j), mark=xn_turned if j == J - 1 else None)

            def turn_ctx(i, x_count):
                pe.wait_ge(ld_ctx, 16 * i + 16)
                pe.wait_ge(x32_ok, LEAD + x_count)
                for j in range(J):
                    turn(blk(bank(TURN), j), blk(ctx_raw, j), mark=ctx_turned if j == J - 1 else None)

            pe.wait_ge(ident_ok, 2)
            pe.wait_ge(ld_w0, 16 * NW0)
            for k, w in enumerate((0, 1, 3)):
                turn(blk(bank(0), k), w0raw[:, w, :], mark=set_pe if k == 2 else None)
            pe.wait_ge(set_dve, 1)
            pe.wait_ge(ld_rows, 16 * NROWS)
            cb = bank(1)
            turn(cb[:, VC:VC + 8], vrows[:, :], 8)
            turn(cb[:, CC:CC + 8], crow[:, :], 8)
            turn(cb[:, W2C:W2C + 8], w2row[:, :], 8)
            turn(cb[:, B1C:B1C + 32], moe_b1row[:, :], 32, mark=set_pe)
            pe.wait_ge(set_act, 2)
            pe.wait_ge(set_dve, 2)
            pe.matmul(blk(bank(2), 0), w0raw[:, 2, :], w0T[:, 2, :], start=True, stop=True)
            pe.matmul(blk(bank(2), 1), bcol[:, 0, :], w0T[:, 2, :], start=True, stop=True)
            pe.matmul(blk(bank(2), 2), bcol[0:M, 1, :], wout0[:, :], start=True, stop=True).then_inc(set_pe, 1)
            def a_front(g, x_count):
                pe.wait_ge(x32_ok, LEAD + x_count)
                pe.wait_ge(a_ke, LEAD + g)
                pe.matmul(bank(3), w0T[:, 0, :], x32[:, :], start=True, stop=True).then_inc(a_q, 1)
                pe.wait_ge(ctxA_ok, LEAD + g + 1)
                pe.wait_ge(a_ve, LEAD + g)
                for j in range(J):
                    ins = pe.matmul(blk(bank(4), j), blk(ctxA, j), wvo[:, :], start=True, stop=True)
                ins.then_inc(a_v, 1)
                pe.wait_ge(a_qe, LEAD + g + 1)
                pe.matmul(bank(3), w0T[:, 1, :], ctxA, start=True, stop=True).then_inc(a_k, 1)
                pe.wait_ge(a_ke, LEAD + g + 1)
                pe.wait_ge(a_se, LEAD + g)
                for j in range(J):
                    ins = pe.matmul(blk(bank(5), j), blk(qA, j), blk(kA, j), start=True, stop=True)
                ins.then_inc(a_s, 1)

            def a_back(g):
                pe.wait_ge(a_p, LEAD + J * g + J)
                pe.wait_ge(x_done[A_PH], LEAD + J * g)
                for j in range(J):
                    turn(blk(bank(6), j), blk(eA, j), mark=a_t if j == J - 1 else None)
                pe.wait_ge(a_te, LEAD + g + 1)
                pe.wait_ge(a_ve, LEAD + g + 1)
                for j in range(J):
                    ins = pe.matmul(blk(bank(6), j), blk(ptA, j), blk(vA, j), start=True, stop=True)
                ins.then_inc(a_o, 1)

            def b_hidden(i):
                pe.wait_ge(xsplit_ok, LEAD + i + 1)
                for k in range(HT):
                    pe.wait_ge(b_r, LEAD + HT * i + max(k - 1, 0))
                    w = slice(P * k, P * (k + 1))
                    split_mm(bank(k % 2), wzhi[:, w], wzlo[:, w], xhi[:, :], xlo[:, :], mark=b_z)

            def b_out(i, js):
                if js[0] == 0:
                    pe.wait_ge(b_r, LEAD + HT * i + HT)
                    pe.wait_ge(x_done[B_PH], LEAD + i)
                for j in js:
                    for k in range(HT):
                        ins = pe.matmul(blk(bank(2), j), blk(zb[:, k, :], j), w2o[:, k, :],
                                        start=(k == 0), stop=(k == HT - 1))
                if js[-1] == J - 1:
                    ins.then_inc(b_o, 1)

            def ahead(g, more):
                if more:
                    turn_x(2 * g + 1)
                    turn_ctx(g + 1, 2 * g + 2)
                    a_front(g + 1, 2 * g + 2)
                    turn_x(2 * g + 2, (ctxA_ok, g + 2))
                else:
                    turn_x(2 * g + 1)

            def ab_step(i, more=True):
                b_hidden(i)
                b_out(i, (0, 1))
                a_back(i + 1)
                b_out(i, (2, 3))
                ahead(i + 1, more)

            pe.wait_ge(set_act, 3)
            turn_x(0)
            turn_ctx(0, 1)
            a_front(0, 1)
            pe.wait_ge(ld_w, 16 * NLW)
            for k in range(3):
                for half in range(2):
                    s = 2 * k + half
                    b = SETUP_BANKS[s % 3]
                    if s >= 3:
                        pe.wait_ge(set_act, s + 1)
                    for a in range(4):
                        src = (wq_raw if k == 0 else wkv_raw[:, 1024 * (k - 1):1024 * k])
                        turn(blk(bank(b), a), blk(src, 4 * half + a), mark=set_pe if a == 3 else None)
            for s in range(8):
                b = SETUP_BANKS[s % 3]
                pe.wait_ge(set_act, min(9, 7 + s))
                if s >= 3:
                    pe.wait_ge(set_dve, 5 + s - 3)
                for a in range(4):
                    h = 8 * (s % 4 // 2) + 2 * a + s % 2
                    r = DH * (h % 2)
                    left, right = (wT[0], wT[1]) if s < 4 else (wT[2], wo_raw)
                    ins = pe.matmul(blk(bank(b), a), left[r:r + DH, h // 2, :], right[r:r + DH, h // 2, :],
                                    start=True, stop=True)
                ins.then_inc(set_pe, 1)
            a_back(0)
            ahead(0, True)
            with pe.Fori(0, G - 2) as i:
                ab_step(i)
            ab_step(G - 2, False)
            b_hidden(G - 1)
            b_out(G - 1, (0, 1, 2, 3))
            turn_x(C_NORM)

            def c_step(i, first=False, last=False, tail=False):
                def feed_bank(f):
                    if f < 2:
                        pe.wait_ge(c_ve, LEAD + QUADS * i)
                        pe.wait_ge(c_qe, LEAD + 16 * i)
                    else:
                        kind, s, a = FEEDS[f - 2]
                        if kind == "q":
                            pe.wait_ge(c_qe, LEAD + 16 * i + q_before(f - 2) + 1)
                        else:
                            pe.wait_ge(c_ve, LEAD + QUADS * i + s + 1)
                    return bank(4 + f % 2)

                def feed_q(f):
                    b = feed_bank(f)
                    _, s, a = FEEDS[f]
                    c = slice(0, N // 2) if s < 8 else slice(N // 2, N)
                    for k in range(2):
                        h = 4 * (s % 4) + 2 * a + k
                        w = slice(P * h, P * (h + 1))
                        split_mm(b[:, N // 2 * k:N // 2 * (k + 1)], mhi[:, w], mlo[:, w], xhi[:, c], xlo[:, c],
                                 mark=c_fed if k else None)

                def feed_v(f):
                    b = feed_bank(f)
                    _, s, _ = FEEDS[f]
                    j, q = s // 4, s % 4
                    if q == 0:
                        pe.wait_ge(c_csplit, LEAD + J * i + j + 1)
                    w = slice(N * q, N * (q + 1))
                    split_mm(b, blk(chi, j), blk(clo, j), vohi[:, w], volo[:, w], mark=c_fed)

                def scores(s):
                    j, q = s // 4, s % 4
                    if q == 0:
                        pe.wait_ge(c_c32, LEAD + J * i + j + 1)
                    if j % 2 == 0:
                        pe.wait_ge(c_qe, LEAD + 16 * i + 8 * (j // 2) + 2 * q + 2)
                    pe.wait_ge(c_exp, LEAD + QUADS * i + (max(s - 1, 0) if first else s - 1))
                    for a in range(4):
                        ins = pe.matmul(blk(bank(s % 2), a), blk(qp[:, 4 * q + a, :], j % 2), blk(c32, j),
                                        start=True, stop=True)
                    ins.then_inc(c_s, 1)

                def turn_p(u):
                    pe.wait_ge(c_norm, LEAD + QUADS * i + u + 1)
                    pe.wait_ge(c_te, LEAD + QUADS * i + (max(u - 1, 0) if first else u - 1))
                    for a in range(4):
                        turn(blk(bank(2 + u % 2), a), blk(pr[:, u % 4, :], a), mark=c_t if a == 3 else None)

                def attend(u):
                    j, q = u // 4, u % 4
                    pe.wait_ge(c_te, LEAD + QUADS * i + u + 1)
                    pe.wait_ge(c_ve, LEAD + QUADS * i + u + 1)
                    if q == 0:
                        pe.wait_ge(x_done[C_PH], LEAD + J * i + j)
                    for a in range(4):
                        h = 4 * q + a
                        ins = pe.matmul(bank(6)[:, 0:P], blk(pt[:, u % 2, :], a), blk(vp[:, j % 2, :], h),
                                        start=(h == 0), stop=(h == HEADS - 1))
                    ins.then_inc(c_pv, 1)

                if not tail:
                    pe.wait_ge(xsplit_ok, LEAD + G + i + 1)
                for s in range(QUADS, QUADS + 4) if tail else range(QUADS):
                    if s < QUADS:
                        for f, (kind, fs, _) in enumerate(FEEDS):
                            if fs == s:
                                (feed_q if kind == "q" else feed_v)(f)
                        scores(s)
                    if s - 3 < QUADS and (s >= 3 or not first):
                        turn_p(s - 3)
                    if s >= 4 or not first:
                        attend(s - 4)
                    if s == 10:
                        turn_x(C_NORM + 1 + i)

            pe.wait_ge(x_done[B_PH], LEAD + G)
            c_step(0, first=True)
            with pe.Fori(1, G - 1) as i:
                c_step(i)
            c_step(G - 1, last=True)
            c_step(G - 1, tail=True)

            def logits(n):
                pe.wait_ge(x32_ok, LEAD + D_NORM + n + 1)
                for j in range(J):
                    ins = pe.matmul(bank(6)[:, E * j:E * (j + 1)], blk(x32, j), wg[:, :], start=True, stop=True)
                ins.then_inc(d_lg, 1)

            def d_step(i, first=False, last=False):
                def layer1(e):
                    for c in range(HC):
                        if e == 0:
                            pe.wait_ge(d_g, LEAD + E * HC * i)
                        else:
                            pe.wait_ge(d_g, LEAD + E * HC * i + HC * (e - 1) + c + 1)
                        w = slice(HID * e + P * c, HID * e + P * (c + 1))
                        split_mm(bank(c), w1hi[:, w], w1lo[:, w], xhi[:, :], xlo[:, :], mark=d_l1)

                def layer2(e):
                    pe.wait_ge(d_h, LEAD + E * i + e + 1)
                    pe.wait_ge(d_comb, LEAD + E * i + e - 1)
                    for j in range(J):
                        for c in range(HC):
                            k, w = HC * (e % 2) + c, HC * (e % E) + c
                            dst = blk(bank(4 + e % 2), j)
                            pe.matmul(dst, blk(hhi[:, k, :], j), w2hi[:, w, :], start=(c == 0), stop=False)
                            pe.matmul(dst, blk(hhi[:, k, :], j), w2lo[:, w, :], start=False, stop=False)
                            ins = pe.matmul(dst, blk(hlo[:, k, :], j), w2hi[:, w, :], start=False, stop=(c == HC - 1))
                    ins.then_inc(d_l2, 1)

                pe.wait_ge(xsplit_ok, LEAD + 2 * G + i + 1)
                for s in range(E + 1):
                    if s < E:
                        layer1(s)
                    if s == 0 and not first:
                        layer2(-1)
                    if s == 1:
                        pe.wait_ge(d_gate, LEAD + i + 1)
                        for j in range(J):
                            ins = pe.transpose(bank(6)[0:E, P * j:P * (j + 1)], gw[:, j, :], ident[:, :])
                        ins.then_inc(d_gt, 1)
                    if s == 4 and not last:
                        turn_x(D_NORM + 1 + i)
                    if s >= 2:
                        layer2(s - 2)
                    if s == 2:
                        pe.wait_ge(d_gte, LEAD + i + 1)
                        for j in range(J):
                            ins = pe.matmul(blk(bank(6), j), gT[:, P * j:P * (j + 1)], b2e[:, :], start=True, stop=True)
                        ins.then_inc(d_b2, 1)
                    if s == 5 and not last:
                        pe.wait_ge(d_init, LEAD + i + 1)
                        logits(i + 1)
                if last:
                    layer2(E - 1)

            pe.wait_ge(x_done[C_PH], LEAD + B)
            pe.wait_ge(c_te, LEAD + QUADS * G)
            logits(0)
            d_step(0, first=True)
            with pe.Fori(1, G - 1) as i:
                d_step(i)
            d_step(G - 1, last=True)

        @block.scalar
        def _(act):
            start(act, "act")

            def empty_turn(n, aff, *freed):
                act.wait_ge(xn_turned, LEAD + n + 1)
                for s, v in freed:
                    act.wait_ge(s, LEAD + v)
                if aff:
                    act.activation(x32[:, :], bank(TURN), ACT.Identity, scale=cols[:, VC + 2:VC + 3],
                                   bias=cols[:, VC + 3:VC + 4]).then_inc(x32_ok, 1)
                else:
                    act.activation(x32[:, :], bank(TURN), ACT.Copy).then_inc(x32_ok, 1)

            def empty_ctx(g):
                act.wait_ge(ctx_turned, LEAD + g + 1)
                act.wait_ge(a_v, LEAD + g)
                act.wait_ge(a_k, LEAD + g)
                act.wait_ge(ctx_kept, LEAD + g)
                act.activation(ctxA, bank(TURN), ACT.Copy).then_inc(ctxA_ok, 1)

            act.wait_ge(set_pe, 1)
            act.activation(w0T[:, :, :].rearrange("p a n -> p (a n)"), bank(0)[:, 0:3 * P], ACT.Copy).then_inc(set_act, 1)
            act.wait_ge(set_pe, 2)
            act.activation(cols[:, 0:B1C + 32], bank(1)[:, 0:B1C + 32], ACT.Copy).then_inc(set_act, 1)
            act.wait_ge(ld_rows, 16 * NROWS)
            act.activation(tgate[:, :], gate[:, :], ACT.Tanh).then_inc(act_own, 1)
            act.wait_ge(set_pe, 3)
            act.activation(wvo[:, :], blk(bank(2), 0), ACT.Copy).then_inc(set_act, 1)

            def a_front(g):
                act.wait_ge(a_q, LEAD + g + 1)
                act.wait_ge(a_s, LEAD + g)
                act.activation(qA, bank(3), ACT.Identity, bias=cols[:, VC:VC + 1]).then_inc(a_qe, 1)
                act.wait_ge(a_k, LEAD + g + 1)
                act.activation(kA, bank(3), ACT.Identity, bias=cols[:, VC + 1:VC + 2]).then_inc(a_ke, 1)
                act.wait_ge(a_s, LEAD + g + 1)
                act.wait_ge(a_exp, LEAD + g)
                act.activation(sA, bank(5), ACT.Copy, scale=P ** -0.5).then_inc(a_se, 1)
                act.wait_ge(a_v, LEAD + g + 1)
                act.wait_ge(a_o, LEAD + g)
                act.activation(vA, bank(4), ACT.Copy).then_inc(a_ve, 1)

            def a_exps(g):
                act.wait_ge(a_first, LEAD + g + 1)
                act.wait_ge(a_se, LEAD + g + 1)
                act.wait_ge(a_t, LEAD + g)
                for j in range(J):
                    ins = act.activation(blk(eA, j), blk(sA, j), ACT.Exp, bias=negA[:, j:j + 1])
                ins.then_inc(a_exp, 1)

            def a_turned(g):
                act.wait_ge(a_t, LEAD + g + 1)
                act.wait_ge(a_o, LEAD + g)
                act.activation(ptA, bank(6), ACT.Copy).then_inc(a_te, 1)

            def b_hidden(i, ks):
                act.wait_ge(b_o, LEAD + i)
                for k in ks:
                    act.wait_ge(b_z, LEAD + HT * i + k + 1)
                    act.activation(zb[:, k, :], bank(k % 2), ACT.Relu, bias=cols[:, CC + k:CC + k + 1]).then_inc(b_r, 1)

            def ahead(g, more, *freed):
                if more:
                    empty_turn(2 * g + 1, False, (xsplit_ok, g))
                    empty_ctx(g + 1)
                    a_front(g + 1)
                    empty_turn(2 * g + 2, False, (a_q, g + 2), *freed)
                else:
                    empty_turn(2 * g + 1, False, (xsplit_ok, g), *freed)

            def ab_step(i, more=True):
                b_hidden(i, range(0, 4))
                a_exps(i + 1)
                b_hidden(i, range(4, HT))
                a_turned(i + 1)
                ahead(i + 1, more, (b_z, HT * i + HT))

            empty_turn(0, False)
            empty_ctx(0)
            a_front(0)
            for s in range(6):
                act.wait_ge(set_pe, 4 + s)
                act.activation(wT[s // 2][:, 4 * (s % 2):4 * (s % 2) + 4, :].rearrange("p a n -> p (a n)"),
                               bank(SETUP_BANKS[s % 3]), ACT.Copy).then_inc(set_act, 1)
            act.wait_ge(act_own, 1)
            for s in range(8):
                act.wait_ge(set_pe, 10 + s)
                src = bank(SETUP_BANKS[s % 3]).rearrange("p (a n) -> p a n", n=P)
                if s < 4:
                    act.activation(four_heads(mhi, s), src, ACT.Copy, scale=-1.0 / 8).then_inc(act_own, 1)
                else:
                    act.activation(four_heads(vohi, s), src, ACT.Copy, scale=tgate[:, 0:1]).then_inc(act_own, 1)
            a_exps(0)
            a_turned(0)
            ahead(0, True)
            with act.Fori(0, G - 2) as i:
                ab_step(i)
            ab_step(G - 2, False)
            b_hidden(G - 1, range(HT))
            empty_turn(C_NORM, True, (b_z, HT * G), (xsplit_ok, G))

            def c_step(i, first=False, last=False, tail=False):
                for s in range(QUADS, QUADS + 3) if tail else range(QUADS):
                    for f, (kind, fs, a) in enumerate(FEEDS):
                        if fs == s and kind == "q":
                            h = 4 * (s % 4) + 2 * a
                            act.wait_ge(c_fed, LEAD + NF * i + f + 1)
                            act.activation(qp[:, h:h + 2, :].rearrange("p h n -> p (h n)"), bank(4 + f % 2),
                                           ACT.Copy).then_inc(c_qe, 1)
                    u = s - 1
                    if u < QUADS and (u >= 0 or not first):
                        act.wait_ge(c_max, LEAD + QUADS * i + u + 1)
                        if u >= 4 or not first:
                            act.wait_ge(c_t, LEAD + QUADS * i + u - 3)
                        for a in range(4):
                            ins = act.activation(blk(pr[:, u % 4, :], a), blk(bank(u % 2), a), ACT.Exp, scale=-1.0,
                                                 bias=nmax[:, u % 4, a:a + 1], accum_out=psums[:, u % 4, a:a + 1])
                        ins.then_inc(c_exp, 1)
                    u = s - 3
                    if u < QUADS and (u >= 0 or not first):
                        act.wait_ge(c_t, LEAD + QUADS * i + u + 1)
                        if u >= 2 or not first:
                            act.wait_ge(c_pv, LEAD + QUADS * i + u - 1)
                        act.activation(pt[:, u % 2, :], bank(2 + u % 2), ACT.Copy).then_inc(c_te, 1)
                    if s == 12:
                        empty_turn(C_NORM + 1 + i, not last, (c_fed, NF * i + 27))

            c_step(0, first=True)
            with act.Fori(1, G - 1) as i:
                c_step(i)
            c_step(G - 1, last=True)
            c_step(G - 1, tail=True)

            def gate_exp(n):
                act.wait_ge(d_lgs, LEAD + n + 1)
                act.activation(ge[:, :, :], lg[:, :, :], ACT.Exp).then_inc(d_ex, 1)

            def d_step(i, last):
                for e in range(E):
                    act.wait_ge(d_h, LEAD + E * i + e - 1)
                    for c in range(HC):
                        act.wait_ge(d_l1, LEAD + E * HC * i + HC * e + c + 1)
                        act.activation(hid[:, HC * (e % 2) + c, :], bank(c), ACT.Gelu,
                                       bias=cols[:, B1C + HC * e + c:B1C + HC * e + c + 1]).then_inc(d_g, 1)
                    k = slice(HC * (e % 2), HC * (e % 2 + 1))
                    act.wait_ge(d_g, LEAD + E * HC * i + HC * (e + 1))
                    act.wait_ge(d_l2, LEAD + E * i + e - 1)
                    act.activation(hhi[:, k, :], hid[:, k, :], ACT.Copy).then_inc(d_hi, 1)
                    if e == 1:
                        act.wait_ge(d_gt, LEAD + i + 1)
                        act.wait_ge(d_b2, LEAD + i)
                        act.activation(gT[:, :], bank(6)[0:E, :], ACT.Copy, scale=float(W2SCALE)).then_inc(d_gte, 1)
                    if e == 4 and not last:
                        empty_turn(D_NORM + 1 + i, False, (d_lg, i + 1))
                    if e == 6 and not last:
                        gate_exp(i + 1)

            gate_exp(0)
            groups(act, d_step)

        @block.vector
        def _(dve):
            start(dve, "dve")
            own = Own(dve, dve_own, gone_by)

            def moments(src):
                dve.sem_inc(gone_by, 1)
                for j in range(J):
                    own.did(dve.bn_stats(stats[:, j, :], blk(src, j)))
                own.after_apart()
                for j in range(J):
                    own.did(dve.bn_aggr(mv[:, j, :], stats[:, j, :]))
                own.after()
                own.did(dve.tensor_scalar(var[:, :], mv[:, :, 1], LN_EPS, None, ALU.add))

            def rstd():
                own.after()
                own.did(dve.tensor_scalar(nwt[:, 0, :].bitcast(I32), var[:, :].bitcast(I32), 1, None,
                                          ALU.arith_shift_right))
                own.after()
                own.did(dve.tensor_scalar(nwt[:, 1, :].bitcast(I32), nwt[:, 0, :].bitcast(I32), -1.0,
                                          float(0x5F3759DF), ALU.mult, ALU.add))
                for y, z in ((1, 4), (4, 1), (1, 0)):
                    own.after()
                    own.did(dve.tensor_tensor(nwt[:, 2, :], nwt[:, y, :], nwt[:, y, :], ALU.mult))
                    own.after()
                    own.did(dve.scalar_tensor_tensor(nwt[:, 3, :], nwt[:, 2, :], -0.5, var[:, :], ALU.mult, ALU.mult))
                    own.after()
                    own.did(dve.scalar_tensor_tensor(nwt[:, z, :], nwt[:, 3, :], 1.5, nwt[:, y, :], ALU.add, ALU.mult))

            def scale(src, n=None):
                if n is not None:
                    dve.wait_ge(xn_turned, LEAD + n)
                own.after()
                for j in range(J):
                    ins = dve.tensor_scalar(blk(xn1 if n is None else xn, j), blk(src, j), mv[:, j, 0:1],
                                            nwt[:, 0, j:j + 1], ALU.subtract, ALU.mult)
                    if n is not None and j == J - 1:
                        ins.then_inc(xn_ok, 1)
                    else:
                        own.did(ins)

            MOMENTS, RSTD, SCALE = 2 * J + 1, 11, J - 1
            NORM = MOMENTS + RSTD + SCALE

            def norm(src, n):
                moments(src)
                rstd()
                scale(src, n)

            def split_x(n):
                dve.wait_ge(x32_ok, LEAD + n + 1)
                own.did(dve.tensor_copy(xhi[:, :], x32[:, :]))
                own.after()
                dve.tensor_tensor(xlo[:, :], x32[:, :], xhi[:, :].bitcast(F32), ALU.subtract).then_inc(xsplit_ok, 1)

            dve.wait_ge(ld_rows, 16 * NROWS)
            own.did(dve.tensor_tensor(crow[:, :].rearrange("k (q h) -> k q h", h=INNER),
                                      w1row[:, :].rearrange("k (q h) -> k q h", h=INNER),
                                      binrow[:, 0:M // HT].unsqueeze(2).to_broadcast([HT, M // HT, INNER]), ALU.mult))
            own.after()
            dve.tensor_tensor(crow[:, :], crow[:, :], b1row[:, :], ALU.add).then_inc(set_dve, 1)
            dve.wait_ge(set_act, 2)
            own.did(dve.tensor_copy(bcol[:, 0, :], cols[:, VC + 4:VC + 5].to_broadcast([P, P])))
            dve.tensor_copy(bcol[0:M, 1, :], cols[0:M, VC + 5:VC + 6].to_broadcast([M, P])).then_inc(set_dve, 1)
            dve.wait_ge(set_act, 3)
            own.did(dve.tensor_tensor(boA[:, :], blk(bank(2), 1), bo_in[:, 0, :], ALU.add))
            own.did(dve.tensor_tensor(boB[:, :], blk(bank(2), 2), bo_in[:, 1, :], ALU.add))
            dve.wait_ge(act_own, 1)
            own.did(dve.tensor_scalar(boC[:, :], bo_in[:, 2, :], tgate[:, 0:1], None, ALU.mult))
            dve.wait_ge(ld_x, 16)
            norm(x_all[:, 0, :], 0)
            own.did(dve.tensor_tensor(wz32.rearrange("p (m h) -> p m h", h=INNER),
                                      w1b.rearrange("p (m h) -> p m h", h=INNER),
                                      win[:, :].unsqueeze(2).to_broadcast([P, M, INNER]), ALU.mult))
            own.after()
            own.did(dve.tensor_copy(wzhi[:, :], wz32))
            own.after()
            dve.tensor_tensor(wzlo[:, :], wz32, wzhi[:, :].bitcast(F32), ALU.subtract).then_inc(set_dve, 1)
            dve.wait_ge(ld_w, 16 * NLW)
            for k in range(HT):
                ins = dve.tensor_scalar(w2o[:, k, :], woutrep[:, k, :], cols[:, W2C + k:W2C + k + 1], None, ALU.mult)
            ins.then_inc(set_dve, 1)
            for s in range(8):
                dve.wait_ge(act_own, 2 + s)
                src = bank(SETUP_BANKS[s % 3]).rearrange("p (a n) -> p a n", n=P)
                if s < 4:
                    dve.scalar_tensor_tensor(four_heads(mlo, s), src, -1.0 / 8, four_heads(mhi, s).bitcast(F32),
                                             ALU.mult, ALU.subtract).then_inc(set_dve, 1)
                else:
                    dve.scalar_tensor_tensor(four_heads(volo, s), src, tgate[:, 0:1], four_heads(vohi, s).bitcast(F32),
                                             ALU.mult, ALU.subtract).then_inc(set_dve, 1)

            def choose(g):
                dve.wait_ge(a_se, LEAD + g + 1)
                dve.sem_inc(gone_by, 1)
                for r in range(TOPK // 8):
                    src = sA if r == 0 else work
                    for j in range(J):
                        own.did(dve.max(top8[:, r, j, :], blk(src, j)))
                    if r == 0:
                        own.after()
                        dve.wait_ge(a_exp, LEAD + g)
                        own.did(dve.tensor_scalar(negA[:, :], top8[:, 0, :, 0], -1.0, None, ALU.mult))
                    own.after_apart()
                    for j in range(J):
                        ins = dve.match_replace(blk(work, j), top8[:, r, j, :], blk(src, j), BLANK)
                        if r == 0 and j == J - 1:
                            ins.then_inc(a_first, 1)
                            dve.wait_ge(a_first, LEAD + g + 1)
                        else:
                            own.did(ins)
                    own.after_apart()
                dve.wait_ge(a_exp, LEAD + g + 1)
                for j in range(J):
                    dve.scalar_tensor_tensor(blk(eA, j), blk(work, j), BLANK, blk(eA, j), ALU.is_equal, ALU.mult,
                                             accum_out=sumA[:, j:j + 1]).then_inc(a_p, 1)
                dve.wait_ge(a_p, LEAD + J * g + J)
                own.did(dve.reciprocal(rA[:, :], sumA[:, :]))

            CHOOSE = 8 * J + 1

            def a_update(g, xb_count):
                dve.wait_ge(a_o, LEAD + g + 1)
                dve.wait_ge(xb_ok, LEAD + xb_count)
                own.after()
                for j in range(J):
                    xj = blk(grp(x_all, g), j)
                    dve.scalar_tensor_tensor(xj, blk(bank(6), j), rA[:, j:j + 1], xj, ALU.mult,
                                             ALU.add).then_inc(x_done[A_PH], 1)

            def b_update(i, xb_count):
                dve.wait_ge(b_o, LEAD + i + 1)
                dve.wait_ge(xb_ok, LEAD + xb_count)
                x = grp(x_all, i)
                dve.tensor_tensor(x, x, bank(2), ALU.add).then_inc(x_done[B_PH], 1)

            def ab_step(i, more=True):
                g = i + 1
                choose(g)
                if more:
                    dve.wait_ge(ld_x, 16 * (i + 2) + 16)
                    norm(grp(x_all, i + 2), 2 * g + 1)
                a_update(g, 2 * i + 2)
                b_update(i, 2 * i + 3)
                dve.wait_ge(x_done[A_PH], LEAD + J * g + J)
                norm(grp(x_all, g), 2 * g + 2 if more else 2 * g + 1)
                split_x(2 * g + 2 if more else 2 * g + 1)

            choose(0)
            dve.wait_ge(ld_x, 32)
            norm(x_all[:, 1, :], 1)
            a_update(0, 1)
            dve.wait_ge(x_done[A_PH], LEAD + J)
            norm(x_all[:, 0, :], 2)
            split_x(2)
            with dve.Fori(0, G - 2) as i:
                own.loop(i, 0, CHOOSE + 2 * NORM + 1)
                ab_step(i)
            own.end_loop(G - 2)
            ab_step(G - 2, False)

            def split_ctx(src, j):
                own.did(dve.tensor_copy(blk(chi, j), src))
                own.after()
                dve.tensor_tensor(blk(clo, j), src, blk(chi, j).bitcast(F32), ALU.subtract).then_inc(c_csplit, 1)

            dve.wait_ge(ctx_kept, LEAD + 1)
            for j in range(J):
                split_ctx(ctxT_all[:, 0, P * j:P * (j + 1)], j)
            dve.wait_ge(x_done[B_PH], LEAD + 1)
            moments(x_all[:, 0, :])
            rstd()
            scale(x_all[:, 0, :])
            own.after()
            norm(xn1, C_NORM)
            b_update(G - 1, 2 * G)
            split_x(C_NORM)

            def c_step(i, first=False, last=False, tail=False):
                nxt = None if tail else x_all[:, 0, :] if last else grp(x_all, i + 1)
                for s in range(QUADS, QUADS + 5) if tail else range(QUADS):
                    if s % 4 == 0 and (s >= 8 or not first):
                        j = s // 4 - 2
                        dve.wait_ge(c_pv, LEAD + QUADS * i + 4 * j + 4)
                        if j == 0:
                            dve.wait_ge(xb_ok, LEAD + C_NORM + 1 + i)
                        xj = blk(grp(x_all, i if j >= 0 else i - 1), j % J)
                        dve.tensor_tensor(xj, xj, bank(6)[:, 0:P], ALU.add).then_inc(x_done[C_PH], 1)
                    if s < QUADS:
                        f = FEEDS.index(("v", s, 0))
                        dve.wait_ge(c_fed, LEAD + NF * i + f + 1)
                        dve.tensor_copy(vp[:, s // 4 % 2, N * (s % 4):N * (s % 4 + 1)], bank(4 + f % 2)).then_inc(c_ve, 1)
                        dve.wait_ge(c_s, LEAD + QUADS * i + s + 1)
                        dve.tensor_reduce(nmax[:, s % 4, :], bank(s % 2).rearrange("p (a n) -> p a n", n=P),
                                          AX_X, ALU.min).then_inc(c_max, 1)
                    u = s - 2
                    if u < QUADS and (u >= 0 or not first):
                        dve.wait_ge(c_exp, LEAD + QUADS * i + u + 1)
                        own.did(dve.reciprocal(prec[:, u % 4, :], psums[:, u % 4, :]))
                        own.after()
                        pv = pr[:, u % 4, :].rearrange("p (a n) -> p a n", n=P)
                        dve.tensor_tensor(pv, pv, prec[:, u % 4, :].unsqueeze(2).to_broadcast([P, 4, P]),
                                          ALU.mult).then_inc(c_norm, 1)
                    if s == 2 and not last:
                        moments(nxt)
                    if s == 3 and not last:
                        rstd()
                    if s == 4 and not last:
                        scale(nxt)
                    if s == 6:
                        own.after()
                        if last:
                            dve.wait_ge(x_done[C_PH], LEAD + J)
                        moments(nxt if last else xn1)
                    if s == 7:
                        rstd()
                    if s == 8:
                        scale(nxt if last else xn1, C_NORM + 1 + i)
                    if s == 13:
                        split_x(C_NORM + 1 + i)
                    if s % 4 == 1:
                        j = s // 4 - 1
                        if j < 0:
                            if not first and not tail:
                                split_ctx(blk(grp(ctxT_all, i), J - 1), J - 1)
                        elif not last and not tail:
                            split_ctx(blk(grp(ctxT_all, i + 1), j), j)

            c_step(0, first=True)
            with dve.Fori(1, G - 1) as i:
                own.loop(i, 1, QUADS + 2 * NORM + 1 + 1 + J)
                c_step(i)
            own.end_loop(G - 2)
            c_step(G - 1, last=True)
            c_step(G - 1, tail=True)

            def split_h(i, e):
                k = slice(HC * (e % 2), HC * (e % 2 + 1))
                dve.wait_ge(d_hi, LEAD + E * i + e + 1)
                dve.wait_ge(d_l2, LEAD + E * i + e - 1)
                dve.tensor_tensor(hlo[:, k, :], hid[:, k, :], hhi[:, k, :], ALU.subtract).then_inc(d_h, 1)

            def acc_init(i):
                dve.wait_ge(d_b2, LEAD + i + 1)
                dve.wait_ge(d_store, 16 * LEAD + 16 * i)
                dve.tensor_tensor(acc[:, :], grp(x_all, i), bank(6), ALU.add).then_inc(d_init, 1)
                dve.wait_ge(d_init, LEAD + i + 1)

            def bcast(a):
                return a.unsqueeze(2).to_broadcast([P, J, E])

            def gate_logits(n):
                dve.wait_ge(d_lg, LEAD + n + 1)
                own.did(dve.tensor_tensor(lg[:, :, :], bank(6)[:, 0:J * E].rearrange("p (j e) -> p j e", e=E),
                                          bg[:, :].unsqueeze(1).to_broadcast([P, J, E]), ALU.add))
                own.after()
                own.did(dve.tensor_reduce(lmax[:, :], lg[:, :, :], AX_X, ALU.max))
                own.after()
                dve.tensor_tensor(lg[:, :, :], lg[:, :, :], bcast(lmax[:, :]), ALU.subtract).then_inc(d_lgs, 1)

            def gates(n):
                dve.wait_ge(d_ex, LEAD + n + 1)
                own.did(dve.tensor_reduce(gs[:, :], ge[:, :, :], AX_X, ALU.add))
                own.after()
                own.did(dve.reciprocal(gr[:, :], gs[:, :]))
                own.after()
                own.did(dve.tensor_tensor(lg[:, :, :], ge[:, :, :], bcast(gr[:, :]), ALU.mult))
                own.after_apart()
                for j in range(J):
                    own.did(dve.max(g8[:, j, :], lg[:, j, :]))
                own.after_apart()
                for j in range(J):
                    own.did(dve.max_index(gi[:, j, :], g8[:, j, :], lg[:, j, :]))
                own.after()
                own.did(dve.tensor_copy(gif[:, :, :], gi[:, :, :]))
                own.after()
                for k in range(2):
                    own.did(dve.tensor_tensor(gm[:, k, :, :], iota[:, :].unsqueeze(1).to_broadcast([P, J, E]),
                                              bcast(gif[:, :, k]), ALU.is_equal))
                own.after()
                own.did(dve.tensor_tensor(gm[:, 0, :, :], gm[:, 0, :, :], gm[:, 1, :, :], ALU.add))
                own.after()
                own.did(dve.tensor_tensor(ge[:, :, :], lg[:, :, :], gm[:, 0, :, :], ALU.mult))
                own.after()
                own.did(dve.tensor_reduce(gs[:, :], ge[:, :, :], AX_X, ALU.add))
                own.after()
                own.did(dve.tensor_scalar(gs[:, :], gs[:, :], GATE_EPS, None, ALU.max))
                own.after()
                own.did(dve.reciprocal(gr[:, :], gs[:, :]))
                own.after()
                own.did(dve.tensor_tensor(gnext[:, :, :], ge[:, :, :], bcast(gr[:, :]), ALU.mult))

            def use_gates(*free):
                own.after()
                for s, v in free:
                    dve.wait_ge(s, LEAD + v)
                dve.tensor_scalar(gw[:, :, :], gnext[:, :, :], 1.0 / W2SCALE, None, ALU.mult).then_inc(d_gate, 1)

            def d_step(i, last):
                dve.wait_ge(d_gate, LEAD + i + 1)
                for s in range(1, E + 3):
                    if s == E and not last:
                        dve.wait_ge(d_l1, LEAD + E * HC * i + E * HC)
                        split_x(D_NORM + 1 + i)
                    if s <= E:
                        split_h(i, s - 1)
                    if s == 3:
                        acc_init(i)
                    if s >= 3:
                        e = s - 3
                        dve.wait_ge(d_l2, LEAD + E * i + e + 1)
                        for j in range(J):
                            ins = dve.scalar_tensor_tensor(blk(acc, j), blk(bank(4 + e % 2), j), gw[:, j, e:e + 1],
                                                           blk(acc, j), ALU.mult, ALU.add)
                        ins.then_inc(d_comb, 1)
                        dve.wait_ge(d_comb, LEAD + E * i + e + 1)
                    if not last:
                        if s == 1:
                            moments(grp(x_all, i + 1))
                        elif s == 2:
                            rstd()
                            scale(grp(x_all, i + 1), D_NORM + 1 + i)
                        elif s == 6:
                            gate_logits(i + 1)
                        elif s == 9:
                            gates(i + 1)
                if not last:
                    use_gates((d_gt, i + 1))

            dve.wait_ge(x_done[C_PH], LEAD + B)
            gate_logits(0)
            gates(0)
            use_gates()
            GATES = 2 + 3 + 2 * J + 1 + 2 + 1 + 1 + 1 + 1 + 1 + 1
            with dve.Fori(0, G - 1) as i:
                own.loop(i, 0, GATES + NORM + 1)
                d_step(i, False)
            own.end_loop(G - 1)
            d_step(G - 1, True)


_INS = ['x', 'ctx_1024', 'L0_xattn_Wq', 'L0_xattn_bq', 'L0_xattn_Wk', 'L0_xattn_bk', 'L0_xattn_Wv', 'L0_xattn_bv',
        'L0_xattn_Wo', 'L0_xattn_bo', 'L0_ffn_Win', 'L0_ffn_bin_', 'L0_ffn_W1', 'L0_ffn_b1', 'L0_ffn_W2',
        'L0_ffn_b2', 'L0_ffn_Wout', 'L0_ffn_bout', 'L1_xattn_ln_gamma', 'L1_xattn_ln_beta', 'L1_xattn_w_q',
        'L1_xattn_w_kv', 'L1_xattn_w_out', 'L1_xattn_b_out', 'L1_xattn_gate', 'L1_ffn_Wg', 'L1_ffn_bg',
        'L1_ffn_W1', 'L1_ffn_b1', 'L1_ffn_W2', 'L1_ffn_b2']


def kernel(**inputs):
    import numpy as np
    import concourse.bacc as bacc
    from concourse.bass_utils import run_bass_kernel_spmd

    nc = bacc.Bacc("TRN2", target_bir_lowering=False, num_devices=1)
    arrays, t = {}, {}
    for name in _INS:
        a = np.ascontiguousarray(inputs[name])
        arrays[f"in_{name}"] = a
        t[name] = nc.dram_tensor(f"in_{name}", a.shape, mybir.dt.from_np(a.dtype), kind="ExternalInput").ap()
    out = nc.dram_tensor("out_0", (B, P, P), F32, kind="ExternalOutput").ap()
    build(nc, t, out)
    r = run_bass_kernel_spmd(nc, [arrays], core_ids=[0])
    return r.results[0]["out_0"]
```

```python
from contextlib import ExitStack

import concourse.bass as bass
from concourse import mybir

F32 = mybir.dt.float32
F32R = mybir.dt.float32r
F16 = mybir.dt.float16
I32 = mybir.dt.int32
U32 = mybir.dt.uint32
ALU = mybir.AluOpType
ACT = mybir.ActivationFunctionType
AX_X = mybir.AxisListType.X

P = 128
B = 32
J = 4
G = B // J
N = J * P
TOPK = 32
BLANK = -3.0e38
M, INNER = 64, 16
HT = M * INNER // P
HEADS, DH = 16, 64
QUADS = HEADS // 4 * J
E, HID = 8, 512
HC = HID // P
LN_EPS = 1e-5
GATE_EPS = 1e-12
LEAD = 2
A_PH, B_PH, C_PH = range(3)
W2SCALE = 256
PSCALE, VSCALE = 1024, 64
C_NORM, D_NORM = 2 * G, 3 * G


class Own:

    def __init__(self, eng, sem, gone_by):
        self.eng, self.sem, self.gone_by = eng, sem, gone_by
        self.base, self.n, self.i, self.per, self.first = 0, 0, 0, 0, 0

    def loop(self, i, first, per):
        self.base += self.n
        self.i, self.first, self.per, self.n = i, first, per, 0

    def end_loop(self, rounds):
        assert self.n == self.per, f"{self.n} marks in a round, {self.per} said"
        self.base += rounds * self.per
        self.i, self.per, self.first, self.n = 0, 0, 0, 0

    def did(self, ins):
        ins.then_inc(self.sem, 1)
        self.n += 1

    def after(self, n=None):
        n = self.n if n is None else n
        self.eng.wait_ge(self.sem, self.i * self.per + (self.base - self.first * self.per + n))

    def after_apart(self, n=None):
        self.after(n)
        self.eng.sem_inc(self.gone_by, 1)


def build(nc, t, out):
    with ExitStack() as ctx:
        def sb(name, shape, dt=F32):
            return ctx.enter_context(nc.sbuf_tensor(name, shape, dt))

        def sem(name):
            return ctx.enter_context(nc.semaphore(name))

        x_all = sb("x_all", [P, G, N])
        ctxT_all = sb("ctxT_all", [P, G, N])
        ctx_raw = sb("ctx_raw", [P, N])
        ident = sb("ident", [P, P])
        xn1 = ctx_raw[:, :]
        xn = sb("xn", [P, N])
        x32 = sb("x32", [P, N])
        xhi = sb("xhi", [P, N], F32R)
        xlo = sb("xlo", [P, N], F32R)
        stats = sb("stats", [P, 2, J, 6])
        mv = sb("mv", [P, 2, J, 2])
        var = sb("var", [P, 2, J])
        nwt = sb("nwt", [P, 2, 5, J])

        hid = sb("hid", [P, 8, N])
        w0raw = sb("w0raw", [P, 4, P])
        w0T = sb("w0T", [P, 3, P])
        wvo = sb("wvo", [P, P])
        ctxA = hid[:, 0, :]
        qA = hid[:, 1, :]
        kA = hid[:, 2, :]
        vA = hid[:, 3, :]
        sA = hid[:, 4, :]
        work = hid[:, 5, :]
        top8 = sb("top8", [P, 4, J, 8])
        negA = sb("negA", [P, J])
        eA = hid[:, 6, :]
        sumA = sb("sumA", [P, J])
        rA = sb("rA", [P, J])
        ptA = hid[:, 7, :]

        boA = sb("boA", [P, P])
        boB = sb("boB", [P, P])
        boC = sb("boC", [P, P])
        bo_in = sb("bo_in", [P, 3, P])

        vrows = sb("vrows", [8, P])
        w1row = sb("w1row", [HT, P])
        b1row = sb("b1row", [HT, P])
        binrow = sb("binrow", [HT, P])
        w2row = sb("w2row", [HT, P])
        crow = sb("crow", [HT, P])
        moe_b1row = sb("moe_b1row", [E * HC, P])
        cols = sb("cols", [P, 64])
        VC, CC, W2C, B1C = 0, 8, 16, 24
        bcol = sb("bcol", [P, 2, P])

        win = sb("win", [P, M])
        w2o = sb("w2o", [P, HT, P])
        wout0 = sb("wout0", [M, P])
        wzhi = sb("wzhi", [P, HT * P], F32R)
        wzlo = sb("wzlo", [P, HT * P], F32R)

        gate = sb("gate", [P, 1])
        tgate = sb("tgate", [P, 1])
        mhi = sb("mhi", [P, HEADS * P], F32R)
        mlo = sb("mlo", [P, HEADS * P], F32R)
        vohi = sb("vohi", [P, HEADS * P], F32R)
        volo = sb("volo", [P, HEADS * P], F32R)
        chi = sb("chi", [P, N], F32R)
        clo = sb("clo", [P, N], F32R)
        c32 = sb("c32", [P, N])
        vp = sb("vp", [P, 2, HEADS * P])
        qp = sb("qp", [P, HEADS, N // 2])
        pr = hid[:, 0:4, :]
        pt = hid[:, 4:6, :].rearrange("p k n -> p (k n)").bitcast(F16).rearrange("p (a k n) -> p a k n", a=2, n=N)
        pthi, ptlo = pt[:, 0, :, :], pt[:, 1, :, :]
        v16 = vp[:, :, :].rearrange("p j n -> p (j n)").bitcast(F16).rearrange("p (a j n) -> p a j n", a=2, j=2)
        vhi, vlo = v16[:, 0, :, :], v16[:, 1, :, :]
        nmax = sb("nmax", [P, 4, 4])
        psums = sb("psums", [P, 4, 4])
        prec = sb("prec", [P, 4, 4])

        w1hi = sb("w1hi", [P, E * HID], F32R)
        w1lo = sb("w1lo", [P, E * HID], F32R)
        w2hi = sb("w2hi", [P, E * HC, P], F16)
        w2lo = sb("w2lo", [P, E * HC, P], F16)
        h16 = vp[:, :, :].rearrange("p j n -> p (j n)").bitcast(F16).rearrange("p (a k n) -> p a k n", a=2, n=N)
        hhi, hlo = h16[:, 0, :, :], h16[:, 1, :, :]
        wg = sb("wg", [P, E])
        bg = sb("bg", [P, E])
        b2e = sb("b2e", [E, P])
        iota = sb("iota", [P, E])
        iota_i = sb("iota_i", [P, E], I32)
        lg = sb("lg", [P, J, E])
        lmax = sb("lmax", [P, J])
        ge = sb("ge", [P, J, E])
        gs = sb("gs", [P, J])
        gr = sb("gr", [P, J])
        g8 = sb("g8", [P, J, 8])
        gi = sb("gi", [P, J, 8], U32)
        gif = sb("gif", [P, J, 8])
        gm = sb("gm", [P, 2, J, E])
        gnext = sb("gnext", [P, J, E])
        gw = sb("gw", [P, J, E])
        gT = ctx_raw[0:E, :]
        acc = c32

        zb = vp[:, :, :].rearrange("p j n -> p (j n)").rearrange("p (k n) -> p k n", n=N)
        w1_raw = c32
        w2_raw = sb("w2_raw", [P, HC, P])

        vflat = vp[:, :, :].rearrange("p j n -> p (j n)")
        wq_raw = vflat[:, 0:1024]
        wkv_raw = vflat[:, 1024:3072]
        wo_raw = vflat[:, 3072:4096].rearrange("p (a n) -> p a n", n=P)
        qflat = qp[:, :, :].rearrange("p h n -> p (h n)")
        wT = [qflat[:, 1024 * k:1024 * (k + 1)].rearrange("p (a n) -> p a n", n=P) for k in range(3)]
        w1b = qflat[:, 3072:4096]
        wz32 = w2hi[:, :, :].rearrange("p a n -> p (a n)").bitcast(F32)[:, 0:1024]
        woutrep = w2lo[:, :, :].rearrange("p a n -> p (a n)").bitcast(F32)[:, 0:1024].rearrange("p (k n) -> p k n", n=P)

        ps = ctx.enter_context(nc.psum_tensor("ps", [P, 8, N], F32))

        ld_w0 = sem("ld_w0")
        ld_rows = sem("ld_rows")
        ld_small = sem("ld_small")
        ld_w = sem("ld_w")
        ld_wo = sem("ld_wo")
        ld_e = sem("ld_e")
        e_split = sem("e_split")
        ctx_kept = sem("ctx_kept")
        xb_ok = sem("xb_ok")
        ld_x = [sem(f"ld_x{k}") for k in range(3)]
        ld_ctx = sem("ld_ctx")
        ident_ok = sem("ident_ok")
        pool_own = sem("pool_own")
        w1_split = sem("w1_split")
        dve_own = sem("dve_own")
        act_own = sem("act_own")
        gone_by = sem("gone_by")
        set_pe = sem("set_pe")
        set_act = sem("set_act")
        set_pool = sem("set_pool")
        set_dve = sem("set_dve")
        xn_ok = sem("xn_ok")
        xn_turned = sem("xn_turned")
        x32_ok = sem("x32_ok")
        xsplit_ok = sem("xsplit_ok")
        ctx_turned = sem("ctx_turned")
        ctxA_ok = sem("ctxA_ok")
        x_done = [sem(f"x_done{p}") for p in range(3)]
        a_q, a_k, a_v, a_s, a_t, a_o = map(sem, ("a_q", "a_k", "a_v", "a_s", "a_t", "a_o"))
        a_qe, a_ke, a_ve, a_se, a_te = map(sem, ("a_qe", "a_ke", "a_ve", "a_se", "a_te"))
        a_first = sem("a_first")
        a_exp = sem("a_exp")
        a_p = sem("a_p")
        b_z, b_r, b_o = map(sem, ("b_z", "b_r", "b_o"))
        c_fed, c_qe, c_ve, c_s, c_max = map(sem, ("c_fed", "c_qe", "c_ve", "c_s", "c_max"))
        c_exp, c_norm, c_t, c_te, c_pv = map(sem, ("c_exp", "c_norm", "c_t", "c_te", "c_pv"))
        c_vh, c_th = sem("c_vh"), sem("c_th")
        c_rec = sem("c_rec")
        c_csplit, c_c32 = sem("c_csplit"), sem("c_c32")
        d_lg, d_lgs, d_ex, d_gate, d_gt, d_gte, d_b2, d_init = map(
            sem, ("d_lg", "d_lgs", "d_ex", "d_gate", "d_gt", "d_gte", "d_b2", "d_init"))
        d_hi = sem("d_hi")
        d_h = sem("d_h")
        d_l1, d_g, d_l2, d_comb, d_store = map(sem, ("d_l1", "d_g", "d_l2", "d_comb", "d_store"))

        SIGNALS = {
            "pe": (xn_turned, ctx_turned, a_q, a_k, a_v, a_s, a_t, a_o, b_z, b_o, c_fed, c_s, c_t, c_pv,
                   d_lg, d_gt, d_b2, d_l1, d_l2),
            "act": (x32_ok, ctxA_ok, a_qe, a_ke, a_ve, a_se, a_te, a_exp, b_r, c_qe, c_exp, c_vh, c_th, d_ex, d_g, d_gte,
                    d_hi),
            "dve": (xn_ok, xsplit_ok, a_first, a_p, c_ve, c_te, c_max, c_rec, c_csplit, d_lgs, d_gate,
                    d_init, d_comb, d_h, *x_done),
            "pool": (w1_split, c_norm, c_c32, e_split, ctx_kept, xb_ok),
        }

        def start(eng, who):
            for s in SIGNALS[who]:
                eng.sem_inc(s, LEAD)

        NW0, NROWS, NSMALL, NLW, NWO = 4, 14, 10, 3, P // INNER

        def grp(a, i):
            return a[:, bass.ds(i, 1), :].rearrange("p a n -> p (a n)")

        def blk(a, j):
            return a[:, P * j:P * (j + 1)]

        def bank(b):
            return ps[:, b, :]

        AHEAD = 4
        Q_FEEDS = {0: [(0, 4), (0, 5)], 1: [(0, 6)], 2: [(0, 7)],
                   5: [(1, 0)], 6: [(1, 1), (1, 2)], 7: [(1, 3)], 8: [(1, 4), (1, 5)], 9: [(1, 6)], 10: [(1, 7)],
                   13: [(2, 0)], 14: [(2, 1), (2, 2)], 15: [(2, 3)]}

        def feeds(last):
            all_, nq = [], 0
            for s in range(QUADS):
                qs = [f for f in Q_FEEDS.get(s, []) if f[0] < 2 or not last]
                for what in qs[:1] + [None] + qs[1:]:
                    if what is None:
                        all_.append((len(all_), s, "v", None, None, s))
                    else:
                        all_.append((len(all_), s, "q", *what, nq))
                        nq += 1
            return all_

        NF, NQ = len(feeds(False)), 2 * HEADS // 2
        assert NF % 2 == 0 and AHEAD % 2 == 0

        def q_count(s):
            pair, quad = s // 8, s % 4
            return 2 * quad + 2 - AHEAD + 8 * pair

        SETUP_BANKS = (0, 1, 2)

        def four_heads(w, s):
            return w[:, :].rearrange("p (g a o n) -> p g a o n", g=2, a=4, o=2)[:, s % 4 // 2, :, s % 2, :]

        Z_BANKS = (0, 1, 4)
        TURN = 7

        assert E == G

        block = ctx.enter_context(nc.Block())

        @block.sync
        def _(sp):
            sp.sem_inc(d_store, 16 * LEAD)
            x_v = t["x"].rearrange("(g j) t d -> t g j d", j=J)
            c_v = t["ctx_1024"].rearrange("(g j) t d -> t g j d", j=J)

            def load_ctx(i):
                if not isinstance(i, int) or i > 0:
                    sp.wait_ge(ctx_turned, LEAD + i)
                    sp.sem_inc(gone_by, 1)
                sp.dma_start(ctx_raw[:, :].rearrange("p (j d) -> p j d", j=J),
                             c_v[:, bass.ds(i, 1), :, :].rearrange("t a j d -> t (a j) d")).then_inc(ld_ctx, 16)

            sp.dma_start(x_all[:, 0, :].rearrange("p (j d) -> p j d", j=J), x_v[:, 0, :, :]).then_inc(ld_x[0], 16)
            for k, name in enumerate(("L0_xattn_Wq", "L0_xattn_Wk", "L0_xattn_Wv", "L0_xattn_Wo")):
                sp.dma_start(w0raw[:, k, :], t[name]).then_inc(ld_w0, 16)
            load_ctx(0)

            def row(a):
                return a.rearrange("(a n) -> a n", a=1)

            for r, name in enumerate(("L0_xattn_bq", "L0_xattn_bk", "L1_xattn_ln_gamma", "L1_xattn_ln_beta",
                                      "L0_xattn_bv")):
                sp.dma_start(vrows[r:r + 1, :], row(t[name])).then_inc(ld_rows, 16)
            sp.dma_start(vrows[5:6, 0:M], row(t["L0_ffn_b2"])).then_inc(ld_rows, 16)
            sp.dma_start(vrows[5:6, M:P], row(t["L0_ffn_b2"])).then_inc(ld_rows, 16)
            for r in (6, 7):
                sp.dma_start(vrows[r:r + 1, :], row(t["L0_xattn_bq"])).then_inc(ld_rows, 16)
            flat = "(k q) h -> k (q h)"
            sp.dma_start(w1row[:, :], t["L0_ffn_W1"].rearrange(flat, k=HT)).then_inc(ld_rows, 16)
            sp.dma_start(b1row[:, :], t["L0_ffn_b1"].rearrange(flat, k=HT)).then_inc(ld_rows, 16)
            sp.dma_start(w2row[:, :], t["L0_ffn_W2"].rearrange(flat, k=HT)).then_inc(ld_rows, 16)
            sp.dma_start(binrow[:, 0:M // HT], t["L0_ffn_bin_"].rearrange("(k q) -> k q", k=HT)).then_inc(ld_rows, 16)
            sp.dma_start(moe_b1row[:, :], t["L1_ffn_b1"].rearrange("e (c p) -> (e c) p", p=P)).then_inc(ld_rows, 16)
            sp.dma_start(x_all[:, 1, :].rearrange("p (j d) -> p j d", j=J), x_v[:, 1, :, :]).then_inc(ld_x[1], 16)
            load_ctx(1)
            wo4 = t["L0_ffn_Wout"].rearrange("(k q) n -> q k n", k=HT)
            for q in range(P // INNER):
                sp.dma_start(woutrep[INNER * q:INNER * (q + 1), :, :],
                             wo4[q:q + 1, :, :].to_broadcast([INNER, HT, P])).then_inc(ld_wo, 16)
            sp.dma_start(x_all[:, 2:G, :].rearrange("p g (j d) -> p g j d", j=J), x_v[:, 2:G, :, :]).then_inc(ld_x[2], 16)
            with sp.Fori(2, G) as i:
                sp.wait_ge(ld_ctx, 16 * i)
                sp.sem_inc(gone_by, 1)
                load_ctx(i)
            out_v = out.rearrange("(g j) t d -> t g j d", j=J)
            with sp.Fori(0, G) as i:
                sp.wait_ge(d_comb, LEAD + E * i + E)
                sp.sem_inc(gone_by, 1)
                sp.dma_start(out_v[:, bass.ds(i, 1), :, :].rearrange("t a j d -> t (a j) d"),
                             acc[:, :].rearrange("p (j d) -> p j d", j=J)).then_inc(d_store, 16)
            sp.wait_ge(d_store, 16 * LEAD + 16 * G)

        @block.gpsimd
        def _(pool):
            start(pool, "pool")
            pool.memset(ident[:, :], 0.0).then_inc(pool_own, 1)
            pool.iota(iota_i[:, :], pattern=[[1, E]], base=0, channel_multiplier=0).then_inc(pool_own, 1)
            pool.wait_ge(pool_own, 2)
            pool.affine_select(out=ident[:, :], in_=ident[:, :], compare_op=ALU.not_equal, fill=1.0, base=0,
                               pattern=[[-1, P]], channel_multiplier=1).then_inc(ident_ok, 1)
            pool.tensor_copy(iota[:, :], iota_i[:, :]).then_inc(ident_ok, 1)

            def row(a):
                return a.rearrange("(a n) -> a n", a=1)

            for r, name in enumerate(("L0_xattn_bo", "L0_ffn_bout", "L1_xattn_b_out")):
                pool.dma_start(bo_in[:, r, :], row(t[name]).to_broadcast([P, P])).then_inc(ld_small, 16)
            pool.dma_start(gate[:, :], row(t["L1_xattn_gate"]).to_broadcast([P, 1])).then_inc(ld_small, 16)
            pool.dma_start(win[:, :], t["L0_ffn_Win"]).then_inc(ld_small, 16)
            pool.dma_start(w1b, row(t["L0_ffn_W1"].rearrange("m h -> (m h)")).to_broadcast([P, M * INNER])).then_inc(ld_small, 16)
            pool.dma_start(wout0[:, :], t["L0_ffn_Wout"]).then_inc(ld_small, 16)
            pool.dma_start(bg[:, :], row(t["L1_ffn_bg"]).to_broadcast([P, E])).then_inc(ld_small, 16)
            pool.dma_start(wg[:, :], t["L1_ffn_Wg"]).then_inc(ld_small, 16)
            pool.dma_start(b2e[:, :], t["L1_ffn_b2"]).then_inc(ld_small, 16)

            def add_bias(i, count, bias):
                pool.wait_ge(xn_ok, LEAD + count)
                x = grp(x_all, i).rearrange("p (j d) -> p j d", j=J)
                pool.tensor_tensor(x, x, bias[:, :].unsqueeze(1).to_broadcast([P, J, P]), ALU.add).then_inc(xb_ok, 1)

            def keep_ctx(i):
                pool.wait_ge(ctxA_ok, LEAD + i + 1)
                pool.tensor_copy(grp(ctxT_all, i), ctxA).then_inc(ctx_kept, 1)

            def load_expert(e):
                pool.wait_ge(e_split, LEAD + e)
                pool.wait_ge(w1_split, LEAD + e)
                pool.sem_inc(gone_by, 1)
                pool.dma_start(w1_raw[:, :].unsqueeze(1),
                               t["L1_ffn_W1"].rearrange("e p h -> p e h")[:, bass.ds(e, 1), :]).then_inc(ld_e, 16)
                pool.dma_start(w2_raw[:, :, :],
                               t["L1_ffn_W2"].rearrange("e (c p) n -> p e c n", p=P)[:, bass.ds(e, 1), :, :]
                               .rearrange("p a c n -> p (a c) n")).then_inc(ld_e, 16)

            def split_expert(e):
                pool.wait_ge(ld_e, 32 * e + 32)
                w = w1hi[:, :].rearrange("p (e h) -> p e h", e=E)[:, bass.ds(e, 1), :]
                l = w1lo[:, :].rearrange("p (e h) -> p e h", e=E)[:, bass.ds(e, 1), :]
                w2 = w2hi[:, :, :].rearrange("p (e c) n -> p e (c n)", e=E)[:, bass.ds(e, 1), :]
                l2 = w2lo[:, :, :].rearrange("p (e c) n -> p e (c n)", e=E)[:, bass.ds(e, 1), :]
                raw, raw2 = w1_raw[:, :].unsqueeze(1), w2_raw[:, :, :].rearrange("p c n -> p (c n)").unsqueeze(1)
                pool.tensor_copy(w, raw).then_inc(pool_own, 1)
                pool.tensor_scalar(raw2, raw2, float(W2SCALE), None, ALU.mult).then_inc(pool_own, 1)
                pool.wait_ge(pool_own, 2 + 3 * e + 2)
                pool.tensor_copy(w2, raw2).then_inc(pool_own, 1)
                pool.tensor_tensor(l, raw, w.bitcast(F32), ALU.subtract).then_inc(w1_split, 1)
                pool.wait_ge(pool_own, 2 + 3 * e + 3)
                pool.tensor_tensor(l2, raw2, w2, ALU.subtract).then_inc(e_split, 1)

            def a_step(g):
                keep_ctx(g + 1)
                add_bias(g + 1, 2 * g + 2, boA)
                if isinstance(g, int):
                    pool.wait_ge(set_dve, 11)
                add_bias(g, 2 * g + 3, boB)

            load_expert(0)
            pool.wait_ge(ld_small, 16 * NSMALL)
            pool.tensor_tensor(wz32.rearrange("p (m h) -> p m h", h=INNER), w1b.rearrange("p (m h) -> p m h", h=INNER),
                               win[:, :].unsqueeze(2).to_broadcast([P, M, INNER]), ALU.mult).then_inc(set_pool, 1)
            pool.wait_ge(set_pool, 1)
            pool.tensor_copy(wzhi[:, :], wz32).then_inc(set_pool, 1)
            pool.wait_ge(set_pool, 2)
            pool.tensor_tensor(wzlo[:, :], wz32, wzhi[:, :].bitcast(F32), ALU.subtract).then_inc(set_pool, 1)
            keep_ctx(0)
            pool.wait_ge(set_dve, 3)
            add_bias(0, 1, boA)
            pool.wait_ge(set_act, 3)
            pool.wait_ge(ld_wo, 16 * NWO)
            pool.tensor_tensor(w2o[:, :, :], woutrep[:, :, :],
                               cols[:, W2C:W2C + HT].unsqueeze(2).to_broadcast([P, HT, P]), ALU.mult).then_inc(set_pool, 1)
            a_step(0)
            with pool.Fori(0, G - 2) as i:
                a_step(i + 1)
                split_expert(i)
                load_expert(i + 1)
            add_bias(G - 1, 2 * G, boB)
            split_expert(E - 2)
            load_expert(E - 1)
            split_expert(E - 1)
            pool.wait_ge(ctx_kept, LEAD + G)
            pool.wait_ge(w1_split, LEAD + E)
            for j in range(J):
                pool.tensor_copy(blk(c32, j), ctxT_all[:, 0, P * j:P * (j + 1)]).then_inc(c_c32, 1)

            def c_step(i, last=False):
                add_bias(i, C_NORM + 1 + i, boC)
                for u in range(QUADS):
                    pool.wait_ge(c_rec, LEAD + QUADS * i + u + 1)
                    pv = pr[:, u % 4, :].rearrange("p (a n) -> p a n", n=P)
                    pool.tensor_tensor(pv, pv, prec[:, u % 4, :].unsqueeze(2).to_broadcast([P, 4, P]),
                                       ALU.mult).then_inc(c_norm, 1)
                    if u % 4 == 2 and not last:
                        j = u // 4
                        pool.wait_ge(c_s, LEAD + QUADS * i + 4 * j + 4)
                        pool.tensor_copy(blk(c32, j), blk(grp(ctxT_all, i + 1), j)).then_inc(c_c32, 1)

            with pool.Fori(0, G - 1) as i:
                c_step(i)
            c_step(G - 1, last=True)

        @block.tensor
        def _(pe):
            start(pe, "pe")

            def turn(dst, src, n=P, mark=None):
                ins = pe.transpose(dst, src, ident[0:n, 0:n])
                if mark is not None:
                    ins.then_inc(mark, 1)

            def split_mm(dst, wh, wl, ah, al, mark=None):
                pe.matmul(dst, wh, ah, start=True, stop=False)
                pe.matmul(dst, wh, al, start=False, stop=False)
                ins = pe.matmul(dst, wl, ah, start=False, stop=True)
                if mark is not None:
                    ins.then_inc(mark, 1)

            def turn_x(n, *free):
                pe.wait_ge(xn_ok, LEAD + n + 1)
                pe.wait_ge(x32_ok, LEAD + n)
                for s, v in free:
                    pe.wait_ge(s, LEAD + v)
                for j in range(J):
                    turn(blk(bank(TURN), j), blk(xn, j), mark=xn_turned if j == J - 1 else None)

            def turn_ctx(i, x_count):
                pe.wait_ge(ld_ctx, 16 * i + 16)
                pe.wait_ge(x32_ok, LEAD + x_count)
                for j in range(J):
                    turn(blk(bank(TURN), j), blk(ctx_raw, j), mark=ctx_turned if j == J - 1 else None)

            def a_key(g):
                pe.wait_ge(a_qe, LEAD + g)
                pe.wait_ge(ctxA_ok, LEAD + g + 1)
                pe.matmul(bank(3), w0T[:, 1, :], ctxA, start=True, stop=True).then_inc(a_k, 1)

            def a_value(g):
                pe.wait_ge(a_ve, LEAD + g)
                pe.wait_ge(ctxA_ok, LEAD + g + 1)
                for j in range(J):
                    ins = pe.matmul(blk(bank(4), j), blk(ctxA, j), wvo[:, :], start=True, stop=True)
                ins.then_inc(a_v, 1)

            def a_query(g, x_count):
                pe.wait_ge(x32_ok, LEAD + x_count)
                pe.wait_ge(a_ke, LEAD + g + 1)
                pe.matmul(bank(3), w0T[:, 0, :], x32[:, :], start=True, stop=True).then_inc(a_q, 1)

            def a_scores(g):
                pe.wait_ge(a_qe, LEAD + g + 1)
                pe.wait_ge(a_se, LEAD + g)
                for j in range(J):
                    ins = pe.matmul(blk(bank(5), j), blk(qA, j), blk(kA, j), start=True, stop=True)
                ins.then_inc(a_s, 1)

            def a_turn(g):
                pe.wait_ge(a_p, LEAD + J * g + J)
                pe.wait_ge(x_done[A_PH], LEAD + J * g)
                for j in range(J):
                    turn(blk(bank(6), j), blk(eA, j), mark=a_t if j == J - 1 else None)

            def a_attend(g):
                pe.wait_ge(a_te, LEAD + g + 1)
                pe.wait_ge(a_ve, LEAD + g + 1)
                for j in range(J):
                    ins = pe.matmul(blk(bank(6), j), blk(ptA, j), blk(vA, j), start=True, stop=True)
                ins.then_inc(a_o, 1)

            def b_hidden(i, v_count):
                pe.wait_ge(xsplit_ok, LEAD + i + 1)
                for k in range(HT):
                    pe.wait_ge(b_r, LEAD + HT * i + max(k - 2, 0))
                    if k == 2:
                        pe.wait_ge(a_ve, LEAD + v_count)
                    w = slice(P * k, P * (k + 1))
                    split_mm(bank(Z_BANKS[k % 3]), wzhi[:, w], wzlo[:, w], xhi[:, :], xlo[:, :], mark=b_z)

            def b_out(i, first, end):
                if first == 0:
                    pe.wait_ge(b_r, LEAD + HT * i + HT)
                    pe.wait_ge(x_done[B_PH], LEAD + i)
                for n in range(first * HT // 2, end * HT // 2):
                    j, k = n // HT, n % HT
                    ins = pe.matmul(blk(bank(2), j), blk(zb[:, k, :], j), w2o[:, k, :],
                                    start=(k == 0), stop=(k == HT - 1))
                if end == 2 * J:
                    ins.then_inc(b_o, 1)

            def ab_step(i, more=True):
                g = i + 1
                b_hidden(i, g + 1)
                if more:
                    turn_ctx(g + 1, 2 * g + 1)
                b_out(i, 0, 2)
                if more:
                    a_key(g + 1)
                b_out(i, 2, 3)
                a_turn(g)
                b_out(i, 3, 4)
                a_attend(g)
                if more:
                    turn_x(2 * g + 1, (ctxA_ok, g + 2))
                    a_value(g + 1)
                    a_query(g + 1, 2 * g + 2)
                b_out(i, 4, 5)
                if more:
                    a_scores(g + 1)
                b_out(i, 5, 7)
                turn_x(2 * g + 2 if more else 2 * g + 1)
                b_out(i, 7, 8)

            pe.wait_ge(ident_ok, 2)
            pe.wait_ge(ld_w0, 16 * NW0)
            for k, w in enumerate((0, 1, 3)):
                turn(blk(bank(0), k), w0raw[:, w, :], mark=set_pe if k == 2 else None)
            turn_x(0)
            turn_ctx(0, 1)
            pe.wait_ge(set_act, 1)
            pe.matmul(blk(bank(6), 0), w0raw[:, 2, :], w0T[:, 2, :], start=True, stop=True).then_inc(set_pe, 1)
            pe.wait_ge(ld_rows, 16 * NROWS)
            cb = bank(1)
            turn(cb[:, VC:VC + 8], vrows[:, :], 8)
            turn(cb[:, W2C:W2C + 8], w2row[:, :], 8)
            turn(cb[:, B1C:B1C + 32], moe_b1row[:, :], 32)
            pe.wait_ge(set_dve, 1)
            turn(cb[:, CC:CC + 8], crow[:, :], 8, mark=set_pe)
            a_key(0)
            pe.wait_ge(set_act, 2)
            a_value(0)
            a_query(0, 1)
            a_scores(0)
            pe.wait_ge(set_dve, 2)
            pe.wait_ge(ld_small, 16 * NSMALL)
            pe.matmul(blk(bank(6), 1), bcol[:, 0, :], w0T[:, 2, :], start=True, stop=True)
            pe.matmul(blk(bank(6), 2), bcol[0:M, 1, :], wout0[:, :], start=True, stop=True).then_inc(set_pe, 1)
            pe.wait_ge(ld_w, 16 * NLW)
            for k in range(3):
                for half in range(2):
                    s = 2 * k + half
                    b = SETUP_BANKS[s % 3]
                    if s >= 3:
                        pe.wait_ge(set_act, s + 1)
                    for a in range(4):
                        src = (wq_raw if k == 0 else wkv_raw[:, 1024 * (k - 1):1024 * k])
                        turn(blk(bank(b), a), blk(src, 4 * half + a), mark=set_pe if a == 3 else None)

            def per_head(s):
                b = SETUP_BANKS[s % 3]
                pe.wait_ge(set_act, min(9, 7 + s))
                if s >= 3:
                    pe.wait_ge(set_dve, 4 + s - 3)
                for a in range(4):
                    h = 8 * (s % 4 // 2) + 2 * a + s % 2
                    r = DH * (h % 2)
                    left, right = (wT[0], wT[1]) if s < 4 else (wT[2], wo_raw)
                    ins = pe.matmul(blk(bank(b), a), left[r:r + DH, h // 2, :], right[r:r + DH, h // 2, :],
                                    start=True, stop=True)
                ins.then_inc(set_pe, 1)

            turn_ctx(1, 1)
            a_key(1)
            for s in range(3):
                per_head(s)
            pe.wait_ge(set_dve, 3)
            a_turn(0)
            a_attend(0)
            a_value(1)
            turn_x(1, (ctxA_ok, 2))
            a_query(1, 2)
            a_scores(1)
            for s in range(3, 6):
                per_head(s)
            turn_x(2)
            for s in range(6, 8):
                per_head(s)
            pe.wait_ge(set_pool, 4)
            pe.wait_ge(set_dve, 11)
            with pe.Fori(0, G - 2) as i:
                ab_step(i)
            ab_step(G - 2, False)
            b_hidden(G - 1, G)
            b_out(G - 1, 0, 6)
            turn_x(C_NORM)
            b_out(G - 1, 6, 8)

            def early_layer1(c):
                if c == 0:
                    pe.wait_ge(xsplit_ok, LEAD + 2 * G + 1)
                    pe.wait_ge(c_exp, LEAD + QUADS * G)
                if c >= 2:
                    pe.wait_ge(c_te, LEAD + QUADS * G + c - 3)
                w = slice(P * c, P * (c + 1))
                split_mm(bank(c), w1hi[:, w], w1lo[:, w], xhi[:, :], xlo[:, :], mark=d_l1)

            def feed_q(b, pair, k):
                c = slice(0, N // 2) if pair % 2 == 0 else slice(N // 2, N)
                for h in (2 * k, 2 * k + 1):
                    w = slice(P * h, P * (h + 1))
                    split_mm(b[:, N // 2 * (h % 2):N // 2 * (h % 2 + 1)], mhi[:, w], mlo[:, w], xhi[:, c], xlo[:, c],
                             mark=c_fed if h % 2 else None)

            def c_step(i, first=False, last=False, tail=False):
                order = feeds(last)

                def feed_bank(f):
                    if f < 2:
                        pe.wait_ge(c_ve, LEAD + QUADS * i)
                        pe.wait_ge(c_qe, LEAD + AHEAD + NQ * i)
                    else:
                        _, s, kind, _, _, n = order[f - 2]
                        if kind == "q":
                            pe.wait_ge(c_qe, LEAD + AHEAD + NQ * i + n + 1)
                        else:
                            pe.wait_ge(c_ve, LEAD + QUADS * i + s + 1)
                    return bank(4 + f % 2)

                def feed_v(f, s):
                    b = feed_bank(f)
                    j, q = s // 4, s % 4
                    if q == 0:
                        pe.wait_ge(c_csplit, LEAD + J * i + j + 1)
                    w = slice(N * q, N * (q + 1))
                    split_mm(b, blk(chi, j), blk(clo, j), vohi[:, w], volo[:, w], mark=c_fed)

                def scores(s):
                    j, q = s // 4, s % 4
                    if q == 0:
                        pe.wait_ge(c_c32, LEAD + J * i + j + 1)
                    if j % 2 == 0:
                        pe.wait_ge(c_qe, LEAD + AHEAD + NQ * i + q_count(s))
                    pe.wait_ge(c_exp, LEAD + QUADS * i + (max(s - 1, 0) if first else s - 1))
                    for a in range(4):
                        ins = pe.matmul(blk(bank(s % 2), a), blk(qp[:, 4 * q + a, :], j % 2), blk(c32, j),
                                        start=True, stop=True)
                    ins.then_inc(c_s, 1)

                def turn_p(u):
                    pe.wait_ge(c_norm, LEAD + QUADS * i + u + 1)
                    pe.wait_ge(c_te, LEAD + QUADS * i + (max(u - 1, 0) if first else u - 1))
                    for a in range(4):
                        turn(blk(bank(2 + u % 2), a), blk(pr[:, u % 4, :], a), mark=c_t if a == 3 else None)

                def attend(u):
                    j, q = u // 4, u % 4
                    pe.wait_ge(c_te, LEAD + QUADS * i + u + 1)
                    pe.wait_ge(c_ve, LEAD + QUADS * i + u + 1)
                    if q == 0:
                        pe.wait_ge(x_done[C_PH], LEAD + J * i + j)
                    for a in range(4):
                        h = 4 * q + a
                        ph, v = blk(pthi[:, u % 2, :], a), blk(vhi[:, j % 2, :], h)
                        pe.matmul(bank(6)[:, 0:P], ph, v, start=(h == 0), stop=False)
                        pe.matmul(bank(6)[:, 0:P], ph, blk(vlo[:, j % 2, :], h), start=False, stop=False)
                        ins = pe.matmul(bank(6)[:, 0:P], blk(ptlo[:, u % 2, :], a), v,
                                        start=False, stop=(h == HEADS - 1))
                    ins.then_inc(c_pv, 1)

                for s in range(QUADS, QUADS + 4) if tail else range(QUADS):
                    if s < QUADS:
                        for f, fs, kind, pair, k, n in order:
                            if fs != s:
                                continue
                            if kind == "v":
                                feed_v(f, s)
                            else:
                                if pair == 2 and k == 0:
                                    pe.wait_ge(xsplit_ok, LEAD + G + i + 2)
                                feed_q(feed_bank(f), pair, k)
                        scores(s)
                    if s - 3 < QUADS and (s >= 3 or not first):
                        turn_p(s - 3)
                    if tail and QUADS < s:
                        early_layer1(s - QUADS - 1)
                    if s >= 4 or not first:
                        attend(s - 4)
                    if s == 9:
                        turn_x(C_NORM + 1 + i)

            pe.wait_ge(xsplit_ok, LEAD + G + 1)
            for f in range(AHEAD):
                if f >= 2:
                    pe.wait_ge(c_qe, LEAD + f - 1)
                feed_q(bank(4 + f % 2), 0, f)
            pe.wait_ge(x_done[B_PH], LEAD + G)
            c_step(0, first=True)
            with pe.Fori(1, G - 1) as i:
                c_step(i)
            c_step(G - 1, last=True)
            def logits(n, b=6):
                pe.wait_ge(x32_ok, LEAD + D_NORM + n + 1)
                for j in range(J):
                    ins = pe.matmul(bank(b)[:, E * j:E * (j + 1)], blk(x32, j), wg[:, :], start=True, stop=True)
                ins.then_inc(d_lg, 1)

            def d_step(i, first=False, last=False):
                def layer1(e):
                    for c in range(HC):
                        if e == 0:
                            pe.wait_ge(d_g, LEAD + E * HC * i)
                        else:
                            pe.wait_ge(d_g, LEAD + E * HC * i + HC * (e - 1) + c + 1)
                        w = slice(HID * e + P * c, HID * e + P * (c + 1))
                        split_mm(bank(c), w1hi[:, w], w1lo[:, w], xhi[:, :], xlo[:, :], mark=d_l1)

                def layer2(e):
                    pe.wait_ge(d_h, LEAD + E * i + e + 1)
                    pe.wait_ge(d_comb, LEAD + E * i + e - 1)
                    for j in range(J):
                        for c in range(HC):
                            k, w = HC * (e % 2) + c, HC * (e % E) + c
                            dst = blk(bank(4 + e % 2), j)
                            pe.matmul(dst, blk(hhi[:, k, :], j), w2hi[:, w, :], start=(c == 0), stop=False)
                            pe.matmul(dst, blk(hhi[:, k, :], j), w2lo[:, w, :], start=False, stop=False)
                            ins = pe.matmul(dst, blk(hlo[:, k, :], j), w2hi[:, w, :], start=False, stop=(c == HC - 1))
                    ins.then_inc(d_l2, 1)

                pe.wait_ge(xsplit_ok, LEAD + 2 * G + i + 1)
                for s in range(E + 1):
                    if s < E and not (first and s == 0):
                        layer1(s)
                    if s == 0 and not first:
                        layer2(-1)
                    if s == 2:
                        pe.wait_ge(d_gate, LEAD + i + 1)
                        for j in range(J):
                            ins = pe.transpose(bank(6)[0:E, P * j:P * (j + 1)], gw[:, j, :], ident[:, :])
                        ins.then_inc(d_gt, 1)
                    if s == 4 and not last:
                        turn_x(D_NORM + 1 + i)
                    if s >= 2:
                        layer2(s - 2)
                    if s == 3:
                        pe.wait_ge(d_gte, LEAD + i + 1)
                        for j in range(J):
                            ins = pe.matmul(blk(bank(6), j), gT[:, P * j:P * (j + 1)], b2e[:, :], start=True, stop=True)
                        ins.then_inc(d_b2, 1)
                    if s == 5 and not last:
                        pe.wait_ge(d_init, LEAD + i + 1)
                        logits(i + 1)
                if last:
                    layer2(E - 1)

            logits(0, TURN)
            c_step(G - 1, tail=True)
            early_layer1(3)
            pe.wait_ge(x_done[C_PH], LEAD + B)
            d_step(0, first=True)
            with pe.Fori(1, G - 1) as i:
                d_step(i)
            d_step(G - 1, last=True)

        @block.scalar
        def _(act):
            start(act, "act")

            def empty_turn(n, aff, *freed):
                act.wait_ge(xn_turned, LEAD + n + 1)
                for s, v in freed:
                    act.wait_ge(s, LEAD + v)
                if aff:
                    act.activation(x32[:, :], bank(TURN), ACT.Identity, scale=cols[:, VC + 2:VC + 3],
                                   bias=cols[:, VC + 3:VC + 4]).then_inc(x32_ok, 1)
                else:
                    act.activation(x32[:, :], bank(TURN), ACT.Copy).then_inc(x32_ok, 1)

            def take_upper(n, *freed):
                act.wait_ge(xn_turned, LEAD + n + 1)
                for s, v in freed:
                    act.wait_ge(s, LEAD + v)
                act.activation(xhi[:, :], bank(TURN), ACT.Copy).then_inc(x32_ok, 1)

            def empty_ctx(g):
                act.wait_ge(ctx_turned, LEAD + g + 1)
                act.wait_ge(a_v, LEAD + g)
                act.wait_ge(a_k, LEAD + g)
                act.wait_ge(ctx_kept, LEAD + g)
                act.activation(ctxA, bank(TURN), ACT.Copy).then_inc(ctxA_ok, 1)

            def a_key(g):
                act.wait_ge(a_k, LEAD + g + 1)
                act.wait_ge(a_s, LEAD + g)
                act.activation(kA, bank(3), ACT.Identity, bias=cols[:, VC + 1:VC + 2]).then_inc(a_ke, 1)

            def a_value(g):
                act.wait_ge(a_v, LEAD + g + 1)
                act.wait_ge(a_o, LEAD + g)
                act.activation(vA, bank(4), ACT.Copy).then_inc(a_ve, 1)

            def a_query(g):
                act.wait_ge(a_q, LEAD + g + 1)
                act.wait_ge(a_s, LEAD + g)
                act.activation(qA, bank(3), ACT.Identity, bias=cols[:, VC:VC + 1]).then_inc(a_qe, 1)

            def a_scores(g):
                act.wait_ge(a_s, LEAD + g + 1)
                act.wait_ge(a_exp, LEAD + g)
                act.activation(sA, bank(5), ACT.Copy, scale=P ** -0.5).then_inc(a_se, 1)

            def a_exps(g):
                act.wait_ge(a_first, LEAD + g + 1)
                act.wait_ge(a_se, LEAD + g + 1)
                act.wait_ge(a_t, LEAD + g)
                for j in range(J):
                    ins = act.activation(blk(eA, j), blk(sA, j), ACT.Exp, bias=negA[:, j:j + 1])
                ins.then_inc(a_exp, 1)

            def a_turned(g):
                act.wait_ge(a_t, LEAD + g + 1)
                act.wait_ge(a_o, LEAD + g)
                act.activation(ptA, bank(6), ACT.Copy).then_inc(a_te, 1)

            def b_hidden(i, ks):
                act.wait_ge(b_o, LEAD + i)
                for k in ks:
                    act.wait_ge(b_z, LEAD + HT * i + k + 1)
                    act.activation(zb[:, k, :], bank(Z_BANKS[k % 3]), ACT.Relu, bias=cols[:, CC + k:CC + k + 1]).then_inc(b_r, 1)

            def ab_step(i, more=True):
                g = i + 1
                b_hidden(i, range(HT))
                a_exps(g)
                if more:
                    empty_ctx(g + 1)
                    a_key(g + 1)
                a_turned(g)
                if more:
                    empty_turn(2 * g + 1, False, (xsplit_ok, g))
                    a_value(g + 1)
                    a_query(g + 1)
                    a_scores(g + 1)
                    take_upper(2 * g + 2, (b_z, HT * i + HT))
                else:
                    take_upper(2 * g + 1, (xsplit_ok, g), (b_z, HT * i + HT))

            act.wait_ge(set_pe, 1)
            act.activation(w0T[:, :, :].rearrange("p a n -> p (a n)"), bank(0)[:, 0:3 * P], ACT.Copy).then_inc(set_act, 1)
            empty_turn(0, False)
            empty_ctx(0)
            act.wait_ge(set_pe, 2)
            act.activation(wvo[:, :], blk(bank(6), 0), ACT.Copy).then_inc(set_act, 1)
            act.dma_start(wq_raw, t["L1_xattn_w_q"]).then_inc(ld_w, 16)
            act.dma_start(wkv_raw, t["L1_xattn_w_kv"]).then_inc(ld_w, 16)
            act.dma_start(wo_raw, t["L1_xattn_w_out"].rearrange("(a p) n -> p a n", p=P)).then_inc(ld_w, 16)
            act.wait_ge(set_pe, 3)
            act.activation(cols[:, 0:B1C + 32], bank(1)[:, 0:B1C + 32], ACT.Copy).then_inc(set_act, 1)
            act.wait_ge(set_act, 3)
            a_key(0)
            a_value(0)
            a_query(0)
            a_scores(0)
            act.wait_ge(ld_small, 16 * NSMALL)
            act.activation(tgate[:, :], gate[:, :], ACT.Tanh).then_inc(act_own, 1)
            for s in range(6):
                act.wait_ge(set_pe, 5 + s)
                act.activation(wT[s // 2][:, 4 * (s % 2):4 * (s % 2) + 4, :].rearrange("p a n -> p (a n)"),
                               bank(SETUP_BANKS[s % 3]), ACT.Copy).then_inc(set_act, 1)

            def per_head(s):
                act.wait_ge(set_pe, 11 + s)
                src = bank(SETUP_BANKS[s % 3]).rearrange("p (a n) -> p a n", n=P)
                if s < 4:
                    act.activation(four_heads(mhi, s), src, ACT.Copy, scale=-1.0 / 8).then_inc(act_own, 1)
                else:
                    act.activation(four_heads(vohi, s), src, ACT.Copy, scale=tgate[:, 0:1]).then_inc(act_own, 1)

            act.wait_ge(act_own, 1)
            empty_ctx(1)
            a_key(1)
            a_exps(0)
            for s in range(3):
                per_head(s)
            a_turned(0)
            a_value(1)
            empty_turn(1, False)
            a_query(1)
            a_scores(1)
            for s in range(3, 6):
                per_head(s)
            take_upper(2)
            for s in range(6, 8):
                per_head(s)
            with act.Fori(0, G - 2) as i:
                ab_step(i)
            ab_step(G - 2, False)
            b_hidden(G - 1, range(HT))
            empty_turn(C_NORM, True, (b_z, HT * G), (xsplit_ok, G))

            def take_q(f, k):
                act.activation(qp[:, 2 * k:2 * k + 2, :].rearrange("p h n -> p (h n)"), bank(4 + f % 2),
                               ACT.Copy).then_inc(c_qe, 1)

            def c_step(i, first=False, last=False, tail=False):
                for s in range(QUADS, QUADS + 3) if tail else range(QUADS):
                    for f, fs, kind, pair, k, n in feeds(last):
                        if fs != s:
                            continue
                        act.wait_ge(c_fed, LEAD + AHEAD + NF * i + f + 1)
                        if kind == "q":
                            take_q(f, k)
                        else:
                            act.activation(vhi[:, s // 4 % 2, N * (s % 4):N * (s % 4 + 1)], bank(4 + f % 2),
                                           ACT.Copy, scale=float(VSCALE)).then_inc(c_vh, 1)
                    u = s - 1
                    if u < QUADS and (u >= 0 or not first):
                        act.wait_ge(c_max, LEAD + QUADS * i + u + 1)
                        if u >= 4 or not first:
                            act.wait_ge(c_t, LEAD + QUADS * i + u - 3)
                        for a in range(4):
                            ins = act.activation(blk(pr[:, u % 4, :], a), blk(bank(u % 2), a), ACT.Exp, scale=-1.0,
                                                 bias=nmax[:, u % 4, a:a + 1], accum_out=psums[:, u % 4, a:a + 1])
                        ins.then_inc(c_exp, 1)
                    u = s - 3
                    if u < QUADS and (u >= 0 or not first):
                        act.wait_ge(c_t, LEAD + QUADS * i + u + 1)
                        if u >= 2 or not first:
                            act.wait_ge(c_pv, LEAD + QUADS * i + u - 1)
                        act.activation(pthi[:, u % 2, :], bank(2 + u % 2), ACT.Copy,
                                       scale=float(PSCALE)).then_inc(c_th, 1)
                    if s == 10:
                        empty_turn(C_NORM + 1 + i, not last, (xsplit_ok, G + i + 1))

            for f in range(AHEAD):
                act.wait_ge(c_fed, LEAD + f + 1)
                take_q(f, f)
            c_step(0, first=True)
            with act.Fori(1, G - 1) as i:
                c_step(i)
            c_step(G - 1, last=True)
            c_step(G - 1, tail=True)

            def gate_exp(n):
                act.wait_ge(d_lgs, LEAD + n + 1)
                act.activation(ge[:, :, :], lg[:, :, :], ACT.Exp).then_inc(d_ex, 1)

            def d_step(i, last):
                for e in range(E):
                    act.wait_ge(d_h, LEAD + E * i + e - 1)
                    for c in range(HC):
                        act.wait_ge(d_l1, LEAD + E * HC * i + HC * e + c + 1)
                        act.activation(hid[:, HC * (e % 2) + c, :], bank(c), ACT.Gelu,
                                       bias=cols[:, B1C + HC * e + c:B1C + HC * e + c + 1]).then_inc(d_g, 1)
                    if e == 2:
                        act.wait_ge(d_gt, LEAD + i + 1)
                        act.wait_ge(d_b2, LEAD + i)
                        act.activation(gT[:, :], bank(6)[0:E, :], ACT.Copy, scale=float(W2SCALE)).then_inc(d_gte, 1)
                    k = slice(HC * (e % 2), HC * (e % 2 + 1))
                    act.wait_ge(d_g, LEAD + E * HC * i + HC * (e + 1))
                    act.wait_ge(d_l2, LEAD + E * i + e - 1)
                    act.activation(hhi[:, k, :], hid[:, k, :], ACT.Copy).then_inc(d_hi, 1)
                    if e == 4 and not last:
                        empty_turn(D_NORM + 1 + i, False, (d_lg, i + 1))
                    if e == 6 and not last:
                        gate_exp(i + 1)

            gate_exp(0)
            with act.Fori(0, G - 1) as i:
                d_step(i, False)
            d_step(G - 1, True)

        @block.vector
        def _(dve):
            start(dve, "dve")
            own = Own(dve, dve_own, gone_by)

            def moments(src, k=0):
                dve.sem_inc(gone_by, 1)
                for j in range(J):
                    own.did(dve.bn_stats(stats[:, k, j, :], blk(src, j)))
                own.after_apart()
                for j in range(J):
                    own.did(dve.bn_aggr(mv[:, k, j, :], stats[:, k, j, :]))
                own.after()
                own.did(dve.tensor_scalar(var[:, k, :], mv[:, k, :, 1], LN_EPS, None, ALU.add))

            def rstd_step(done, m, k=0):
                own.after(done)
                v, w = var[:, k, :], nwt[:, k, :, :]
                half, yy = w[:, 3, :], w[:, 2, :]
                if m == 0:
                    own.did(dve.tensor_scalar(w[:, 0, :].bitcast(I32), v.bitcast(I32), 1, None, ALU.arith_shift_right))
                elif m == 1:
                    own.did(dve.tensor_scalar(w[:, 1, :].bitcast(I32), w[:, 0, :].bitcast(I32), -1.0,
                                              float(0x5F3759DF), ALU.mult, ALU.add))
                else:
                    a, b = ((1, 4), (4, 1), (1, 0))[(m - 2) // 3]
                    if m % 3 == 2:
                        own.did(dve.tensor_tensor(yy, w[:, a, :], w[:, a, :], ALU.mult))
                    elif m % 3 == 0:
                        own.did(dve.scalar_tensor_tensor(half, yy, -0.5, v, ALU.mult, ALU.mult))
                    else:
                        own.did(dve.scalar_tensor_tensor(w[:, b, :], half, 1.5, w[:, a, :], ALU.add, ALU.mult))
                return own.n

            def rstd(k=0, first=0):
                done = own.n
                for m in range(first, RSTD):
                    done = rstd_step(done, m, k)

            def scale(src, n=None, k=0):
                if n is not None:
                    dve.wait_ge(xn_turned, LEAD + n)
                own.after()
                for j in range(J):
                    ins = dve.tensor_scalar(blk(xn1 if n is None else xn, j), blk(src, j), mv[:, k, j, 0:1],
                                            nwt[:, k, 0, j:j + 1], ALU.subtract, ALU.mult)
                    if n is not None and j == J - 1:
                        ins.then_inc(xn_ok, 1)
                    else:
                        own.did(ins)

            MOMENTS, RSTD, SCALE = 2 * J + 1, 11, J - 1
            NORM = MOMENTS + RSTD + SCALE
            PIECES = 4 + RSTD + J

            def norm_piece(done, m, src, n=None):
                if m < 3:
                    own.after_apart(done)
                elif m == 3 or m >= 4 + RSTD:
                    own.after(done)
                if m < 2:
                    for j in (2 * m, 2 * m + 1):
                        own.did(dve.bn_stats(stats[:, 0, j, :], blk(src, j)))
                elif m == 2:
                    for j in range(J):
                        own.did(dve.bn_aggr(mv[:, 0, j, :], stats[:, 0, j, :]))
                elif m == 3:
                    own.did(dve.tensor_scalar(var[:, 0, :], mv[:, 0, :, 1], LN_EPS, None, ALU.add))
                elif m < 4 + RSTD:
                    return rstd_step(done, m - 4)
                else:
                    j = m - 4 - RSTD
                    if n is not None and j == 0:
                        dve.wait_ge(xn_turned, LEAD + n)
                    ins = dve.tensor_scalar(blk(xn1 if n is None else xn, j), blk(src, j), mv[:, 0, j, 0:1],
                                            nwt[:, 0, 0, j:j + 1], ALU.subtract, ALU.mult)
                    if n is not None and j == J - 1:
                        ins.then_inc(xn_ok, 1)
                    else:
                        own.did(ins)
                return own.n

            def norm(src, n):
                moments(src)
                rstd()
                scale(src, n)

            def split_upper(n):
                dve.wait_ge(x32_ok, LEAD + n + 1)
                own.did(dve.tensor_copy(xhi[:, :], x32[:, :]))

            def split_lower():
                own.after()
                dve.tensor_tensor(xlo[:, :], x32[:, :], xhi[:, :].bitcast(F32), ALU.subtract).then_inc(xsplit_ok, 1)

            def split_x(n):
                split_upper(n)
                split_lower()

            def split_turned(n):
                dve.wait_ge(x32_ok, LEAD + n + 1)
                dve.tensor_tensor(xlo[:, :], bank(TURN), xhi[:, :].bitcast(F32), ALU.subtract).then_inc(xsplit_ok, 1)

            def choose(g):
                done = own.n
                dve.wait_ge(a_se, LEAD + g + 1)
                dve.sem_inc(gone_by, 1)
                for r in range(TOPK // 8):
                    src = sA if r == 0 else work
                    for j in range(J):
                        own.did(dve.max(top8[:, r, j, :], blk(src, j)))
                    found = own.n
                    done = rstd_step(done, 2 * r, 1)
                    if r == 0:
                        own.after(found)
                        dve.wait_ge(a_exp, LEAD + g)
                        own.did(dve.tensor_scalar(negA[:, :], top8[:, 0, :, 0], -1.0, None, ALU.mult))
                        found = own.n
                    own.after_apart(found)
                    for j in range(J):
                        ins = dve.match_replace(blk(work, j), top8[:, r, j, :], blk(src, j), BLANK)
                        if r == 0 and j == J - 1:
                            ins.then_inc(a_first, 1)
                        else:
                            own.did(ins)
                    blanked = own.n
                    done = rstd_step(done, 2 * r + 1, 1)
                    if r == 0:
                        dve.wait_ge(a_first, LEAD + g + 1)
                    own.after_apart(blanked)
                dve.wait_ge(a_exp, LEAD + g + 1)
                for j in range(J):
                    dve.scalar_tensor_tensor(blk(eA, j), blk(work, j), BLANK, blk(eA, j), ALU.is_equal, ALU.mult,
                                             accum_out=sumA[:, j:j + 1]).then_inc(a_p, 1)
                rstd_step(done, TOPK // 4, 1)
                dve.wait_ge(a_p, LEAD + J * g + J)
                own.did(dve.reciprocal(rA[:, :], sumA[:, :]))
                rstd(1, TOPK // 4 + 1)

            CHOOSE = 8 * J + 1

            def a_update(g, xb_count):
                dve.wait_ge(a_o, LEAD + g + 1)
                dve.wait_ge(xb_ok, LEAD + xb_count)
                own.after()
                for j in range(J):
                    xj = blk(grp(x_all, g), j)
                    dve.scalar_tensor_tensor(xj, blk(bank(6), j), rA[:, j:j + 1], xj, ALU.mult,
                                             ALU.add).then_inc(x_done[A_PH], 1)

            def b_update(i, xb_count):
                dve.wait_ge(b_o, LEAD + i + 1)
                dve.wait_ge(xb_ok, LEAD + xb_count)
                x = grp(x_all, i)
                dve.tensor_tensor(x, x, bank(2), ALU.add).then_inc(x_done[B_PH], 1)

            def ab_step(i, phase=0):
                g = i + 1
                choose(g)
                if phase < 2:
                    scale(grp(x_all, i + 2), 2 * g + 1, 1)
                else:
                    dve.wait_ge(ctx_turned, LEAD + G)
                    scale(x_all[:, 0, :], None, 1)
                a_update(g, 2 * i + 2)
                dve.wait_ge(x_done[A_PH], LEAD + J * g + J)
                norm(grp(x_all, g), 2 * g + 2 if phase < 2 else 2 * g + 1)
                if phase == 0:
                    moments(grp(x_all, i + 3), 1)
                elif phase == 1:
                    dve.wait_ge(x_done[B_PH], LEAD + 1)
                    moments(x_all[:, 0, :], 1)
                else:
                    moments(xn1, 1)
                split_turned(2 * g + 2 if phase < 2 else 2 * g + 1)
                b_update(i, 2 * i + 3)

            dve.wait_ge(ld_x[0], 16)
            norm(x_all[:, 0, :], 0)
            dve.wait_ge(ld_rows, 16 * NROWS)
            own.did(dve.tensor_tensor(crow[:, :].rearrange("k (q h) -> k q h", h=INNER),
                                      w1row[:, :].rearrange("k (q h) -> k q h", h=INNER),
                                      binrow[:, 0:M // HT].unsqueeze(2).to_broadcast([HT, M // HT, INNER]), ALU.mult))
            own.after()
            dve.tensor_tensor(crow[:, :], crow[:, :], b1row[:, :], ALU.add).then_inc(set_dve, 1)
            dve.wait_ge(set_act, 3)
            own.did(dve.tensor_copy(bcol[:, 0, :], cols[:, VC + 4:VC + 5].to_broadcast([P, P])))
            dve.tensor_copy(bcol[0:M, 1, :], cols[0:M, VC + 5:VC + 6].to_broadcast([M, P])).then_inc(set_dve, 1)
            dve.wait_ge(ld_x[1], 16)
            moments(x_all[:, 1, :], 1)
            choose(0)
            dve.wait_ge(ld_small, 16 * NSMALL)
            dve.wait_ge(set_pe, 4)
            own.did(dve.tensor_tensor(boA[:, :], blk(bank(6), 1), bo_in[:, 0, :], ALU.add))
            own.after()
            dve.tensor_tensor(boB[:, :], blk(bank(6), 2), bo_in[:, 1, :], ALU.add).then_inc(set_dve, 1)

            def per_head(s):
                dve.wait_ge(act_own, 2 + s)
                src = bank(SETUP_BANKS[s % 3]).rearrange("p (a n) -> p a n", n=P)
                if s < 4:
                    dve.scalar_tensor_tensor(four_heads(mlo, s), src, -1.0 / 8, four_heads(mhi, s).bitcast(F32),
                                             ALU.mult, ALU.subtract).then_inc(set_dve, 1)
                else:
                    dve.scalar_tensor_tensor(four_heads(volo, s), src, tgate[:, 0:1], four_heads(vohi, s).bitcast(F32),
                                             ALU.mult, ALU.subtract).then_inc(set_dve, 1)

            scale(x_all[:, 1, :], 1, 1)
            per_head(0)
            a_update(0, 1)
            for s in range(1, 3):
                per_head(s)
            dve.wait_ge(x_done[A_PH], LEAD + J)
            norm(x_all[:, 0, :], 2)
            for s in range(3, 6):
                per_head(s)
            split_turned(2)
            for s in range(6, 8):
                per_head(s)
            own.did(dve.tensor_scalar(boC[:, :], bo_in[:, 2, :], tgate[:, 0:1], None, ALU.mult))
            dve.wait_ge(ld_x[2], 16)
            moments(x_all[:, 2, :], 1)
            with dve.Fori(0, G - 3) as i:
                own.loop(i, 0, CHOOSE + 2 * NORM)
                ab_step(i)
            own.end_loop(G - 3)
            ab_step(G - 3, 1)
            ab_step(G - 2, 2)

            def split_ctx(src, j):
                own.did(dve.tensor_copy(blk(chi, j), src))
                own.after()
                dve.tensor_tensor(blk(clo, j), src, blk(chi, j).bitcast(F32), ALU.subtract).then_inc(c_csplit, 1)

            dve.wait_ge(ctx_kept, LEAD + 1)
            rstd(1)
            scale(xn1, C_NORM, 1)
            for j in range(J):
                split_ctx(ctxT_all[:, 0, P * j:P * (j + 1)], j)
            split_x(C_NORM)
            b_update(G - 1, 2 * G)

            def c_step(i, first=False, last=False, tail=False):
                done = own.n
                nxt = None if tail else x_all[:, 0, :] if last else grp(x_all, i + 1)
                for s in range(QUADS, QUADS + 5) if tail else range(QUADS):
                    if s % 4 == 0 and (s >= 8 or not first):
                        j = s // 4 - 2
                        dve.wait_ge(c_pv, LEAD + QUADS * i + 4 * j + 4)
                        if j == 0:
                            dve.wait_ge(xb_ok, LEAD + C_NORM + 1 + i)
                        xj = blk(grp(x_all, i if j >= 0 else i - 1), j % J)
                        dve.scalar_tensor_tensor(xj, bank(6)[:, 0:P], 1.0 / (PSCALE * VSCALE), xj, ALU.mult,
                                                 ALU.add).then_inc(x_done[C_PH], 1)
                    u = s - 2
                    if u < QUADS and (u >= 0 or not first):
                        dve.wait_ge(c_exp, LEAD + QUADS * i + u + 1)
                        if u >= 4 or not first:
                            dve.wait_ge(c_norm, LEAD + QUADS * i + u - 3)
                        dve.reciprocal(prec[:, u % 4, :], psums[:, u % 4, :]).then_inc(c_rec, 1)
                    if s == 4 and last:
                        dve.wait_ge(x_done[C_PH], LEAD + J)

                    def beside(p):
                        nonlocal done
                        m = 5 * (s % 4) + p
                        if s < 4 and not last and m < PIECES:
                            done = norm_piece(done, m, nxt)
                        elif 4 <= s < 8 and m < PIECES:
                            done = norm_piece(done, m, nxt if last else xn1, C_NORM + 1 + i)
                        elif s == 11 and p == 1:
                            split_upper(C_NORM + 1 + i)
                        elif s == 11 and p == 2:
                            split_lower()

                    beside(0)
                    if s < QUADS:
                        f = next(f for f, fs, kind, *_ in feeds(last) if (fs, kind) == (s, "v"))
                        v = (s // 4 % 2, slice(N * (s % 4), N * (s % 4 + 1)))
                        dve.wait_ge(c_vh, LEAD + QUADS * i + s + 1)
                        dve.scalar_tensor_tensor(vlo[:, v[0], v[1]], bank(4 + f % 2), float(VSCALE),
                                                 vhi[:, v[0], v[1]], ALU.mult, ALU.subtract).then_inc(c_ve, 1)
                        beside(1)
                        dve.wait_ge(c_s, LEAD + QUADS * i + s + 1)
                        dve.tensor_reduce(nmax[:, s % 4, :], bank(s % 2).rearrange("p (a n) -> p a n", n=P),
                                          AX_X, ALU.min).then_inc(c_max, 1)
                        beside(2)
                    beside(3)
                    u = s - 3
                    if u < QUADS and (u >= 0 or not first):
                        dve.wait_ge(c_th, LEAD + QUADS * i + u + 1)
                        dve.scalar_tensor_tensor(ptlo[:, u % 2, :], bank(2 + u % 2), float(PSCALE), pthi[:, u % 2, :],
                                                 ALU.mult, ALU.subtract).then_inc(c_te, 1)
                    beside(4)
                    if s % 4 == 1:
                        j = s // 4 - 1
                        if j < 0:
                            if not first and not tail:
                                split_ctx(blk(grp(ctxT_all, i), J - 1), J - 1)
                        elif not last and not tail:
                            split_ctx(blk(grp(ctxT_all, i + 1), j), j)

            c_step(0, first=True)
            with dve.Fori(1, G - 1) as i:
                own.loop(i, 1, 2 * NORM + 1 + 1 + J)
                c_step(i)
            own.end_loop(G - 2)
            c_step(G - 1, last=True)

            def split_h(i, e):
                k = slice(HC * (e % 2), HC * (e % 2 + 1))
                dve.wait_ge(d_l2, LEAD + E * i + e - 1)
                dve.wait_ge(d_hi, LEAD + E * i + e + 1)
                dve.tensor_tensor(hlo[:, k, :], hid[:, k, :], hhi[:, k, :], ALU.subtract).then_inc(d_h, 1)

            def acc_init(i):
                dve.wait_ge(d_b2, LEAD + i + 1)
                dve.wait_ge(d_store, 16 * LEAD + 16 * i)
                dve.tensor_tensor(acc[:, :], grp(x_all, i), bank(6), ALU.add).then_inc(d_init, 1)
                dve.wait_ge(d_init, LEAD + i + 1)

            def bcast(a):
                return a.unsqueeze(2).to_broadcast([P, J, E])

            def gate_logits(n, b=6):
                dve.wait_ge(d_lg, LEAD + n + 1)
                own.did(dve.tensor_tensor(lg[:, :, :], bank(b)[:, 0:J * E].rearrange("p (j e) -> p j e", e=E),
                                          bg[:, :].unsqueeze(1).to_broadcast([P, J, E]), ALU.add))
                own.after()
                own.did(dve.tensor_reduce(lmax[:, :], lg[:, :, :], AX_X, ALU.max))
                own.after()
                dve.tensor_tensor(lg[:, :, :], lg[:, :, :], bcast(lmax[:, :]), ALU.subtract).then_inc(d_lgs, 1)

            def softmax(n):
                dve.wait_ge(d_ex, LEAD + n + 1)
                own.did(dve.tensor_reduce(gs[:, :], ge[:, :, :], AX_X, ALU.add))
                own.after()
                own.did(dve.reciprocal(gr[:, :], gs[:, :]))
                own.after()
                own.did(dve.tensor_tensor(lg[:, :, :], ge[:, :, :], bcast(gr[:, :]), ALU.mult))

            def gates():
                own.after_apart()
                for j in range(J):
                    own.did(dve.max(g8[:, j, :], lg[:, j, :]))
                own.after_apart()
                for j in range(J):
                    own.did(dve.max_index(gi[:, j, :], g8[:, j, :], lg[:, j, :]))
                own.after()
                own.did(dve.tensor_copy(gif[:, :, :], gi[:, :, :]))
                own.after()
                for k in range(2):
                    own.did(dve.tensor_tensor(gm[:, k, :, :], iota[:, :].unsqueeze(1).to_broadcast([P, J, E]),
                                              bcast(gif[:, :, k]), ALU.is_equal))
                own.after()
                own.did(dve.tensor_tensor(gm[:, 0, :, :], gm[:, 0, :, :], gm[:, 1, :, :], ALU.add))
                own.after()
                own.did(dve.tensor_tensor(ge[:, :, :], lg[:, :, :], gm[:, 0, :, :], ALU.mult))
                own.after()
                own.did(dve.tensor_reduce(gs[:, :], ge[:, :, :], AX_X, ALU.add))
                own.after()
                own.did(dve.tensor_scalar(gs[:, :], gs[:, :], GATE_EPS, None, ALU.max))
                own.after()
                own.did(dve.reciprocal(gr[:, :], gs[:, :]))
                own.after()
                own.did(dve.tensor_tensor(gnext[:, :, :], ge[:, :, :], bcast(gr[:, :]), ALU.mult))

            def use_gates(*free):
                own.after()
                for s, v in free:
                    dve.wait_ge(s, LEAD + v)
                dve.tensor_scalar(gw[:, :, :], gnext[:, :, :], 1.0 / W2SCALE, None, ALU.mult).then_inc(d_gate, 1)

            def d_step(i, last):
                dve.wait_ge(d_gate, LEAD + i + 1)

                def combine(e):
                    dve.wait_ge(d_l2, LEAD + E * i + e + 1)
                    for j in range(J):
                        ins = dve.scalar_tensor_tensor(blk(acc, j), blk(bank(4 + e % 2), j), gw[:, j, e:e + 1],
                                                       blk(acc, j), ALU.mult, ALU.add)
                    ins.then_inc(d_comb, 1)
                    dve.wait_ge(d_comb, LEAD + E * i + e + 1)

                for s in range(1, E + 3):
                    if s == E:
                        combine(E - 3)
                        if not last:
                            dve.wait_ge(d_l1, LEAD + E * HC * i + E * HC)
                            split_x(D_NORM + 1 + i)
                            softmax(i + 1)
                    if s <= E:
                        split_h(i, s - 1)
                    if s == 3:
                        acc_init(i)
                    if s >= 3 and s != E:
                        combine(s - 3)
                    if not last:
                        if s == 1:
                            moments(grp(x_all, i + 1))
                        elif s == 2:
                            rstd()
                            scale(grp(x_all, i + 1), D_NORM + 1 + i)
                        elif s == 6:
                            gate_logits(i + 1)
                        elif s == 9:
                            gates()
                if not last:
                    use_gates((d_gt, i + 1))

            gate_logits(0, TURN)
            c_step(G - 1, tail=True)
            dve.wait_ge(x_done[C_PH], LEAD + B)
            softmax(0)
            gates()
            use_gates()
            GATES = 2 + 3 + 2 * J + 1 + 2 + 1 + 1 + 1 + 1 + 1 + 1
            with dve.Fori(0, G - 1) as i:
                own.loop(i, 0, GATES + NORM + 1)
                d_step(i, False)
            own.end_loop(G - 1)
            d_step(G - 1, True)


_INS = ['x', 'ctx_1024', 'L0_xattn_Wq', 'L0_xattn_bq', 'L0_xattn_Wk', 'L0_xattn_bk', 'L0_xattn_Wv', 'L0_xattn_bv',
        'L0_xattn_Wo', 'L0_xattn_bo', 'L0_ffn_Win', 'L0_ffn_bin_', 'L0_ffn_W1', 'L0_ffn_b1', 'L0_ffn_W2',
        'L0_ffn_b2', 'L0_ffn_Wout', 'L0_ffn_bout', 'L1_xattn_ln_gamma', 'L1_xattn_ln_beta', 'L1_xattn_w_q',
        'L1_xattn_w_kv', 'L1_xattn_w_out', 'L1_xattn_b_out', 'L1_xattn_gate', 'L1_ffn_Wg', 'L1_ffn_bg',
        'L1_ffn_W1', 'L1_ffn_b1', 'L1_ffn_W2', 'L1_ffn_b2']


def kernel(**inputs):
    import numpy as np
    import concourse.bacc as bacc
    from concourse.bass_utils import run_bass_kernel_spmd

    nc = bacc.Bacc("TRN2", target_bir_lowering=False, num_devices=1)
    arrays, t = {}, {}
    for name in _INS:
        a = np.ascontiguousarray(inputs[name])
        arrays[f"in_{name}"] = a
        t[name] = nc.dram_tensor(f"in_{name}", a.shape, mybir.dt.from_np(a.dtype), kind="ExternalInput").ap()
    out = nc.dram_tensor("out_0", (B, P, P), F32, kind="ExternalOutput").ap()
    build(nc, t, out)
    r = run_bass_kernel_spmd(nc, [arrays], core_ids=[0])
    return r.results[0]["out_0"]
```
